# Optimizing a Trainium2 kernel written in Bass

```python
import numpy as np
import jax
import jax.numpy as jnp

def _softmax(x, axis=-1):
    return jax.nn.softmax(x, axis=axis)

def _gelu(x):
    return jax.nn.gelu(x, approximate=True)

def _silu(x):
    return jax.nn.silu(x)

def _sigmoid(x):
    return jax.nn.sigmoid(x)

def _layernorm(x, axis=-1, eps=1e-05):
    m = jnp.mean(x, axis=axis, keepdims=True)
    v = jnp.var(x, axis=axis, keepdims=True)
    return (x - m) / jnp.sqrt(v + eps)

def _scatter_add(tgt, idx, src, axis=0):
    return tgt.at[idx].add(src)

def _segment_sum(src, seg, n):
    return jax.ops.segment_sum(src, seg, n)
kernel_name = 'mk_xattn_ffn_d4_seqx_r4_bca531'

def setup_inputs(seed: int=0):
    np.random.seed(seed)
    _w = jnp.asarray

    def _rec_inputs():
        import jax
        import jax.numpy as jnp
        _rk = jax.random.key(seed)
        x = -0.0002928 + 1 * jax.random.normal(jax.random.fold_in(_rk, 1), (8, 256, 256), jnp.float32)
        _lenS = 256 - jax.random.randint(jax.random.fold_in(_rk, 7), (8,), 0, max(1, 256 // 4) + 1, jnp.int32)
        _lenS2 = 256 - jax.random.randint(jax.random.fold_in(_rk, 8), (8,), 0, max(1, 256 // 4) + 1, jnp.int32)
        _ctx_1024P = jax.random.normal(jax.random.fold_in(_rk, 11), (8, 16, 256), jnp.float32)
        _ctx_1024c = jax.random.dirichlet(jax.random.fold_in(_rk, 511), 0.3 * jnp.ones((16,), jnp.float32), (8, 256))
        _ctx_1024t = jnp.einsum('bsk,bkd->bsd', _ctx_1024c, _ctx_1024P)
        _ctx_1024t = _ctx_1024t * jax.lax.rsqrt(jnp.mean(jnp.square(_ctx_1024t)) + 1e-12) * 0.953939
        ctx_1024 = -1.39393e-06 + 0.999914 * (_ctx_1024t + 0.3 * jax.random.normal(jax.random.fold_in(_rk, 611), (8, 256, 256), jnp.float32))
        _validS = jnp.arange(256)[None, :] < _lenS[:, None]
        _validS2 = jnp.arange(256)[None, :] < _lenS2[:, None]
        _causal = jnp.tril(jnp.ones((256, 256), dtype=bool))
        mask_BxS2_ff1 = jnp.where(jnp.ones((8, 256), dtype=bool), 1.0, 0.0).astype(jnp.float32)
        return (x, ctx_1024, mask_BxS2_ff1)
    x, ctx_1024, mask_BxS2_ff1 = _rec_inputs()

    def _L0_xattn_setup():
        import jax, jax.numpy as jnp
        import numpy as np
        D_MODEL = 256
        N_HEADS = 16
        D_K = D_MODEL // N_HEADS

        def _mha(Q, K, V, W_Q, b_Q, W_K, b_K, W_V, b_V, W_O, b_O):
            B, S, _ = Q.shape

            def proj(x, W, b):
                y = jnp.einsum('bsd,de->bse', x, W) + b
                return y.reshape(B, S, N_HEADS, D_K).transpose(0, 2, 1, 3)
            q = proj(Q, W_Q, b_Q)
            k = proj(K, W_K, b_K)
            v = proj(V, W_V, b_V)
            scores = jnp.einsum('bhqd,bhkd->bhqk', q, k) / jnp.sqrt(jnp.float32(D_K))
            attn = jax.nn.softmax(scores, axis=-1)
            out = jnp.einsum('bhqk,bhkd->bhqd', attn, v)
            out = out.transpose(0, 2, 1, 3).reshape(B, S, D_MODEL)
            return jnp.einsum('bsd,de->bse', out, W_O) + b_O
        key = jax.random.key(seed)
        ks = jax.random.split(key, 11)
        B, S = (2, 512)
        scale = 1.0 / np.sqrt(D_MODEL)
        inp = {'Q': jax.random.normal(ks[0], (B, S, D_MODEL), jnp.float32), 'K': jax.random.normal(ks[1], (B, S, D_MODEL), jnp.float32), 'V': jax.random.normal(ks[2], (B, S, D_MODEL), jnp.float32), 'W_Q': jax.random.normal(ks[3], (D_MODEL, D_MODEL), jnp.float32) * scale, 'b_Q': jnp.zeros((D_MODEL,), jnp.float32), 'W_K': jax.random.normal(ks[4], (D_MODEL, D_MODEL), jnp.float32) * scale, 'b_K': jnp.zeros((D_MODEL,), jnp.float32), 'W_V': jax.random.normal(ks[5], (D_MODEL, D_MODEL), jnp.float32) * scale, 'b_V': jnp.zeros((D_MODEL,), jnp.float32), 'W_O': jax.random.normal(ks[6], (D_MODEL, D_MODEL), jnp.float32) * scale, 'b_O': jnp.zeros((D_MODEL,), jnp.float32)}
        return inp
    _L0_xattn_all = _L0_xattn_setup()
    _L0_xattn_in = {k: v for k, v in _L0_xattn_all.items() if k in ('W_Q', 'b_Q', 'W_K', 'b_K', 'W_V', 'b_V', 'W_O', 'b_O')}
    del _L0_xattn_all

    def _L0_ffn_setup():
        import jax, jax.numpy as jnp
        import numpy as np
        B, S, H, E = (2, 2048, 256, 8)
        SCALE = 0.5
        key = jax.random.key(seed)
        k1, k2 = jax.random.split(key)
        x = jax.random.normal(k1, (B, S, H), dtype=jnp.float32)
        gate_w = jax.random.normal(k2, (E, H), dtype=jnp.float32) * 0.02
        coeff = SCALE * (1.0 + 0.05 * jnp.arange(E, dtype=jnp.float32))
        expert_w = coeff[:, None, None] * jnp.eye(H, dtype=jnp.float32)
        return {'x': x, 'gate_w': gate_w, 'expert_w': expert_w}
    _L0_ffn_all = _L0_ffn_setup()
    _L0_ffn_in = {k: v for k, v in _L0_ffn_all.items() if k in ('gate_w', 'expert_w')}
    del _L0_ffn_all

    def _L1_xattn_setup():
        import jax, jax.numpy as jnp
        import numpy as np
        DIM, HEADS, DEPTH, SEQ, LOCAL_W = (256, 16, 7, 512, 64)
        HEAD_DIM = DIM // HEADS
        SCALE = 1.0 / HEAD_DIM ** 0.5

        def cantor_mask(S, depth, local_window):
            idx = np.arange(S)
            d = np.abs(idx[:, None] - idx[None, :])
            x = d.copy()
            ok = np.ones_like(d, dtype=bool)
            for _ in range(depth):
                ok &= x % 3 != 1
                x //= 3
            ok &= x == 0
            return jnp.asarray(ok | (d <= local_window))
        key = jax.random.key(seed)
        ks = jax.random.split(key, 8)
        B = 2
        s = 0.02
        return {'query': jax.random.normal(ks[0], (B, SEQ, DIM), jnp.float32), 'key_value': jax.random.normal(ks[1], (B, SEQ, DIM), jnp.float32), 'Wq': jax.random.normal(ks[2], (DIM, DIM), jnp.float32) * s, 'bq': jnp.zeros((DIM,), jnp.float32), 'Wkv': jax.random.normal(ks[3], (DIM, 2 * DIM), jnp.float32) * s, 'bkv': jnp.zeros((2 * DIM,), jnp.float32), 'Wo': jax.random.normal(ks[4], (DIM, DIM), jnp.float32) * s, 'bo': jnp.zeros((DIM,), jnp.float32)}
    _L1_xattn_all = _L1_xattn_setup()
    _L1_xattn_in = {k: v for k, v in _L1_xattn_all.items() if k in ('Wq', 'bq', 'Wkv', 'bkv', 'Wo', 'bo')}
    del _L1_xattn_all

    def _L1_ffn_setup():
        import jax, jax.numpy as jnp
        import numpy as np
        B, S, DIM = (4, 1024, 256)
        BASE_COUPLING = 0.1
        NUM_CYCLES = 3

        def _gelu(x):
            return jax.nn.gelu(x, approximate=False)

        def _coupling_net(h, w1, b1, w2, b2, w3, b3, w4, b4):
            h = _gelu(h @ w1 + b1)
            h = _gelu(h @ w2 + b2)
            h = _gelu(h @ w3 + b3)
            return jax.nn.sigmoid(h @ w4 + b4)

        def _global_net(h, w1, b1, w2, b2, w3, b3):
            h = _gelu(h @ w1 + b1)
            h = _gelu(h @ w2 + b2)
            return jax.nn.sigmoid(h @ w3 + b3)

        def _twist(x):
            o_r, o_i, p_r, p_i = jnp.split(x, 4, axis=-1)
            return jnp.concatenate([p_r, -p_i, -o_r, o_i], axis=-1)
        key = jax.random.key(seed)
        ks = jax.random.split(key, 9)
        d = DIM

        def w(k, fan_in, fan_out):
            return jax.random.normal(k, (fan_in, fan_out), dtype=jnp.float32) / np.sqrt(fan_in).astype(np.float32)
        inp = {'x': jax.random.normal(ks[0], (B, S, d), dtype=jnp.float32)}
        cn_dims = [(d, d), (d, d // 2), (d // 2, d // 4), (d // 4, 1)]
        for i, (a, b) in enumerate(cn_dims):
            inp[f'cn_w{i + 1}'] = w(ks[1 + i], a, b)
            inp[f'cn_b{i + 1}'] = jnp.zeros((b,), dtype=jnp.float32)
        gc_dims = [(d, d // 2), (d // 2, d // 4), (d // 4, 1)]
        for i, (a, b) in enumerate(gc_dims):
            inp[f'gc_w{i + 1}'] = w(ks[5 + i], a, b)
            inp[f'gc_b{i + 1}'] = jnp.zeros((b,), dtype=jnp.float32)
        inp['adaptive_range'] = jnp.full((1,), 0.2, dtype=jnp.float32)
        return inp
    _L1_ffn_all = _L1_ffn_setup()
    _L1_ffn_in = {k: v for k, v in _L1_ffn_all.items() if k in ('cn_w1', 'cn_b1', 'cn_w2', 'cn_b2', 'cn_w3', 'cn_b3', 'cn_w4', 'cn_b4', 'gc_w1', 'gc_b1', 'gc_w2', 'gc_b2', 'gc_w3', 'gc_b3', 'adaptive_range')}
    del _L1_ffn_all

    def _L2_xattn_setup():
        import jax, jax.numpy as jnp
        import numpy as np
        B, S, D, H = (4, 1024, 256, 16)
        DV = D // H
        key = jax.random.key(seed)
        ks = jax.random.split(key, 8)

        def gl(k, shape):
            fan_in, fan_out = (shape[0], shape[-1])
            lim = np.sqrt(6.0 / (fan_in + fan_out)).astype(np.float32)
            return jax.random.uniform(k, shape, jnp.float32, -lim, lim)
        return {'q': jax.random.normal(ks[0], (B, S, D), jnp.float32), 'k': jax.random.normal(ks[1], (B, S, D), jnp.float32), 'v': jax.random.normal(ks[2], (B, S, D), jnp.float32), 'wq': gl(ks[3], (D, H)), 'bq': jnp.zeros((H,), jnp.float32), 'wk': gl(ks[4], (D, H)), 'bk': jnp.zeros((H,), jnp.float32), 'wv': gl(ks[5], (D, D)), 'bv': jnp.zeros((D,), jnp.float32), 'wo': gl(ks[6], (D, D)), 'bo': jnp.zeros((D,), jnp.float32)}
    _L2_xattn_all = _L2_xattn_setup()
    _L2_xattn_in = {k: v for k, v in _L2_xattn_all.items() if k in ('wq', 'bq', 'wk', 'bk', 'wv', 'bv', 'wo', 'bo')}
    del _L2_xattn_all

    def _L2_ffn_setup():
        import jax, jax.numpy as jnp
        import numpy as np
        B, S, D, O, E, R = (8, 512, 256, 256, 8, 4)
        TOP_K = 2
        SCALING = 4.0 / 4.0
        key = jax.random.key(seed)
        k0, k1, k2, k3, k4 = jax.random.split(key, 5)
        hidden_states = jax.random.normal(k0, (B, S, D), dtype=jnp.float32)
        W_lin = jax.random.normal(k1, (O, D), dtype=jnp.float32) * 0.02
        b_lin = jnp.zeros((O,), dtype=jnp.float32)
        gate_w = jax.random.normal(k2, (E, D), dtype=jnp.float32) * 0.02
        left = jax.random.normal(k3, (E, D, R), dtype=jnp.float32) * 0.02
        right = jax.random.normal(k4, (E, R, O), dtype=jnp.float32) * 0.02
        return {'hidden_states': hidden_states, 'W_lin': W_lin, 'b_lin': b_lin, 'gate_w': gate_w, 'left': left, 'right': right}
    _L2_ffn_all = _L2_ffn_setup()
    _L2_ffn_in = {k: v for k, v in _L2_ffn_all.items() if k in ('W_lin', 'b_lin', 'gate_w', 'left', 'right')}
    del _L2_ffn_all

    def _L3_xattn_setup():
        import jax, jax.numpy as jnp
        import numpy as np
        import math
        B, L, D, NUM_HEADS = (4, 512, 256, 16)
        HEAD_SIZE = D // NUM_HEADS
        key = jax.random.key(seed)
        ks = jax.random.split(key, 9)
        s = 1.0 / math.sqrt(D)
        return {'query_states': jax.random.normal(ks[0], (B, L, D), jnp.float32), 'key_states': jax.random.normal(ks[1], (B, L, D), jnp.float32), 'value_states': jax.random.normal(ks[2], (B, L, D), jnp.float32), 'attention_mask': jnp.ones((B, L), jnp.float32), 'Wq': jax.random.normal(ks[3], (D, D), jnp.float32) * s, 'bq': jnp.zeros((D,), jnp.float32), 'Wk': jax.random.normal(ks[4], (D, D), jnp.float32) * s, 'bk': jnp.zeros((D,), jnp.float32), 'Wv': jax.random.normal(ks[5], (D, D), jnp.float32) * s, 'bv': jnp.zeros((D,), jnp.float32)}
    _L3_xattn_all = _L3_xattn_setup()
    _L3_xattn_in = {k: v for k, v in _L3_xattn_all.items() if k in ('Wq', 'bq', 'Wk', 'bk', 'Wv', 'bv')}
    del _L3_xattn_all

    def _L3_ffn_setup():
        import jax, jax.numpy as jnp
        import numpy as np
        DIM = 256
        HIDDEN = 768
        SCALE = 1.0 / 127.0

        def _dequant(w_int, dtype):
            return w_int.astype(dtype) * jnp.asarray(SCALE, dtype)
        key = jax.random.key(seed)
        k_x, k_g, k_u, k_d = jax.random.split(key, 4)
        x = jax.random.normal(k_x, (4, 512, DIM), dtype=jnp.float32)
        w_gate = jax.random.randint(k_g, (HIDDEN, DIM), -127, 128, dtype=jnp.int32)
        w_up = jax.random.randint(k_u, (HIDDEN, DIM), -127, 128, dtype=jnp.int32)
        w_down = jax.random.randint(k_d, (DIM, HIDDEN), -127, 128, dtype=jnp.int32)
        return {'x': x, 'w_gate': w_gate, 'w_up': w_up, 'w_down': w_down}
    _L3_ffn_all = _L3_ffn_setup()
    _L3_ffn_in = {k: v for k, v in _L3_ffn_all.items() if k in ('w_gate', 'w_up', 'w_down')}
    del _L3_ffn_all
    return {'x': x, 'ctx_1024': ctx_1024, 'mask_BxS2_ff1': mask_BxS2_ff1, 'L0_xattn_W_Q': _L0_xattn_in['W_Q'], 'L0_xattn_b_Q': _L0_xattn_in['b_Q'], 'L0_xattn_W_K': _L0_xattn_in['W_K'], 'L0_xattn_b_K': _L0_xattn_in['b_K'], 'L0_xattn_W_V': _L0_xattn_in['W_V'], 'L0_xattn_b_V': _L0_xattn_in['b_V'], 'L0_xattn_W_O': _L0_xattn_in['W_O'], 'L0_xattn_b_O': _L0_xattn_in['b_O'], 'L0_ffn_gate_w': _L0_ffn_in['gate_w'], 'L0_ffn_expert_w': _L0_ffn_in['expert_w'], 'L1_xattn_Wq': _L1_xattn_in['Wq'], 'L1_xattn_bq': _L1_xattn_in['bq'], 'L1_xattn_Wkv': _L1_xattn_in['Wkv'], 'L1_xattn_bkv': _L1_xattn_in['bkv'], 'L1_xattn_Wo': _L1_xattn_in['Wo'], 'L1_xattn_bo': _L1_xattn_in['bo'], 'L1_ffn_cn_w1': _L1_ffn_in['cn_w1'], 'L1_ffn_cn_b1': _L1_ffn_in['cn_b1'], 'L1_ffn_cn_w2': _L1_ffn_in['cn_w2'], 'L1_ffn_cn_b2': _L1_ffn_in['cn_b2'], 'L1_ffn_cn_w3': _L1_ffn_in['cn_w3'], 'L1_ffn_cn_b3': _L1_ffn_in['cn_b3'], 'L1_ffn_cn_w4': _L1_ffn_in['cn_w4'], 'L1_ffn_cn_b4': _L1_ffn_in['cn_b4'], 'L1_ffn_gc_w1': _L1_ffn_in['gc_w1'], 'L1_ffn_gc_b1': _L1_ffn_in['gc_b1'], 'L1_ffn_gc_w2': _L1_ffn_in['gc_w2'], 'L1_ffn_gc_b2': _L1_ffn_in['gc_b2'], 'L1_ffn_gc_w3': _L1_ffn_in['gc_w3'], 'L1_ffn_gc_b3': _L1_ffn_in['gc_b3'], 'L1_ffn_adaptive_range': _L1_ffn_in['adaptive_range'], 'L2_xattn_wq': _L2_xattn_in['wq'], 'L2_xattn_bq': _L2_xattn_in['bq'], 'L2_xattn_wk': _L2_xattn_in['wk'], 'L2_xattn_bk': _L2_xattn_in['bk'], 'L2_xattn_wv': _L2_xattn_in['wv'], 'L2_xattn_bv': _L2_xattn_in['bv'], 'L2_xattn_wo': _L2_xattn_in['wo'], 'L2_xattn_bo': _L2_xattn_in['bo'], 'L2_ffn_W_lin': _L2_ffn_in['W_lin'], 'L2_ffn_b_lin': _L2_ffn_in['b_lin'], 'L2_ffn_gate_w': _L2_ffn_in['gate_w'], 'L2_ffn_left': _L2_ffn_in['left'], 'L2_ffn_right': _L2_ffn_in['right'], 'L3_xattn_Wq': _L3_xattn_in['Wq'], 'L3_xattn_bq': _L3_xattn_in['bq'], 'L3_xattn_Wk': _L3_xattn_in['Wk'], 'L3_xattn_bk': _L3_xattn_in['bk'], 'L3_xattn_Wv': _L3_xattn_in['Wv'], 'L3_xattn_bv': _L3_xattn_in['bv'], 'L3_ffn_w_gate': _L3_ffn_in['w_gate'], 'L3_ffn_w_up': _L3_ffn_in['w_up'], 'L3_ffn_w_down': _L3_ffn_in['w_down']}

def reference(x, ctx_1024, mask_BxS2_ff1, L0_xattn_W_Q, L0_xattn_b_Q, L0_xattn_W_K, L0_xattn_b_K, L0_xattn_W_V, L0_xattn_b_V, L0_xattn_W_O, L0_xattn_b_O, L0_ffn_gate_w, L0_ffn_expert_w, L1_xattn_Wq, L1_xattn_bq, L1_xattn_Wkv, L1_xattn_bkv, L1_xattn_Wo, L1_xattn_bo, L1_ffn_cn_w1, L1_ffn_cn_b1, L1_ffn_cn_w2, L1_ffn_cn_b2, L1_ffn_cn_w3, L1_ffn_cn_b3, L1_ffn_cn_w4, L1_ffn_cn_b4, L1_ffn_gc_w1, L1_ffn_gc_b1, L1_ffn_gc_w2, L1_ffn_gc_b2, L1_ffn_gc_w3, L1_ffn_gc_b3, L1_ffn_adaptive_range, L2_xattn_wq, L2_xattn_bq, L2_xattn_wk, L2_xattn_bk, L2_xattn_wv, L2_xattn_bv, L2_xattn_wo, L2_xattn_bo, L2_ffn_W_lin, L2_ffn_b_lin, L2_ffn_gate_w, L2_ffn_left, L2_ffn_right, L3_xattn_Wq, L3_xattn_bq, L3_xattn_Wk, L3_xattn_bk, L3_xattn_Wv, L3_xattn_bv, L3_ffn_w_gate, L3_ffn_w_up, L3_ffn_w_down):
    import jax
    import jax.numpy as jnp

    def _L0_xattn_ref(Q, K, V, W_Q, b_Q, W_K, b_K, W_V, b_V, W_O, b_O):
        import jax, jax.numpy as jnp
        import numpy as np
        D_MODEL = 256
        N_HEADS = 16
        D_K = D_MODEL // N_HEADS

        def _mha(Q, K, V, W_Q, b_Q, W_K, b_K, W_V, b_V, W_O, b_O):
            B, S, _ = Q.shape

            def proj(x, W, b):
                y = jnp.einsum('bsd,de->bse', x, W) + b
                return y.reshape(B, S, N_HEADS, D_K).transpose(0, 2, 1, 3)
            q = proj(Q, W_Q, b_Q)
            k = proj(K, W_K, b_K)
            v = proj(V, W_V, b_V)
            scores = jnp.einsum('bhqd,bhkd->bhqk', q, k) / jnp.sqrt(jnp.float32(D_K))
            attn = jax.nn.softmax(scores, axis=-1)
            out = jnp.einsum('bhqk,bhkd->bhqd', attn, v)
            out = out.transpose(0, 2, 1, 3).reshape(B, S, D_MODEL)
            return jnp.einsum('bsd,de->bse', out, W_O) + b_O
        return _mha(Q, K, V, W_Q, b_Q, W_K, b_K, W_V, b_V, W_O, b_O)

    def _L0_ffn_ref(x, gate_w, expert_w):
        import jax, jax.numpy as jnp
        import numpy as np
        B, S, H, E = (2, 2048, 256, 8)
        SCALE = 0.5
        scores = jnp.einsum('bsh,eh->bse', x, gate_w)
        chosen = jnp.argmax(scores, axis=-1)
        onehot = jax.nn.one_hot(chosen, gate_w.shape[0], dtype=x.dtype)
        expert_out = jnp.einsum('bsh,efh->bsef', x, expert_w)
        return x + jnp.einsum('bsef,bse->bsf', expert_out, onehot)

    def _L1_xattn_ref(query, key_value, Wq, bq, Wkv, bkv, Wo, bo):
        import jax, jax.numpy as jnp
        import numpy as np
        DIM, HEADS, DEPTH, SEQ, LOCAL_W = (256, 16, 7, 512, 64)
        HEAD_DIM = DIM // HEADS
        SCALE = 1.0 / HEAD_DIM ** 0.5

        def cantor_mask(S, depth, local_window):
            idx = np.arange(S)
            d = np.abs(idx[:, None] - idx[None, :])
            x = d.copy()
            ok = np.ones_like(d, dtype=bool)
            for _ in range(depth):
                ok &= x % 3 != 1
                x //= 3
            ok &= x == 0
            return jnp.asarray(ok | (d <= local_window))
        B, S, D = query.shape
        H, hd = (HEADS, HEAD_DIM)
        mask = cantor_mask(S, DEPTH, LOCAL_W)
        q = (query @ Wq + bq).reshape(B, S, H, hd).transpose(0, 2, 1, 3)
        kv = (key_value @ Wkv + bkv).reshape(B, S, 2, H, hd).transpose(2, 0, 3, 1, 4)
        k, v = (kv[0], kv[1])
        scores = jnp.einsum('bhqd,bhkd->bhqk', q, k) * SCALE
        scores = jnp.where(mask, scores, jnp.finfo(scores.dtype).min)
        attn = jax.nn.softmax(scores, axis=-1)
        out = jnp.einsum('bhqk,bhkd->bhqd', attn, v)
        out = out.transpose(0, 2, 1, 3).reshape(B, S, D)
        return out @ Wo + bo

    def _L1_ffn_ref(x, cn_w1, cn_b1, cn_w2, cn_b2, cn_w3, cn_b3, cn_w4, cn_b4, gc_w1, gc_b1, gc_w2, gc_b2, gc_w3, gc_b3, adaptive_range):
        import jax, jax.numpy as jnp
        import numpy as np
        B, S, DIM = (4, 1024, 256)
        BASE_COUPLING = 0.1
        NUM_CYCLES = 3

        def _gelu(x):
            return jax.nn.gelu(x, approximate=False)

        def _coupling_net(h, w1, b1, w2, b2, w3, b3, w4, b4):
            h = _gelu(h @ w1 + b1)
            h = _gelu(h @ w2 + b2)
            h = _gelu(h @ w3 + b3)
            return jax.nn.sigmoid(h @ w4 + b4)

        def _global_net(h, w1, b1, w2, b2, w3, b3):
            h = _gelu(h @ w1 + b1)
            h = _gelu(h @ w2 + b2)
            return jax.nn.sigmoid(h @ w3 + b3)

        def _twist(x):
            o_r, o_i, p_r, p_i = jnp.split(x, 4, axis=-1)
            return jnp.concatenate([p_r, -p_i, -o_r, o_i], axis=-1)
        global_context = x.mean(axis=1, keepdims=True)
        gf = _global_net(global_context, gc_w1, gc_b1, gc_w2, gc_b2, gc_w3, gc_b3)
        out = x
        for _ in range(NUM_CYCLES):
            tf = _coupling_net(out, cn_w1, cn_b1, cn_w2, cn_b2, cn_w3, cn_b3, cn_w4, cn_b4)
            combined = 0.7 * gf + 0.3 * tf
            coupling = BASE_COUPLING + adaptive_range * (combined - 0.5) * 2.0
            out = out + coupling * _twist(out)
        return out

    def _L2_xattn_ref(q, k, v, wq, bq, wk, bk, wv, bv, wo, bo):
        import jax, jax.numpy as jnp
        import numpy as np
        B, S, D, H = (4, 1024, 256, 16)
        DV = D // H
        b, s, d = q.shape
        h = wq.shape[1]
        dv = d // h
        qh = jax.nn.sigmoid(q @ wq + bq)
        kh = jax.nn.sigmoid(k @ wk + bk)
        vh = (v @ wv + bv).reshape(b, s, h, dv)
        kv = jnp.einsum('bsh,bshd->bhd', kh, vh)
        state = jnp.cumsum(kv, axis=1)
        out_h = jnp.einsum('bsh,bhd->bshd', qh, state)
        concat = out_h.reshape(b, s, d)
        return concat @ wo + bo

    def _L2_ffn_ref(hidden_states, W_lin, b_lin, gate_w, left, right):
        import jax, jax.numpy as jnp
        import numpy as np
        B, S, D, O, E, R = (8, 512, 256, 256, 8, 4)
        TOP_K = 2
        SCALING = 4.0 / 4.0
        bsz, seq, d_in = hidden_states.shape
        x = hidden_states.reshape(-1, d_in)
        logits = x @ gate_w.T
        scores = jax.nn.softmax(logits, axis=-1)
        weights, idx = jax.lax.top_k(scores, TOP_K)
        base = x @ W_lin.T + b_lin
        left_sel = left[idx]
        right_sel = right[idx]
        t = jnp.einsum('nd,nkdr->nkr', x, left_sel)
        out_k = jnp.einsum('nkr,nkro->nko', t, right_sel)
        lora = jnp.sum(weights[..., None] * out_k, axis=1) * SCALING
        return (base + lora).reshape(bsz, seq, -1)

    def _L3_xattn_ref(query_states, key_states, value_states, attention_mask, Wq, bq, Wk, bk, Wv, bv):
        import jax, jax.numpy as jnp
        import numpy as np
        import math
        B, L, D, NUM_HEADS = (4, 512, 256, 16)
        HEAD_SIZE = D // NUM_HEADS
        q = jnp.einsum('bld,de->ble', query_states, Wq) + bq
        k = jnp.einsum('bld,de->ble', key_states, Wk) + bk
        v = jnp.einsum('bld,de->ble', value_states, Wv) + bv
        scores = jnp.einsum('bqd,bkd->bqk', q, k) / math.sqrt(HEAD_SIZE)
        scores = scores + (1.0 - attention_mask)[:, None, :] * -10000.0
        probs = jax.nn.softmax(scores, axis=-1)
        context = jnp.einsum('bqk,bkd->bqd', probs, v)
        return context

    def _L3_ffn_ref(x, w_gate, w_up, w_down):
        import jax, jax.numpy as jnp
        import numpy as np
        DIM = 256
        HIDDEN = 768
        SCALE = 1.0 / 127.0

        def _dequant(w_int, dtype):
            return w_int.astype(dtype) * jnp.asarray(SCALE, dtype)
        wg = _dequant(w_gate, x.dtype)
        wu = _dequant(w_up, x.dtype)
        wd = _dequant(w_down, x.dtype)
        gate = jnp.einsum('bsd,hd->bsh', x, wg)
        up = jnp.einsum('bsd,hd->bsh', x, wu)
        h = jax.nn.silu(gate) * up
        return jnp.einsum('bsh,dh->bsd', h, wd)
    x = x + _L0_xattn_ref(_layernorm(x, axis=-1), ctx_1024, ctx_1024, L0_xattn_W_Q, L0_xattn_b_Q, L0_xattn_W_K, L0_xattn_b_K, L0_xattn_W_V, L0_xattn_b_V, L0_xattn_W_O, L0_xattn_b_O)
    x = x + _L0_ffn_ref(_layernorm(x, axis=-1), L0_ffn_gate_w, L0_ffn_expert_w)
    x = x + _L1_xattn_ref(_layernorm(x, axis=-1), ctx_1024, L1_xattn_Wq, L1_xattn_bq, L1_xattn_Wkv, L1_xattn_bkv, L1_xattn_Wo, L1_xattn_bo)
    x = x + _L1_ffn_ref(_layernorm(x, axis=-1), L1_ffn_cn_w1, L1_ffn_cn_b1, L1_ffn_cn_w2, L1_ffn_cn_b2, L1_ffn_cn_w3, L1_ffn_cn_b3, L1_ffn_cn_w4, L1_ffn_cn_b4, L1_ffn_gc_w1, L1_ffn_gc_b1, L1_ffn_gc_w2, L1_ffn_gc_b2, L1_ffn_gc_w3, L1_ffn_gc_b3, L1_ffn_adaptive_range)
    x = x + _L2_xattn_ref(_layernorm(x, axis=-1), ctx_1024, ctx_1024, L2_xattn_wq, L2_xattn_bq, L2_xattn_wk, L2_xattn_bk, L2_xattn_wv, L2_xattn_bv, L2_xattn_wo, L2_xattn_bo)
    x = x + _L2_ffn_ref(_layernorm(x, axis=-1), L2_ffn_W_lin, L2_ffn_b_lin, L2_ffn_gate_w, L2_ffn_left, L2_ffn_right)
    x = x + _L3_xattn_ref(_layernorm(x, axis=-1), ctx_1024, ctx_1024, mask_BxS2_ff1, L3_xattn_Wq, L3_xattn_bq, L3_xattn_Wk, L3_xattn_bk, L3_xattn_Wv, L3_xattn_bv)
    x = x + _L3_ffn_ref(_layernorm(x, axis=-1), L3_ffn_w_gate, L3_ffn_w_up, L3_ffn_w_down)
    return x

_drawn_inputs = setup_inputs


def setup_inputs(seed=0):
    import zlib

    import numpy as np

    out = dict(_drawn_inputs(seed))
    spreads = {'L0_xattn_b_Q': (0.0, 0.571),
     'L0_xattn_b_K': (0.0, 2.0),
     'L0_xattn_b_V': (0.0, 0.1),
     'L0_xattn_b_O': (0.0, 0.1),
     'L1_xattn_bq': (0.0, 0.8),
     'L1_xattn_bkv': (0.0, 0.8),
     'L1_xattn_bo': (0.0, 0.274),
     'L1_ffn_cn_b1': (0.0, 2.0),
     'L1_ffn_cn_b2': (0.0, 2.0),
     'L1_ffn_cn_b3': (0.0, 2.0),
     'L1_ffn_gc_b1': (0.0, 2.0),
     'L1_ffn_gc_b2': (0.0, 2.0),
     'L2_xattn_bq': (0.0, 0.1),
     'L2_xattn_bk': (0.0, 0.1),
     'L2_xattn_bv': (0.0, 0.1),
     'L2_xattn_bo': (0.0, 2.0),
     'L2_ffn_b_lin': (0.0, 2.0),
     'L3_xattn_bq': (0.0, 0.8),
     'L3_xattn_bk': (0.0, 2.0),
     'L3_xattn_bv': (0.0, 2.0)}
    factors = {'L0_ffn_gate_w': 200.0,
     'L1_xattn_Wq': 8.0,
     'L1_xattn_Wkv': 4.744,
     'L1_xattn_Wo': 4.434,
     'L1_ffn_cn_w1': 80.003,
     'L1_ffn_cn_w2': 73.139,
     'L1_ffn_cn_w3': 8.0,
     'L1_ffn_cn_w4': 21.42,
     'L1_ffn_gc_w1': 8.0,
     'L1_ffn_gc_w2': 8.0,
     'L1_ffn_gc_w3': 8.0,
     'L2_ffn_W_lin': 8.0,
     'L2_ffn_gate_w': 56.281,
     'L2_ffn_left': 46.335,
     'L2_ffn_right': 48.567,
     'L3_xattn_Wq': 5.014,
     'L3_xattn_Wk': 5.123,
     'L3_xattn_Wv': 4.408}
    for name, (base, spread) in spreads.items():
        noise = np.random.default_rng([zlib.crc32(name.encode()), seed]).standard_normal(out[name].shape)
        drawn = base * np.exp(spread * noise) if base else spread * noise
        out[name] = jnp.asarray(drawn.astype(out[name].dtype))
    for name, factor in factors.items():
        out[name] = (out[name] * factor).astype(out[name].dtype)
    return out
```

```python
import numpy as np
import concourse.bass as bass
from concourse import mybir
from contextlib import ExitStack

F32 = mybir.dt.float32
BF16 = mybir.dt.bfloat16
I32 = mybir.dt.int32
ALU = mybir.AluOpType
ACT = mybir.ActivationFunctionType
AX = mybir.AxisListType

P = 128
B, S, D = 8, 256, 256
LANES = 2
ITERS = B // LANES
T = S // P
KT = D // P
H, HD = 16, 16
GH = 4
ITEMS = LANES * H // GH
PARTS = 6
QPART = [0, 0, 1, 1, 0, 2]
KPART = [0, 1, 0, 1, 2, 0]
KR = PARTS * HD
KM = KR + 2
E = 8
R = 4
HID = 768
HT = HID // P
LAYERS = 8
EPS = 1e-5
OFF = -1.0e30


def cantor_mask():
    idx = np.arange(S)
    d = np.abs(idx[:, None] - idx[None, :])
    x, ok = d.copy(), np.ones_like(d, dtype=bool)
    for _ in range(7):
        ok &= x % 3 != 1
        x //= 3
    ok &= x == 0
    return ok | (d <= 64)


PACK = [
    ("ident", P, P), ("wk0", P, KT * D), ("bk0", P, KT), ("wv0", P, KT * D), ("bv0", P, D),
    ("wq0", P, KT * D), ("bq0", P, KT), ("wo0", P, KT * D), ("bo0", P, D),
    "cut",
    ("gate0", P, KT * E), ("desc", P, E), ("wk1", P, KT * D), ("bk1", P, KT), ("wv1", P, KT * D),
    ("bv1", P, D), ("wq1", P, KT * D), ("bq1", P, KT), ("wo1", P, KT * D), ("bo1", P, D),
    "cut",
    ("exp0", P, KT * E * D),
    "cut",
    ("cw1", P, KT * D), ("cb1", P, KT), ("cw2", P, KT * P), ("cb2", P, 1), ("cw3", P, 64), ("cb3", 64, 1),
    ("cw4", 64, 1), ("cb4", P, 1), ("gw1", P, KT * P), ("gb1", P, 1), ("gw2", P, 64), ("gb2", 64, 1),
    ("gw3", 64, 1), ("gb3", P, 1), ("range", P, 1), ("mean", P, 1),
    ("aq", P, KT * H), ("ak", P, KT * H), ("baq", H, 1), ("bak", P, T * H), ("av", P, KT * D),
    ("bav", 1, D), ("ao", P, KT * D), ("bao", P, D), ("diag", H, D), ("tri", H, H), ("pick", P, KT * H),
    ("ones", P, P),
    "cut",
    ("lin", P, KT * D), ("blin", P, D), ("gl", P, KT * (E + E * R)), ("right", E * R, D),
    ("wq3", P, KT * D), ("bq3", P, KT), ("wk3", P, KT * D), ("bk3", P, KT), ("wv3", P, KT * D), ("bv3", P, D),
]
COLS, CUTS = {}, [0]
_at = 0
for _e in PACK:
    if _e == "cut":
        CUTS.append(_at)
    else:
        COLS[_e[0]] = (_at, _e[1], _e[2])
        _at += _e[2]
NCOLS = _at
CUTS.append(NCOLS)
IPACK = [("wg", KT * HID), ("wu", KT * HID), ("wd", HT * D)]
NI = sum(n for _, n in IPACK)


def program(nc, x_in, ctx_in, mask_in, pack, nomask, ipack, scratch, out):
    ctx = ExitStack()
    with ctx:
        def sb(name, shape, dt=F32):
            return ctx.enter_context(nc.sbuf_tensor(name, shape, dt))

        per = {}

        def sem(name, n=0):
            s = ctx.enter_context(nc.semaphore(name))
            per[s.name] = n
            return s

        def lane_sem(name, n):
            return [sem(f"{name}{b}", n) for b in range(LANES)]

        def nth(s, it, n):
            return it * per[s.name] + n

        w = sb("w", [P, NCOLS])
        wi = sb("wi", [P, NI])

        def W(name, *dims):
            at, p, n = COLS[name]
            v = w[0:p, at:at + n]
            return v.rearrange("p (a b) -> p a b", a=dims[0]) if dims else v

        ident = W("ident")
        identb = sb("identb", [P, P], BF16)
        maskb = sb("maskb", [P, T, S], BF16)
        bqs = [sb(f"bqs{m}", [P, KT]) for m in range(3)]
        hb4 = sb("hb4", [P, 1])
        hb3 = sb("hb3", [P, 1])
        nbaq = sb("nbaq", [H, 1])
        powm = sb("powm", [P, T])
        epsm = sb("epsm", [P, T])
        junk = sb("junk", [1, 1])
        xin = [sb(f"xin{b}", [P, T, D]) for b in range(LANES)]
        cin = [sb(f"cin{b}", [P, T, D]) for b in range(LANES)]
        mrow = [sb(f"mrow{b}", [1, S]) for b in range(LANES)]
        x = [sb(f"x{b}", [P, T, D]) for b in range(LANES)]
        xb = [sb(f"xb{b}", [P, T, D]) for b in range(LANES)]
        xh = [sb(f"xh{b}", [P, T, D]) for b in range(LANES)]
        xhT = [sb(f"xhT{b}", [P, KT, S]) for b in range(LANES)]
        ctxT = [sb(f"ctxT{b}", [P, KT, S]) for b in range(LANES)]
        bst = [sb(f"bst{b}", [P, T, 6]) for b in range(LANES)]
        mv = [sb(f"mv{b}", [P, T, 2]) for b in range(LANES)]
        veps = [sb(f"veps{b}", [P, T]) for b in range(LANES)]
        rstd = [sb(f"rstd{b}", [P, T]) for b in range(LANES)]
        kf = [sb(f"kf{b}", [P, KT, S]) for b in range(LANES)]
        qf = [sb(f"qf{b}", [P, KT, S]) for b in range(LANES)]
        resid = [sb(f"resid{b}", [P, KT, S]) for b in range(LANES)]
        kparts = [sb(f"kparts{b}", [P, KT, 3, S], BF16) for b in range(LANES)]
        qparts = kparts
        KA = [sb(f"KA{b}", [KM, H, S], BF16) for b in range(LANES)]
        QA = [sb(f"QA{b}", [KM, H, S], BF16) for b in range(LANES)]
        vaug = [sb(f"vaug{b}", [P, T, H, 32]) for b in range(LANES)]
        mx = sb("mx", [P, 2, GH, T])
        mq = sb("mq", [P, 2, T, 2, GH], BF16)
        negm = sb("negm", [2 * GH, 2, S], BF16)
        PT = [sb(f"PT{i}", [P, GH, T, S]) for i in range(2)]
        OT = [sb(f"OT{i}", [P, S]) for i in range(2)]
        rc = sb("rc", [P, T, GH])
        att = [sb(f"att{b}", [P, T, D]) for b in range(LANES)]
        attT = [sb(f"attT{b}", [P, KT, S]) for b in range(LANES)]
        sc = [sb(f"sc{b}", [P, T, E + E * R]) for b in range(LANES)]
        r1 = [sb(f"r1{b}", [P, T, E]) for b in range(LANES)]
        r2 = [sb(f"r2{b}", [P, T, E]) for b in range(LANES)]
        r3 = [sb(f"r3{b}", [P, T, E]) for b in range(LANES)]
        one = [sb(f"one{b}", [P, T, E]) for b in range(LANES)]
        m1 = [sb(f"m1{b}", [P, T]) for b in range(LANES)]
        m2 = [sb(f"m2{b}", [P, T]) for b in range(LANES)]
        o2, h1T, h2T = qf, kf, OT
        h3T = [sb(f"h3T{b}", [64, S]) for b in range(LANES)]
        gcT = [sb(f"gcT{b}", [P, KT]) for b in range(LANES)]
        g1 = [sb(f"g1{b}", [P, 1]) for b in range(LANES)]
        g2 = [sb(f"g2{b}", [64, P]) for b in range(LANES)]
        tg = [sb(f"tg{b}", [P, 1]) for b in range(LANES)]
        cbase = [sb(f"cbase{b}", [P, 1]) for b in range(LANES)]
        r03 = sb("r03", [P, 1])
        r07 = sb("r07", [P, 1])
        th = [sb(f"th{b}", [P, T]) for b in range(LANES)]
        cc = [sb(f"cc{b}", [P, T]) for b in range(LANES)]
        cn = [sb(f"cn{b}", [P, T]) for b in range(LANES)]
        kz = [sb(f"kz{b}", [P, T, H]) for b in range(LANES)]
        kh = [sb(f"kh{b}", [P, T, H]) for b in range(LANES)]
        qh = [sb(f"qh{b}", [H, S]) for b in range(LANES)]
        AT = [sb(f"AT{b}", [P, KT, H]) for b in range(LANES)]
        ks = [sb(f"ks{b}", [1, H]) for b in range(LANES)]
        kvm = [h3T[b][0:H, :] for b in range(LANES)]
        dg = [sb(f"dg{b}", [H, HD]) for b in range(LANES)]
        drep = [sb(f"drep{b}", [H, P]) for b in range(LANES)]
        sx = [sb(f"sx{b}", [P, KT, H]) for b in range(LANES)]
        mm = [sb(f"mm{b}", [H, D]) for b in range(LANES)]
        tw = [sb(f"tw{b}", [P, T, E * R]) for b in range(LANES)]
        twT = [h3T[b][0:E * R, :] for b in range(LANES)]
        v3 = resid
        rs = [sb(f"rs{b}", [P, T]) for b in range(LANES)]
        sg = attT
        hT = [PT[b][:, :, :, :].rearrange("p a b c -> p (a b) c") for b in range(LANES)]

        bank = [ctx.enter_context(nc.psum_tensor(f"bank{i}", [P, 512], F32)) for i in range(8)]
        dense = [[bank[4 * b + i] for i in range(4)] for b in range(LANES)]
        bank5b = bank[5][:, :].bitcast(BF16)

        w_in = [sem(f"w_in{n}") for n in range(len(CUTS) - 1)]
        wi_in = sem("wi_in")
        ready = sem("ready")
        wi_ready = sem("wi_ready")
        x_in_s = lane_sem("x_in", 16)
        c_in_s = lane_sem("c_in", 16)
        m_in_s = lane_sem("m_in", 16)
        ctx_ps = lane_sem("ctx_ps", 1)
        ctx_t = lane_sem("ctx_t", 1)
        stats = lane_sem("stats", LAYERS)
        rstd_s = lane_sem("rstd_s", LAYERS)
        xh_s = lane_sem("xh_s", LAYERS)
        xhT_ps = lane_sem("xhT_ps", LAYERS)
        xhT_s = lane_sem("xhT_s", LAYERS)
        xb_s = lane_sem("xb_s", 5)
        x_new = lane_sem("x_new", LAYERS - 1)
        k_ps, v_ps, q_ps = (lane_sem(n, 2) for n in ("k_ps", "v_ps", "q_ps"))
        k_f, q_f, v_s = (lane_sem(n, 2) for n in ("k_f", "q_f", "v_s"))
        k_split, q_split = (lane_sem(n, 2) for n in ("k_split", "q_split"))
        k_out, q_out = (lane_sem(n, 2 * 16) for n in ("k_out", "q_out"))
        k_rows, q_rows = (lane_sem(n, 2 * 16 * PARTS) for n in ("k_rows", "q_rows"))
        attT_ps, attT_s, o_ps = (lane_sem(n, 2) for n in ("attT_ps", "attT_s", "o_ps"))
        NI2 = 2 * ITEMS
        s_ps = sem("s_ps", NI2 * GH)
        max_s = sem("max_s", NI2 * GH)
        mq_s = sem("mq_s", NI2)
        mT_ps = sem("mT_ps", NI2)
        negm_s = sem("negm_s", NI2)
        m_rows = [sem(f"m_rows{i}", NI2 * 16) for i in range(2)]
        st_ps = sem("st_ps", NI2 * GH)
        exp_s = sem("exp_s", NI2 * GH)
        pv_ps = sem("pv_ps", NI2)
        ot_s = sem("ot_s", NI2)
        otT_ps = sem("otT_ps", NI2)
        att_s = sem("att_s", NI2)
        gate_ps = lane_sem("gate_ps", 1)
        one_s = lane_sem("one_s", 1)
        ex_ps = lane_sem("ex_ps", T * 4)
        ex_used = lane_sem("ex_used", T * 4)
        oT_ps, oT_s = (lane_sem(n, 2) for n in ("oT_ps", "oT_s"))
        o_new = lane_sem("o_new", 3)
        n1_ps = lane_sem("n1_ps", 6)
        n1_s = lane_sem("n1_s", 6)
        n2_ps, n2_s, n3_ps, n3_s, n4_ps, n4_s = (lane_sem(n, 3) for n in ("n2_ps", "n2_s", "n3_ps", "n3_s", "n4_ps", "n4_s"))
        gc_ps, gc_s = (lane_sem(n, 4) for n in ("gc_ps", "gc_s"))
        third_pe, third_act, third_dve = lane_sem("third_pe", 7), lane_sem("third_act", 4), lane_sem("third_dve", 5)
        rank_pe, rank_act, rank_dve = lane_sem("rank_pe", 3), lane_sem("rank_act", 2), lane_sem("rank_dve", 2)
        last_pe, last_act, last_dve = lane_sem("last_pe", 6), lane_sem("last_act", 4), lane_sem("last_dve", 3)
        gu_ps, silu_s, hid_s = (lane_sem(n, HT) for n in ("gu_ps", "silu_s", "hid_s"))
        dn_ps = lane_sem("dn_ps", 1)
        stored = lane_sem("stored", 16)
        DVE_LINKS, ACT_LINKS, POOL_LINKS = 0, 0, 0
        dve_own = sem("dve_own")
        pool_own = sem("pool_own")

        block = ctx.enter_context(nc.Block())

        item = [(b, g) for b in range(LANES) for g in range(H // GH)]
        MHA = {0: dict(k="wk0", bk="bk0", v="wv0", bv="bv0", q="wq0", o="wo0", bo="bo0"),
               1: dict(k="wk1", bk="bk1", v="wv1", bv="bv1", q="wq1", o="wo1", bo="bo1")}
        LANE = range(LANES)

        @block.sync
        def _(sp):
            for n in range(len(CUTS) - 1):
                sp.dma_start(w[:, CUTS[n]:CUTS[n + 1]], pack[:, CUTS[n]:CUTS[n + 1]]).then_inc(w_in[n], 16)
                if n == 0:
                    for b in LANE:
                        sp.dma_start(cin[b][:, :, :], ctx_in[b].rearrange("(t p) d -> p t d", p=P)).then_inc(c_in_s[b], 16)
                        sp.dma_start(xin[b][:, :, :], x_in[b].rearrange("(t p) d -> p t d", p=P)).then_inc(x_in_s[b], 16)
                        sp.dma_start(mrow[b][:, :], mask_in[b:b + 1, :]).then_inc(m_in_s[b], 16)
            for i in range(2):
                sp.dma_start(OT[i][:, :], nomask[:, i * S:(i + 1) * S]).then_inc(wi_in, 16)
            sp.dma_start(wi[:, :].bitcast(I32), ipack).then_inc(wi_in, 16)
            with sp.Fori(0, ITERS) as it:
                for m in range(2):
                    def rows(parts, dst, which, out_s, rows_s, split_s, b):
                        sp.wait_ge(split_s[b], nth(split_s[b], it, m + 1))
                        sp.dma_start(scratch[b, which].rearrange("(k p) c s -> p k c s", p=P),
                                     parts[b][:, :, :, :]).then_inc(out_s[b], 16)

                    def rows2(dst, which, part_of, out_s, rows_s, b):
                        sp.wait_ge(out_s[b], nth(out_s[b], it, 16 * (m + 1)))
                        for c in range(PARTS):
                            sp.dma_start(dst[b][c * HD:(c + 1) * HD, :, :],
                                         scratch[b, which, :, part_of[c], :].rearrange("(h d) s -> d h s", d=HD)
                                         ).then_inc(rows_s[b], 16)

                    for b in LANE:
                        rows(kparts, KA, 1, k_out, k_rows, k_split, b)
                    for b in LANE:
                        rows2(KA, 1, KPART, k_out, k_rows, b)
                    for b in LANE:
                        rows(qparts, QA, 0, q_out, q_rows, q_split, b)
                        rows2(QA, 0, QPART, q_out, q_rows, b)
                    for n, (b, g) in enumerate(item):
                        j = m * ITEMS + n
                        sp.wait_ge(negm_s, nth(negm_s, it, j + 1))
                        for c in range(2):
                            sp.dma_start(QA[b][KR + c:KR + c + 1, g * GH:(g + 1) * GH, :],
                                         negm[c * GH:(c + 1) * GH, j % 2, :]).then_inc(m_rows[j % 2], 16)
                for b in LANE:
                    sp.wait_ge(x_new[b], nth(x_new[b], it, LAYERS - 1))
                    sp.dma_start(out[bass.ds(it * LANES + b, 1), :, :].rearrange("a (t p) d -> p (a t) d", p=P),
                                 x[b][:, :, :]).then_inc(stored[b], 16)
                    nx = (it * LANES + LANES + b) % B
                    sp.wait_ge(stored[b], nth(stored[b], it, 16))
                    sp.dma_start(cin[b][:, :, :], ctx_in[bass.ds(nx, 1), :, :].rearrange("a (t p) d -> p (a t) d", p=P)
                                 ).then_inc(c_in_s[b], 16)
                    sp.dma_start(xin[b][:, :, :], x_in[bass.ds(nx, 1), :, :].rearrange("a (t p) d -> p (a t) d", p=P)
                                 ).then_inc(x_in_s[b], 16)
                    sp.dma_start(mrow[b][:, :], mask_in[bass.ds(nx, 1), :]).then_inc(m_in_s[b], 16)
            for b in LANE:
                sp.wait_ge(stored[b], 16 * ITERS)
                sp.wait_ge(x_in_s[b], 16 * (ITERS + 1))
                sp.wait_ge(c_in_s[b], 16 * (ITERS + 1))
                sp.wait_ge(m_in_s[b], 16 * (ITERS + 1))

        @block.gpsimd
        def _(pool):
            chain = [0]
            per[pool_own.name] = POOL_N = 2 * LAYERS + 2 * 2

            def link(ins, it=None):
                chain[0] += 1
                ins.then_inc(pool_own, 1)
                pool.wait_ge(pool_own, base + it * POOL_N + chain[0])

            base = 0
            pool.memset(powm[:, :], -0.5).then_inc(ready, 1)
            pool.memset(epsm[:, :], EPS).then_inc(ready, 1)
            for b in LANE:
                pool.memset(vaug[b][:, :, :, HD:32], 0.0).then_inc(pool_own, 1)
            pool.wait_ge(pool_own, LANES)
            for b in LANE:
                pool.memset(vaug[b][:, :, :, HD:HD + 1], 1.0).then_inc(ready, 1)
            base = LANES
            pool.wait_ge(ready, 2 + LANES)
            for n in range(len(CUTS) - 1):
                pool.wait_ge(w_in[n], 16)

            with pool.Fori(0, ITERS) as it:
                chain[0] = 0

                def norm(b, L):
                    pool.wait_ge(stats[b], nth(stats[b], it, L + 1))
                    link(pool.tensor_tensor(veps[b][:, :], mv[b][:, :, 1], epsm[:, :], ALU.add), it)
                    pool.tensor_tensor(rstd[b][:, :], veps[b][:, :], powm[:, :], ALU.pow).then_inc(rstd_s[b], 1)

                def plus(b, bias):
                    for t in range(T):
                        last = pool.tensor_tensor(xb[b][:, t, :], x[b][:, t, :], W(bias), ALU.add)
                    last.then_inc(xb_s[b], 1)

                def split(b, f, parts, s):
                    pool.tensor_tensor(resid[b][:, :, :], f[b][:, :, :], parts[b][:, :, 0, :], ALU.subtract)
                    link(pool.tensor_tensor(parts[b][:, :, 1, :], f[b][:, :, :], parts[b][:, :, 0, :], ALU.subtract), it)
                    pool.tensor_tensor(parts[b][:, :, 2, :], resid[b][:, :, :], parts[b][:, :, 1, :], ALU.subtract).then_inc(s[b], 1)

                for m in range(2):
                    L = 2 * m
                    for b in LANE:
                        norm(b, L)
                    for b in LANE:
                        pool.wait_ge(k_f[b], nth(k_f[b], it, m + 1))
                        split(b, kf, kparts, k_split)
                    for b in LANE:
                        plus(b, MHA[m]["bo"])
                    if m == 0:
                        for b in LANE:
                            norm(b, 1)
                        for b in LANE:
                            pool.wait_ge(xh_s[b], nth(xh_s[b], it, 2))
                            pool.tensor_tensor(xb[b][:, :, :], x[b][:, :, :], xh[b][:, :, :], ALU.add).then_inc(xb_s[b], 1)
                    else:
                        for b in LANE:
                            norm(b, 3)
                for L, bias in ((4, "bao"), (5, "blin"), (6, None), (7, None)):
                    for b in LANE:
                        norm(b, L)
                        if bias:
                            plus(b, bias)
                assert chain[0] == POOL_N, chain[0]

        @block.scalar
        def _(act):
            act.wait_ge(ready, 2 + LANES)
            for n in range(len(CUTS) - 1):
                act.wait_ge(w_in[n], 16)
            act.wait_ge(wi_ready, 1)
            with act.Fori(0, ITERS) as it:
                def evac_xhT(b, L):
                    act.wait_ge(xhT_ps[b], nth(xhT_ps[b], it, L + 1))
                    act.copy(xhT[b][:, :, :].rearrange("p k s -> p (k s)"), dense[b][0][:, :]).then_inc(xhT_s[b], 1)

                for b in LANE:
                    act.wait_ge(ctx_ps[b], nth(ctx_ps[b], it, 1))
                    act.copy(ctxT[b][:, :, :].rearrange("p k s -> p (k s)"), dense[b][1][:, :]).then_inc(ctx_t[b], 1)
                for m in range(2):
                    L = 2 * m
                    for b in LANE:
                        act.wait_ge(k_ps[b], nth(k_ps[b], it, m + 1))
                        if m:
                            act.wait_ge(k_split[b], nth(k_split[b], it, m))
                            act.wait_ge(q_out[b], nth(q_out[b], it, 16 * m))
                        for k in range(KT):
                            act.activation(kparts[b][:, k, 0, :], dense[b][2][:, k * S:(k + 1) * S], ACT.Identity,
                                           bias=W(MHA[m]["bk"])[:, k:k + 1])
                            last = act.activation(kf[b][:, k, :], dense[b][2][:, k * S:(k + 1) * S], ACT.Identity,
                                                  bias=W(MHA[m]["bk"])[:, k:k + 1])
                        last.then_inc(k_f[b], 1)
                    for b in LANE:
                        evac_xhT(b, L)
                    for b in LANE:
                        act.wait_ge(q_ps[b], nth(q_ps[b], it, m + 1))
                        for k in range(KT):
                            last = act.activation(qf[b][:, k, :], dense[b][1][:, k * S:(k + 1) * S], ACT.Identity,
                                                  bias=bqs[m][:, k:k + 1], scale=1.0 / HD ** 0.5)
                        last.then_inc(q_f[b], 1)
                    for s in range(ITEMS + 5):
                        j = m * ITEMS + s
                        for h in range(GH):
                            if 0 <= s - 3 < ITEMS:
                                n = j - 3
                                act.wait_ge(st_ps, nth(st_ps, it, GH * n + h + 1))
                                if n >= 2 and h == 0:
                                    act.wait_ge(pv_ps, nth(pv_ps, it, n - 1))
                                act.activation(PT[n % 2][:, h, :, :].rearrange("p t s -> p (t s)"),
                                               bank[2 + h % 2][:, :], ACT.Exp).then_inc(exp_s, 1)
                            if h == 1 and 0 <= s - 1 < ITEMS:
                                act.wait_ge(mT_ps, nth(mT_ps, it, j))
                                if j - 1 >= 2:
                                    act.wait_ge(m_rows[(j - 3) % 2], nth(m_rows[0], it, 32 * ((j - 3) // 2 + 1)))
                                act.copy(negm[:, (j - 1) % 2, :], bank5b[0:2 * GH, 512:512 + S]).then_inc(negm_s, 1)
                            if h == 1 and 0 <= s - 4 < ITEMS:
                                n = j - 4
                                act.wait_ge(pv_ps, nth(pv_ps, it, n + 1))
                                if n >= 2:
                                    act.wait_ge(otT_ps, nth(otT_ps, it, n - 1))
                                act.copy(OT[n % 2][:, :], bank[4][:, 0:S]).then_inc(ot_s, 1)
                    for b in LANE:
                        act.wait_ge(attT_ps[b], nth(attT_ps[b], it, m + 1))
                        act.copy(attT[b][:, :, :].rearrange("p k s -> p (k s)"), dense[b][0][:, :]).then_inc(attT_s[b], 1)
                    for b in LANE:
                        evac_xhT(b, L + 1)
                for b in LANE:
                    act.wait_ge(gc_ps[b], nth(gc_ps[b], it, 1))
                    act.copy(gcT[b][:, :], dense[b][3][:, 0:KT]).then_inc(gc_s[b], 1)
                for b in LANE:
                    act.wait_ge(gc_ps[b], nth(gc_ps[b], it, 2))
                    act.activation(g1[b][:, :], dense[b][3][:, 4:5], ACT.Gelu, bias=W("gb1")).then_inc(gc_s[b], 1)
                for b in LANE:
                    act.wait_ge(gc_ps[b], nth(gc_ps[b], it, 3))
                    act.activation(g2[b][:, :], dense[b][3][0:64, 8:9].to_broadcast([64, P]), ACT.Gelu,
                                   bias=W("gb2")).then_inc(gc_s[b], 1)
                for b in LANE:
                    act.wait_ge(gc_ps[b], nth(gc_ps[b], it, 4))
                    act.activation(tg[b][:, :], dense[b][3][:, 12:13], ACT.Tanh, bias=hb3[:, :], scale=0.5).then_inc(gc_s[b], 1)
                for c in range(3):
                    if c:
                        for b in LANE:
                            act.wait_ge(oT_ps[b], nth(oT_ps[b], it, c))
                            act.copy(xhT[b][:, :, :].rearrange("p k s -> p (k s)"), dense[b][0][:, :]).then_inc(oT_s[b], 1)
                    for k in range(KT):
                        for b in LANE:
                            act.wait_ge(n1_ps[b], nth(n1_ps[b], it, 2 * c + k + 1))
                            act.activation(h1T[b][:, k, :], dense[b][1 + k][:, 0:S], ACT.Gelu,
                                           bias=W("cb1")[:, k:k + 1]).then_inc(n1_s[b], 1)
                    for b in LANE:
                        act.wait_ge(n2_ps[b], nth(n2_ps[b], it, c + 1))
                        act.activation(h2T[b][:, :], dense[b][0][:, 0:S], ACT.Gelu, bias=W("cb2")).then_inc(n2_s[b], 1)
                    for b in LANE:
                        act.wait_ge(n3_ps[b], nth(n3_ps[b], it, c + 1))
                        act.activation(h3T[b][:, :], dense[b][1][0:64, 0:S], ACT.Gelu, bias=W("cb3")).then_inc(n3_s[b], 1)
                    for b in LANE:
                        act.wait_ge(n4_ps[b], nth(n4_ps[b], it, c + 1))
                        act.activation(th[b][:, :], dense[b][2][:, 0:T], ACT.Tanh, bias=hb4[:, :], scale=0.5).then_inc(n4_s[b], 1)
                for b in LANE:
                    act.wait_ge(third_dve[b], nth(third_dve[b], it, 1))
                    act.activation(kh[b][:, :, :], kz[b][:, :, :], ACT.Exp, scale=-1.0).then_inc(third_act[b], 1)
                for b in LANE:
                    act.wait_ge(third_pe[b], nth(third_pe[b], it, 2))
                    act.copy(AT[b][:, :, :].rearrange("p k h -> p (k h)"), dense[b][2][:, 0:KT * H])
                    act.copy(ks[b][:, :], dense[b][2][0:1, 64:64 + H]).then_inc(third_act[b], 1)
                for b in LANE:
                    act.wait_ge(third_pe[b], nth(third_pe[b], it, 5))
                    act.copy(mm[b][:, :], dense[b][3][0:H, 0:D]).then_inc(third_act[b], 1)
                for b in LANE:
                    evac_xhT(b, 4)
                for b in LANE:
                    act.wait_ge(third_pe[b], nth(third_pe[b], it, 6))
                    act.activation(qh[b][:, :], dense[b][1][0:H, 0:S], ACT.Exp, bias=nbaq[:, :], scale=-1.0).then_inc(third_act[b], 1)
                for b in LANE:
                    evac_xhT(b, 5)
                for b in LANE:
                    act.wait_ge(rank_dve[b], nth(rank_dve[b], it, 1))
                    for t in range(T):
                        last = act.activation(r1[b][:, t, :], sc[b][:, t, 0:E], ACT.Exp, bias=m1[b][:, t:t + 1])
                    last.then_inc(rank_act[b], 1)
                for b in LANE:
                    act.wait_ge(rank_pe[b], nth(rank_pe[b], it, 2))
                    act.copy(twT[b], dense[b][2][0:E * R, 0:S]).then_inc(rank_act[b], 1)
                for b in LANE:
                    act.wait_ge(last_pe[b], nth(last_pe[b], it, 1))
                    for k in range(KT):
                        last = act.activation(kf[b][:, k, :], dense[b][2][:, k * S:(k + 1) * S], ACT.Identity,
                                              bias=W("bk3")[:, k:k + 1])
                    last.then_inc(last_act[b], 1)
                for b in LANE:
                    evac_xhT(b, 6)
                for b in LANE:
                    act.wait_ge(last_pe[b], nth(last_pe[b], it, 3))
                    for k in range(KT):
                        last = act.activation(qf[b][:, k, :], dense[b][1][:, k * S:(k + 1) * S], ACT.Identity,
                                              bias=bqs[2][:, k:k + 1], scale=1.0 / HD ** 0.5)
                    last.then_inc(last_act[b], 1)
                for b in LANE:
                    act.wait_ge(last_dve[b], nth(last_dve[b], it, 3))
                    for t in range(T):
                        last = act.activation(att[b][:, t, :], dense[b][0][:, t * S:(t + 1) * S], ACT.Exp,
                                              bias=m1[b][:, t:t + 1], accum_out=rs[b][:, t:t + 1])
                    last.then_inc(last_act[b], 1)
                for b in LANE:
                    act.wait_ge(last_pe[b], nth(last_pe[b], it, 5))
                    act.copy(attT[b][:, :, :].rearrange("p k s -> p (k s)"), dense[b][1][:, :]).then_inc(last_act[b], 1)
                for b in LANE:
                    evac_xhT(b, 7)
                for k in range(HT):
                    for b in LANE:
                        act.wait_ge(gu_ps[b], nth(gu_ps[b], it, k + 1))
                        if k >= 2:
                            act.wait_ge(hid_s[b], nth(hid_s[b], it, k - 1))
                        act.activation(sg[b][:, k % 2, :], dense[b][1 + k % 2][:, 0:S], ACT.Silu).then_inc(silu_s[b], 1)

        @block.vector
        def _(dve):
            chain = [0]
            per[dve_own.name] = DVE_N = 144

            def link(ins, it=None, part=False):
                chain[0] += 1
                ins.then_inc(dve_own, 1)
                dve.wait_ge(dve_own, chain[0] if it is None else base + it * DVE_N + chain[0])
                if part:
                    dve.memset(junk[:, :], 0.0)

            for n in range(len(CUTS) - 1):
                dve.wait_ge(w_in[n], 16)
            dve.tensor_copy(identb[:, :], ident)
            for b in LANE:
                dve.memset(KA[b][KR:KM, :, :], 1.0)
            for m, name in enumerate(("bq0", "bq1", "bq3")):
                dve.tensor_scalar(bqs[m][:, :], W(name), 1.0 / HD ** 0.5, None, ALU.mult)
            dve.tensor_scalar(hb4[:, :], W("cb4"), 0.5, None, ALU.mult)
            dve.tensor_scalar(hb3[:, :], W("gb3"), 0.5, None, ALU.mult)
            dve.tensor_scalar(nbaq[:, :], W("baq"), -1.0, None, ALU.mult)
            dve.tensor_scalar(r03[:, :], W("range"), 0.3, None, ALU.mult)
            dve.tensor_scalar(r07[:, :], W("range"), 0.7, None, ALU.mult)
            dve.wait_ge(wi_in, 48)
            for t in range(T):
                dve.tensor_copy(maskb[:, t, :], OT[t][:, :])
            link(dve.tensor_scalar(wi[:, :], wi[:, :].bitcast(I32), 1.0 / 127.0, None, ALU.mult))
            dve.memset(mx[:, :, :, :], 0.0).then_inc(wi_ready, 1)
            base = chain[0]

            with dve.Fori(0, ITERS) as it:
                chain[0] = 0

                def norm(b, L):
                    for t in range(T):
                        last = dve.bn_stats(bst[b][:, t, :], x[b][:, t, :])
                    link(last, it, part=True)
                    for t in range(T):
                        last = dve.bn_aggr(mv[b][:, t, :], bst[b][:, t, :])
                    last.then_inc(stats[b], 1)

                def norm2(b, L):
                    dve.wait_ge(rstd_s[b], nth(rstd_s[b], it, L + 1))
                    for t in range(T):
                        last = dve.tensor_scalar(xh[b][:, t, :], x[b][:, t, :], mv[b][:, t, 0:1], rstd[b][:, t:t + 1],
                                                 ALU.subtract, ALU.mult)
                    last.then_inc(xh_s[b], 1)

                def update(b, L, ps, out_s, n, early, k):
                    dve.wait_ge(out_s[b], nth(out_s[b], it, n))
                    if early:
                        dve.wait_ge(xb_s[b], nth(xb_s[b], it, k))
                    src = xb if early else x
                    ins = dve.tensor_tensor(x[b][:, :, :].rearrange("p t d -> p (t d)"), ps,
                                            src[b][:, :, :].rearrange("p t d -> p (t d)"), ALU.add)
                    ins.then_inc(x_new[b], 1)
                    dve.wait_ge(x_new[b], nth(x_new[b], it, max(L, 1)))

                def split(b, f, parts, s):
                    link(dve.tensor_copy(parts[b][:, :, 0, :], f[b][:, :, :]), it)
                    link(dve.tensor_tensor(f[b][:, :, :], f[b][:, :, :], parts[b][:, :, 0, :], ALU.subtract), it)
                    link(dve.tensor_copy(parts[b][:, :, 1, :], f[b][:, :, :]), it)
                    dve.tensor_tensor(parts[b][:, :, 2, :], f[b][:, :, :], parts[b][:, :, 1, :], ALU.subtract).then_inc(s[b], 1)

                for m in range(2):
                    L = 2 * m
                    for b in LANE:
                        if m == 0:
                            dve.wait_ge(x_in_s[b], nth(x_in_s[b], it, 16))
                            link(dve.tensor_copy(x[b][:, :, :], xin[b][:, :, :]), it)
                        norm(b, L)
                    for b in LANE:
                        dve.wait_ge(v_ps[b], nth(v_ps[b], it, m + 1))
                        for t in range(T):
                            last = dve.tensor_tensor(
                                vaug[b][:, t, :, 0:HD],
                                dense[b][3][:, t * D:(t + 1) * D].rearrange("p (h d) -> p h d", h=H),
                                W(MHA[m]["bv"]).rearrange("p (h d) -> p h d", h=H), ALU.add)
                        last.then_inc(v_s[b], 1)
                    for b in LANE:
                        norm2(b, L)
                    for b in LANE:
                        dve.wait_ge(q_f[b], nth(q_f[b], it, m + 1))
                        dve.wait_ge(k_out[b], nth(k_out[b], it, 16 * (m + 1)))
                        split(b, qf, qparts, q_split)
                    for s in range(ITEMS + 5):
                        j = m * ITEMS + s
                        for h in range(GH):
                            if s < ITEMS:
                                dve.wait_ge(s_ps, nth(s_ps, it, GH * j + h + 1))
                                dve.tensor_reduce(mx[:, j % 2, h, :], bank[h % 2][:, :].rearrange("p (t s) -> p t s", t=T),
                                                  AX.X, ALU.max).then_inc(max_s, 1)
                            if h == 0 and 0 <= s - 5 < ITEMS:
                                n, (b, g) = j - 5, item[s - 5]
                                dve.wait_ge(otT_ps, nth(otT_ps, it, n + 1))
                                v = bank[5][:, 0:S].rearrange("p (t h e) -> p t h e", t=T, h=GH)
                                link(dve.reciprocal(rc[:, :, :], v[:, :, :, HD]), it)
                                dve.tensor_tensor(
                                    att[b][:, :, g * GH * HD:(g + 1) * GH * HD].rearrange("p t (h d) -> p t h d", h=GH),
                                    v[:, :, :, 0:HD], rc[:, :, :].unsqueeze(3).to_broadcast([P, T, GH, HD]),
                                    ALU.mult).then_inc(att_s, 1)
                        if s < ITEMS:
                            dve.wait_ge(max_s, nth(max_s, it, GH * (j + 1)))
                            if j >= 2:
                                dve.wait_ge(mT_ps, nth(mT_ps, it, j - 1))
                            v = mx[:, j % 2, :, :].rearrange("p h t -> p t h")
                            link(dve.tensor_scalar(mq[:, j % 2, :, 0, :], v, -1.0, None, ALU.mult), it)
                            dve.scalar_tensor_tensor(mq[:, j % 2, :, 1, :], v, -1.0, mq[:, j % 2, :, 0, :],
                                                     ALU.mult, ALU.subtract).then_inc(mq_s, 1)
                    for b in LANE:
                        update(b, L, dense[b][1][:, :], o_ps, m + 1, True, 1 + 2 * m)
                        norm(b, L + 1)
                    for b in LANE:
                        norm2(b, L + 1)
                    if m == 0:
                        for b in LANE:
                            dve.wait_ge(gate_ps[b], nth(gate_ps[b], it, 1))
                            v = dense[b][1][:, 0:T * E].rearrange("p (t e) -> p t e", t=T)
                            link(dve.tensor_reduce(m1[b][:, :], v, AX.X, ALU.max), it)
                            for t in range(T):
                                last = dve.scalar_tensor_tensor(r1[b][:, t, :], v[:, t, :], m1[b][:, t:t + 1], W("desc"),
                                                                ALU.is_equal, ALU.mult)
                            link(last, it)
                            link(dve.tensor_reduce(m2[b][:, :], r1[b][:, :, :], AX.X, ALU.max), it)
                            for t in range(T):
                                last = dve.tensor_scalar(one[b][:, t, :], r1[b][:, t, :], m2[b][:, t:t + 1], None, ALU.is_equal)
                            last.then_inc(one_s[b], 1)
                        for b in LANE:
                            dve.wait_ge(one_s[b], nth(one_s[b], it, 1))
                            dve.wait_ge(xb_s[b], nth(xb_s[b], it, 2))
                        for t in range(T):
                            for i in range(4):
                                for b in LANE:
                                    dve.wait_ge(ex_ps[b], nth(ex_ps[b], it, 4 * t + i + 1))
                                    ps = dense[b][2 + i % 2]
                                    for e in range(2):
                                        k = 2 * i + e
                                        src, dst = (xb, x) if k % 2 == 0 else (x, xb)
                                        if k == 2 * 4 - 1:
                                            dst = x
                                        ins = dve.scalar_tensor_tensor(
                                            dst[b][:, t, :], ps[:, e * D:(e + 1) * D], one[b][:, t, k:k + 1],
                                            src[b][:, t, :], ALU.mult, ALU.add)
                                        if e == 0:
                                            link(ins, it)
                                    ins.then_inc(ex_used[b], 1)
                                    dve.wait_ge(ex_used[b], nth(ex_used[b], it, 4 * t + i + 1))
                for b in LANE:
                    dve.wait_ge(gc_s[b], nth(gc_s[b], it, 4))
                    link(dve.tensor_scalar(cbase[b][:, :], tg[b][:, :], r07[:, :], 0.1, ALU.mult, ALU.add), it)
                for c in range(3):
                    src, dst = (xh, o2) if c % 2 == 0 else (o2, xh)
                    for b in LANE:
                        dve.wait_ge(n4_s[b], nth(n4_s[b], it, c + 1))
                        link(dve.tensor_scalar(cc[b][:, :], th[b][:, :], r03[:, :], cbase[b][:, :], ALU.mult, ALU.add), it)
                        link(dve.tensor_scalar(cn[b][:, :], cc[b][:, :], -1.0, None, ALU.mult), it)
                        for t in range(T):
                            for to, of, sign in ((0, 2, cc), (1, 3, cn), (2, 0, cn), (3, 1, cc)):
                                last = dve.scalar_tensor_tensor(
                                    dst[b][:, t, to * 64:(to + 1) * 64], src[b][:, t, of * 64:(of + 1) * 64],
                                    sign[b][:, t:t + 1], src[b][:, t, to * 64:(to + 1) * 64], ALU.mult, ALU.add)
                        last.then_inc(o_new[b], 1)
                        if c == 2:
                            dve.wait_ge(o_new[b], nth(o_new[b], it, 3))
                            dve.tensor_tensor(x[b][:, :, :], x[b][:, :, :], dst[b][:, :, :], ALU.add).then_inc(x_new[b], 1)
                            dve.wait_ge(x_new[b], nth(x_new[b], it, 3))
                for b in LANE:
                    norm(b, 4)
                for b in LANE:
                    dve.wait_ge(third_pe[b], nth(third_pe[b], it, 1))
                    dve.tensor_tensor(kz[b][:, :, :].rearrange("p t h -> p (t h)"), dense[b][1][:, 0:T * H], W("bak"),
                                      ALU.add).then_inc(third_dve[b], 1)
                for b in LANE:
                    dve.wait_ge(third_act[b], nth(third_act[b], it, 1))
                    link(dve.tensor_scalar(kz[b][:, :, :], kh[b][:, :, :], 1.0, None, ALU.add), it)
                    dve.reciprocal(kh[b][:, :, :], kz[b][:, :, :]).then_inc(third_dve[b], 1)
                for b in LANE:
                    norm2(b, 4)
                for b in LANE:
                    dve.wait_ge(third_pe[b], nth(third_pe[b], it, 3))
                    link(dve.tensor_tensor(kvm[b], dense[b][3][0:H, 0:D], W("diag"), ALU.mult), it)
                    link(dve.tensor_reduce(dg[b][:, :], kvm[b].rearrange("h (g d) -> h d g", d=HD), AX.X, ALU.add), it)
                    dve.tensor_copy(drep[b][:, :].rearrange("h (g d) -> h g d", d=HD),
                                    dg[b][:, :].unsqueeze(1).to_broadcast([H, P // HD, HD])).then_inc(third_dve[b], 1)
                for b in LANE:
                    dve.wait_ge(third_pe[b], nth(third_pe[b], it, 4))
                    dve.tensor_tensor(sx[b][:, :, :], dense[b][2][:, 0:H].unsqueeze(1).to_broadcast([P, KT, H]),
                                      W("pick", KT), ALU.mult).then_inc(third_dve[b], 1)
                for b in LANE:
                    dve.wait_ge(third_act[b], nth(third_act[b], it, 4))
                    link(dve.tensor_scalar(qh[b][:, :], qh[b][:, :], 1.0, None, ALU.add), it)
                    dve.reciprocal(qh[b][:, :], qh[b][:, :]).then_inc(third_dve[b], 1)
                for b in LANE:
                    update(b, 4, dense[b][0][:, :], third_pe, 7, True, 4)
                    norm(b, 5)
                for b in LANE:
                    norm2(b, 5)
                for b in LANE:
                    dve.wait_ge(rank_pe[b], nth(rank_pe[b], it, 1))
                    v = dense[b][1][:, 0:T * 40].rearrange("p (t e) -> p t e", t=T)
                    link(dve.tensor_copy(sc[b][:, :, :], v), it)
                    link(dve.tensor_reduce(m2[b][:, :], sc[b][:, :, 0:E], AX.X, ALU.max), it)
                    dve.tensor_scalar(m1[b][:, :], m2[b][:, :], -1.0, None, ALU.mult).then_inc(rank_dve[b], 1)
                for b in LANE:
                    dve.wait_ge(rank_act[b], nth(rank_act[b], it, 1))
                    link(dve.tensor_reduce(m1[b][:, :], r1[b][:, :, :], AX.X, ALU.add), it)
                    link(dve.reciprocal(m1[b][:, :], m1[b][:, :]), it)
                    link(dve.tensor_copy(r3[b][:, :, :], r1[b][:, :, :]), it)
                    for k in range(2):
                        link(dve.tensor_reduce(m2[b][:, :], r3[b][:, :, :], AX.X, ALU.max), it)
                        for t in range(T):
                            last = dve.scalar_tensor_tensor(r2[b][:, t, :], r3[b][:, t, :], m2[b][:, t:t + 1], W("desc"),
                                                            ALU.is_equal, ALU.mult)
                        link(last, it)
                        link(dve.tensor_reduce(m2[b][:, :], r2[b][:, :, :], AX.X, ALU.max), it)
                        for t in range(T):
                            last = dve.tensor_scalar(one[b][:, t, :], r2[b][:, t, :], m2[b][:, t:t + 1], None, ALU.is_equal)
                        link(last, it)
                        link(dve.scalar_tensor_tensor(r3[b][:, :, :], one[b][:, :, :], -4.0, r3[b][:, :, :], ALU.mult, ALU.add), it)
                    link(dve.scalar_tensor_tensor(r2[b][:, :, :], r3[b][:, :, :], 0.0, r1[b][:, :, :], ALU.is_lt, ALU.mult), it)
                    for t in range(T):
                        last = dve.tensor_scalar(r2[b][:, t, :], r2[b][:, t, :], m1[b][:, t:t + 1], None, ALU.mult)
                    link(last, it)
                    dve.tensor_tensor(tw[b][:, :, :].rearrange("p t (e r) -> p t e r", r=R),
                                      sc[b][:, :, E:E + E * R].rearrange("p t (e r) -> p t e r", r=R),
                                      r2[b][:, :, :].unsqueeze(3).to_broadcast([P, T, E, R]), ALU.mult).then_inc(rank_dve[b], 1)
                for b in LANE:
                    update(b, 5, dense[b][3][:, :], rank_pe, 3, True, 5)
                    norm(b, 6)
                for b in LANE:
                    dve.wait_ge(last_pe[b], nth(last_pe[b], it, 2))
                    for t in range(T):
                        last = dve.tensor_tensor(v3[b][:, t, :], dense[b][3][:, t * D:(t + 1) * D], W("bv3"), ALU.add)
                    last.then_inc(last_dve[b], 1)
                for b in LANE:
                    norm2(b, 6)
                for b in LANE:
                    dve.wait_ge(m_in_s[b], nth(m_in_s[b], it, 16))
                    dve.tensor_scalar(mrow[b][:, :], mrow[b][:, :], -1.0, 10000.0, ALU.add, ALU.mult).then_inc(last_dve[b], 1)
                for b in LANE:
                    dve.wait_ge(last_pe[b], nth(last_pe[b], it, 4))
                    link(dve.tensor_reduce(m2[b][:, :], dense[b][0][:, :].rearrange("p (t s) -> p t s", t=T), AX.X, ALU.max), it)
                    dve.tensor_scalar(m1[b][:, :], m2[b][:, :], -1.0, None, ALU.mult).then_inc(last_dve[b], 1)
                for b in LANE:
                    dve.wait_ge(last_act[b], nth(last_act[b], it, 3))
                    link(dve.reciprocal(m2[b][:, :], rs[b][:, :]), it)
                    dve.wait_ge(last_pe[b], nth(last_pe[b], it, 6))
                    for t in range(T):
                        last = dve.scalar_tensor_tensor(x[b][:, t, :], dense[b][3][:, t * D:(t + 1) * D], m2[b][:, t:t + 1],
                                                        x[b][:, t, :], ALU.mult, ALU.add)
                    last.then_inc(x_new[b], 1)
                    dve.wait_ge(x_new[b], nth(x_new[b], it, 6))
                    norm(b, 7)
                for b in LANE:
                    norm2(b, 7)
                for k in range(HT):
                    for b in LANE:
                        dve.wait_ge(silu_s[b], nth(silu_s[b], it, k + 1))
                        dve.tensor_tensor(hT[b][:, k, :], sg[b][:, k % 2, :], dense[b][1 + k % 2][:, S:2 * S],
                                          ALU.mult).then_inc(hid_s[b], 1)
                for b in LANE:
                    update(b, 7, dense[b][3][:, :], dn_ps, 1, False, 0)
                assert chain[0] == DVE_N, chain[0]

        @block.tensor
        def _(pe):
            pe.wait_ge(ready, 2 + LANES)
            pe.wait_ge(wi_ready, 1)
            for n in range(len(CUTS) - 1):
                pe.wait_ge(w_in[n], 16)

            def project_T(ps, name, src, rows=KT):
                for k in range(rows):
                    for kk in range(KT):
                        last = pe.matmul(ps[:, k * S:(k + 1) * S], W(name, KT)[:, kk, k * P:(k + 1) * P],
                                         src[:, kk, :], start=(kk == 0), stop=(kk == KT - 1))
                return last

            def project(ps, name, src):
                for t in range(T):
                    for kk in range(KT):
                        last = pe.matmul(ps[:, t * D:(t + 1) * D], src[:, kk, t * P:(t + 1) * P],
                                         W(name, KT)[:, kk, :], start=(kk == 0), stop=(kk == KT - 1))
                return last

            def transpose_all(ps, src):
                for k in range(KT):
                    for t in range(T):
                        last = pe.transpose(ps[:, k * S + t * P:k * S + (t + 1) * P], src[:, t, k * P:(k + 1) * P], ident)
                return last

            with pe.Fori(0, ITERS) as it:
                def norm(b, L):
                    pe.wait_ge(xh_s[b], nth(xh_s[b], it, L + 1))
                    transpose_all(dense[b][0], xh[b]).then_inc(xhT_ps[b], 1)

                for b in LANE:
                    pe.wait_ge(c_in_s[b], nth(c_in_s[b], it, 16))
                    transpose_all(dense[b][1], cin[b]).then_inc(ctx_ps[b], 1)
                for m in range(2):
                    L = 2 * m
                    for b in LANE:
                        if m == 0:
                            pe.wait_ge(ctx_t[b], nth(ctx_t[b], it, 1))
                        else:
                            pe.wait_ge(ex_used[b], nth(ex_used[b], it, 8))
                        project_T(dense[b][2], MHA[m]["k"], ctxT[b]).then_inc(k_ps[b], 1)
                        project(dense[b][3], MHA[m]["v"], ctxT[b]).then_inc(v_ps[b], 1)
                    for b in LANE:
                        norm(b, L)
                    for b in LANE:
                        pe.wait_ge(xhT_s[b], nth(xhT_s[b], it, L + 1))
                        project_T(dense[b][1], MHA[m]["q"], xhT[b]).then_inc(q_ps[b], 1)
                    for s in range(ITEMS + 5):
                        j = m * ITEMS + s
                        for h in range(GH):
                            if s < ITEMS:
                                b, g = item[s]
                                hh = g * GH + h
                                if g == 0 and h == 0:
                                    pe.wait_ge(k_rows[b], nth(k_rows[b], it, 16 * PARTS * (m + 1)))
                                    pe.wait_ge(q_rows[b], nth(q_rows[b], it, 16 * PARTS * (m + 1)))
                                    if s == 0:
                                        pe.wait_ge(v_s[1], nth(v_s[1], it, m + 1))
                                if GH * j + h >= 2:
                                    pe.wait_ge(max_s, nth(max_s, it, GH * j + h - 1))
                                ps = bank[h % 2]
                                for t in range(T):
                                    last = pe.matmul(ps[:, t * S:(t + 1) * S], QA[b][0:KR, hh, t * P:(t + 1) * P],
                                                     KA[b][0:KR, hh, :], start=True, stop=(m == 0))
                                    if m == 1:
                                        last = pe.matmul(ps[:, t * S:(t + 1) * S], identb[:, :], maskb[:, t, :],
                                                         start=False, stop=True)
                                last.then_inc(s_ps, 1)
                            if 0 <= s - 3 < ITEMS:
                                n, (b, g) = j - 3, item[s - 3]
                                hh = g * GH + h
                                if h == 0:
                                    pe.wait_ge(m_rows[n % 2], nth(m_rows[0], it, 32 * (n // 2 + 1)))
                                if GH * n + h >= 2:
                                    pe.wait_ge(exp_s, nth(exp_s, it, GH * n + h - 1))
                                ps = bank[2 + h % 2]
                                for t in range(T):
                                    last = pe.matmul(ps[:, t * S:(t + 1) * S], KA[b][0:KM, hh, t * P:(t + 1) * P],
                                                     QA[b][0:KM, hh, :], start=True, stop=(m == 0))
                                    if m == 1:
                                        last = pe.matmul(ps[:, t * S:(t + 1) * S], identb[:, :], maskb[:, t, :],
                                                         start=False, stop=True)
                                last.then_inc(st_ps, 1)
                            if h == 0 and 0 <= s - 4 < ITEMS:
                                n, (b, g) = j - 4, item[s - 4]
                                pe.wait_ge(exp_s, nth(exp_s, it, GH * (n + 1)))
                                if n >= 1:
                                    pe.wait_ge(ot_s, nth(ot_s, it, n))
                                for t in range(T):
                                    for i in range(GH):
                                        last = pe.matmul(bank[4][32 * i:32 * i + 32, 0:S], vaug[b][:, t, g * GH + i, :],
                                                         PT[n % 2][:, i, t, :], start=(t == 0), stop=(t == T - 1),
                                                         tile_position=(0, 32 * i))
                                last.then_inc(pv_ps, 1)
                            if h == 1 and 0 <= s - 1 < ITEMS:
                                n = j - 1
                                pe.wait_ge(mq_s, nth(mq_s, it, n + 1))
                                if n >= 1:
                                    pe.wait_ge(negm_s, nth(negm_s, it, n))
                                if s >= 5:
                                    pe.wait_ge(att_s, nth(att_s, it, j - 4))
                                for t in range(T):
                                    last = pe.transpose(bank5b[0:2 * GH, 512 + t * P:512 + (t + 1) * P],
                                                        mq[:, n % 2, t, :, :].rearrange("p c h -> p (c h)"), identb[:, :])
                                last.then_inc(mT_ps, 1)
                        if 0 <= s - 4 < ITEMS:
                            n = j - 4
                            pe.wait_ge(ot_s, nth(ot_s, it, n + 1))
                            if n >= 1:
                                pe.wait_ge(att_s, nth(att_s, it, n))
                            pe.wait_ge(negm_s, nth(negm_s, it, min(j, (m + 1) * ITEMS)))
                            for t in range(T):
                                last = pe.transpose(bank[5][:, t * P:(t + 1) * P], OT[n % 2][:, t * P:(t + 1) * P], ident)
                            last.then_inc(otT_ps, 1)
                    for b in LANE:
                        pe.wait_ge(att_s, nth(att_s, it, (m + 1) * ITEMS))
                        transpose_all(dense[b][0], att[b]).then_inc(attT_ps[b], 1)
                    for b in LANE:
                        pe.wait_ge(attT_s[b], nth(attT_s[b], it, m + 1))
                        project(dense[b][1], MHA[m]["o"], attT[b]).then_inc(o_ps[b], 1)
                    for b in LANE:
                        norm(b, L + 1)
                    if m == 0:
                        for b in LANE:
                            pe.wait_ge(xhT_s[b], nth(xhT_s[b], it, 2))
                            for t in range(T):
                                for kk in range(KT):
                                    last = pe.matmul(dense[b][1][:, t * E:(t + 1) * E], xhT[b][:, kk, t * P:(t + 1) * P],
                                                     W("gate0", KT)[:, kk, :], start=(kk == 0), stop=(kk == KT - 1))
                            last.then_inc(gate_ps[b], 1)
                        for t in range(T):
                            for i in range(4):
                                for b in LANE:
                                    n = 4 * t + i
                                    if n >= 2:
                                        pe.wait_ge(ex_used[b], nth(ex_used[b], it, n - 1))
                                    for kk in range(KT):
                                        last = pe.matmul(dense[b][2 + i % 2][:, :], xhT[b][:, kk, t * P:(t + 1) * P],
                                                         W("exp0", KT)[:, kk, i * 512:(i + 1) * 512],
                                                         start=(kk == 0), stop=(kk == KT - 1))
                                    last.then_inc(ex_ps[b], 1)
                for b in LANE:
                    for k in range(KT):
                        for t in range(T):
                            last = pe.matmul(dense[b][3][:, k:k + 1], xh[b][:, t, k * P:(k + 1) * P], W("mean"),
                                             start=(t == 0), stop=(t == T - 1))
                    last.then_inc(gc_ps[b], 1)
                for b in LANE:
                    pe.wait_ge(gc_s[b], nth(gc_s[b], it, 1))
                    for kk in range(KT):
                        last = pe.matmul(dense[b][3][:, 4:5], W("gw1", KT)[:, kk, :], gcT[b][:, kk:kk + 1],
                                         start=(kk == 0), stop=(kk == KT - 1))
                    last.then_inc(gc_ps[b], 1)
                for b in LANE:
                    pe.wait_ge(gc_s[b], nth(gc_s[b], it, 2))
                    pe.matmul(dense[b][3][0:64, 8:9], W("gw2"), g1[b][:, :], start=True, stop=True).then_inc(gc_ps[b], 1)
                for b in LANE:
                    pe.wait_ge(gc_s[b], nth(gc_s[b], it, 3))
                    pe.matmul(dense[b][3][:, 12:13], g2[b][:, :], W("gw3"), start=True, stop=True).then_inc(gc_ps[b], 1)
                for c in range(3):
                    for b in LANE:
                        if c == 0:
                            pe.wait_ge(xhT_s[b], nth(xhT_s[b], it, 4))
                        else:
                            pe.wait_ge(o_new[b], nth(o_new[b], it, c))
                            transpose_all(dense[b][0], (o2 if c == 1 else xh)[b]).then_inc(oT_ps[b], 1)
                    if c:
                        for b in LANE:
                            pe.wait_ge(oT_s[b], nth(oT_s[b], it, c))
                    for k in range(KT):
                        for b in LANE:
                            for kk in range(KT):
                                last = pe.matmul(dense[b][1 + k][:, 0:S], W("cw1", KT)[:, kk, k * P:(k + 1) * P],
                                                 xhT[b][:, kk, :], start=(kk == 0), stop=(kk == KT - 1))
                            last.then_inc(n1_ps[b], 1)
                    for b in LANE:
                        for kk in range(KT):
                            pe.wait_ge(n1_s[b], nth(n1_s[b], it, 2 * c + kk + 1))
                            last = pe.matmul(dense[b][0][:, 0:S], W("cw2", KT)[:, kk, :], h1T[b][:, kk, :],
                                             start=(kk == 0), stop=(kk == KT - 1))
                        last.then_inc(n2_ps[b], 1)
                    for b in LANE:
                        pe.wait_ge(n2_s[b], nth(n2_s[b], it, c + 1))
                        pe.matmul(dense[b][1][0:64, 0:S], W("cw3"), h2T[b][:, :], start=True, stop=True).then_inc(n3_ps[b], 1)
                    for b in LANE:
                        pe.wait_ge(n3_s[b], nth(n3_s[b], it, c + 1))
                        for t in range(T):
                            last = pe.matmul(dense[b][2][:, t:t + 1], h3T[b][:, t * P:(t + 1) * P], W("cw4"),
                                             start=True, stop=True)
                        last.then_inc(n4_ps[b], 1)
                for b in LANE:
                    for t in range(T):
                        for kk in range(KT):
                            last = pe.matmul(dense[b][1][:, t * H:(t + 1) * H], ctxT[b][:, kk, t * P:(t + 1) * P],
                                             W("ak", KT)[:, kk, :], start=(kk == 0), stop=(kk == KT - 1))
                    last.then_inc(third_pe[b], 1)
                for b in LANE:
                    pe.wait_ge(n4_s[b], nth(n4_s[b], it, 3))
                    pe.wait_ge(third_dve[b], nth(third_dve[b], it, 2))
                    for k in range(KT):
                        for t in range(T):
                            pe.matmul(dense[b][2][:, k * H:(k + 1) * H], cin[b][:, t, k * P:(k + 1) * P], kh[b][:, t, :],
                                      start=(t == 0), stop=(t == T - 1))
                    for t in range(T):
                        last = pe.matmul(dense[b][2][0:1, 64:64 + H], W("ones")[:, 0:1], kh[b][:, t, :],
                                         start=(t == 0), stop=(t == T - 1))
                    last.then_inc(third_pe[b], 1)
                for b in LANE:
                    pe.wait_ge(third_act[b], nth(third_act[b], it, 2))
                    for kk in range(KT):
                        pe.matmul(dense[b][3][0:H, 0:D], AT[b][:, kk, :], W("av", KT)[:, kk, :], start=(kk == 0), stop=False)
                    pe.matmul(dense[b][3][0:H, 0:D], ks[b][:, :], W("bav"), start=False, stop=True).then_inc(third_pe[b], 1)
                for b in LANE:
                    pe.wait_ge(third_dve[b], nth(third_dve[b], it, 3))
                    pe.matmul(dense[b][2][:, 0:H], drep[b][:, :], W("tri"), start=True, stop=True).then_inc(third_pe[b], 1)
                for b in LANE:
                    pe.wait_ge(third_dve[b], nth(third_dve[b], it, 4))
                    for kk in range(KT):
                        last = pe.matmul(dense[b][3][0:H, 0:D], sx[b][:, kk, :], W("ao", KT)[:, kk, :],
                                         start=(kk == 0), stop=(kk == KT - 1))
                    last.then_inc(third_pe[b], 1)
                for b in LANE:
                    norm(b, 4)
                for b in LANE:
                    pe.wait_ge(xhT_s[b], nth(xhT_s[b], it, 5))
                    for kk in range(KT):
                        last = pe.matmul(dense[b][1][0:H, 0:S], W("aq", KT)[:, kk, :], xhT[b][:, kk, :],
                                         start=(kk == 0), stop=(kk == KT - 1))
                    last.then_inc(third_pe[b], 1)
                for b in LANE:
                    pe.wait_ge(third_dve[b], nth(third_dve[b], it, 5))
                    pe.wait_ge(third_act[b], nth(third_act[b], it, 3))
                    for t in range(T):
                        last = pe.matmul(dense[b][0][:, t * D:(t + 1) * D], qh[b][:, t * P:(t + 1) * P], mm[b][:, :],
                                         start=True, stop=True)
                    last.then_inc(third_pe[b], 1)
                for b in LANE:
                    norm(b, 5)
                for b in LANE:
                    pe.wait_ge(xhT_s[b], nth(xhT_s[b], it, 6))
                    for t in range(T):
                        for kk in range(KT):
                            last = pe.matmul(dense[b][1][:, t * 40:(t + 1) * 40], xhT[b][:, kk, t * P:(t + 1) * P],
                                             W("gl", KT)[:, kk, :], start=(kk == 0), stop=(kk == KT - 1))
                    last.then_inc(rank_pe[b], 1)
                for b in LANE:
                    pe.wait_ge(rank_dve[b], nth(rank_dve[b], it, 2))
                    for t in range(T):
                        last = pe.transpose(dense[b][2][0:E * R, t * P:(t + 1) * P], tw[b][:, t, :], ident)
                    last.then_inc(rank_pe[b], 1)
                for b in LANE:
                    for t in range(T):
                        ps = dense[b][3][:, t * D:(t + 1) * D]
                        for kk in range(KT):
                            pe.matmul(ps, xhT[b][:, kk, t * P:(t + 1) * P], W("lin", KT)[:, kk, :], start=(kk == 0), stop=False)
                        if t == 0:
                            pe.wait_ge(rank_act[b], nth(rank_act[b], it, 2))
                        last = pe.matmul(ps, twT[b][:, t * P:(t + 1) * P], W("right"), start=False, stop=True)
                    last.then_inc(rank_pe[b], 1)
                for b in LANE:
                    project_T(dense[b][2], "wk3", ctxT[b]).then_inc(last_pe[b], 1)
                for b in LANE:
                    pe.wait_ge(x_new[b], nth(x_new[b], it, 5))
                    project(dense[b][3], "wv3", ctxT[b]).then_inc(last_pe[b], 1)
                for b in LANE:
                    norm(b, 6)
                for b in LANE:
                    pe.wait_ge(xhT_s[b], nth(xhT_s[b], it, 7))
                    project_T(dense[b][1], "wq3", xhT[b]).then_inc(last_pe[b], 1)
                for b in LANE:
                    pe.wait_ge(last_act[b], nth(last_act[b], it, 1))
                    pe.wait_ge(last_act[b], nth(last_act[b], it, 2))
                    pe.wait_ge(last_dve[b], nth(last_dve[b], it, 2))
                    for t in range(T):
                        ps = dense[b][0][:, t * S:(t + 1) * S]
                        for kk in range(KT):
                            pe.matmul(ps, qf[b][:, kk, t * P:(t + 1) * P], kf[b][:, kk, :], start=(kk == 0), stop=False)
                        last = pe.matmul(ps, W("ones")[0:1, :], mrow[b][:, :], start=False, stop=True)
                    last.then_inc(last_pe[b], 1)
                for b in LANE:
                    pe.wait_ge(last_act[b], nth(last_act[b], it, 3))
                    transpose_all(dense[b][1], att[b]).then_inc(last_pe[b], 1)
                for b in LANE:
                    pe.wait_ge(last_act[b], nth(last_act[b], it, 4))
                    pe.wait_ge(last_dve[b], nth(last_dve[b], it, 1))
                    for t in range(T):
                        for kk in range(T):
                            last = pe.matmul(dense[b][3][:, t * D:(t + 1) * D], attT[b][:, kk, t * P:(t + 1) * P],
                                             v3[b][:, kk, :], start=(kk == 0), stop=(kk == T - 1))
                    last.then_inc(last_pe[b], 1)
                for b in LANE:
                    norm(b, 7)
                for b in LANE:
                    pe.wait_ge(xhT_s[b], nth(xhT_s[b], it, 8))
                wg = wi[:, 0:KT * HID].rearrange("p (k n) -> p k n", k=KT)
                wu = wi[:, KT * HID:2 * KT * HID].rearrange("p (k n) -> p k n", k=KT)
                wd = wi[:, 2 * KT * HID:NI].rearrange("p (k n) -> p k n", k=HT)
                for k in range(HT):
                    for b in LANE:
                        if k >= 2:
                            pe.wait_ge(hid_s[b], nth(hid_s[b], it, k - 1))
                        for i, ww in enumerate((wg, wu)):
                            for kk in range(KT):
                                last = pe.matmul(dense[b][1 + k % 2][:, i * S:(i + 1) * S], ww[:, kk, k * P:(k + 1) * P],
                                                 xhT[b][:, kk, :], start=(kk == 0), stop=(kk == KT - 1))
                        last.then_inc(gu_ps[b], 1)
                for b in LANE:
                    pe.wait_ge(hid_s[b], nth(hid_s[b], it, HT))
                    for t in range(T):
                        for kk in range(HT):
                            last = pe.matmul(dense[b][3][:, t * D:(t + 1) * D], hT[b][:, kk, t * P:(t + 1) * P],
                                             wd[:, kk, :], start=(kk == 0), stop=(kk == HT - 1))
                    last.then_inc(dn_ps[b], 1)



def tiles(a):
    k, n = a.shape
    return a.reshape(k // P, P, n).transpose(1, 0, 2).reshape(P, -1)


def column(v):
    return v.reshape(-1, P).T


def everywhere(v):
    return np.broadcast_to(v.reshape(1, -1), (P, v.size))


def packed(a):
    wkv, bkv = a["L1_xattn_Wkv"], a["L1_xattn_bkv"]
    heads = np.arange(D) // HD
    parts = {
        "ident": np.eye(P, dtype=np.float32),
        "wk0": tiles(a["L0_xattn_W_K"]), "bk0": column(a["L0_xattn_b_K"]),
        "wv0": tiles(a["L0_xattn_W_V"]), "bv0": everywhere(a["L0_xattn_b_V"]),
        "wq0": tiles(a["L0_xattn_W_Q"]), "bq0": column(a["L0_xattn_b_Q"]),
        "wo0": tiles(a["L0_xattn_W_O"]), "bo0": everywhere(a["L0_xattn_b_O"]),
        "gate0": tiles(a["L0_ffn_gate_w"].T), "desc": everywhere(np.arange(E, 0, -1).astype(np.float32)),
        "exp0": tiles(a["L0_ffn_expert_w"].transpose(2, 0, 1).reshape(D, E * D)),
        "wk1": tiles(wkv[:, :D]), "bk1": column(bkv[:D]), "wv1": tiles(wkv[:, D:]), "bv1": everywhere(bkv[D:]),
        "wq1": tiles(a["L1_xattn_Wq"]), "bq1": column(a["L1_xattn_bq"]),
        "wo1": tiles(a["L1_xattn_Wo"]), "bo1": everywhere(a["L1_xattn_bo"]),
        "cw1": tiles(a["L1_ffn_cn_w1"]), "cb1": column(a["L1_ffn_cn_b1"]),
        "cw2": tiles(a["L1_ffn_cn_w2"]), "cb2": column(a["L1_ffn_cn_b2"]),
        "cw3": a["L1_ffn_cn_w3"], "cb3": a["L1_ffn_cn_b3"].reshape(64, 1),
        "cw4": a["L1_ffn_cn_w4"], "cb4": everywhere(a["L1_ffn_cn_b4"]),
        "gw1": tiles(a["L1_ffn_gc_w1"]), "gb1": column(a["L1_ffn_gc_b1"]),
        "gw2": a["L1_ffn_gc_w2"], "gb2": a["L1_ffn_gc_b2"].reshape(64, 1),
        "gw3": a["L1_ffn_gc_w3"], "gb3": everywhere(a["L1_ffn_gc_b3"]),
        "range": everywhere(a["L1_ffn_adaptive_range"]), "mean": np.full((P, 1), 1.0 / S, np.float32),
        "aq": tiles(a["L2_xattn_wq"]), "ak": tiles(a["L2_xattn_wk"]), "baq": a["L2_xattn_bq"].reshape(H, 1),
        "bak": np.tile(everywhere(a["L2_xattn_bk"]), (1, T)), "av": tiles(a["L2_xattn_wv"]),
        "bav": a["L2_xattn_bv"].reshape(1, D), "ao": tiles(a["L2_xattn_wo"]), "bao": everywhere(a["L2_xattn_bo"]),
        "diag": (heads[None, :] == np.arange(H)[:, None]).astype(np.float32),
        "tri": np.triu(np.ones((H, H), np.float32)),
        "pick": tiles((heads[:, None] == np.arange(H)[None, :]).astype(np.float32)),
        "ones": np.ones((P, P), np.float32),
        "lin": tiles(a["L2_ffn_W_lin"].T), "blin": everywhere(a["L2_ffn_b_lin"]),
        "gl": tiles(np.concatenate([a["L2_ffn_gate_w"].T, a["L2_ffn_left"].transpose(1, 0, 2).reshape(D, E * R)], 1)),
        "right": a["L2_ffn_right"].reshape(E * R, D),
        "wq3": tiles(a["L3_xattn_Wq"]), "bq3": column(a["L3_xattn_bq"]),
        "wk3": tiles(a["L3_xattn_Wk"]), "bk3": column(a["L3_xattn_bk"]),
        "wv3": tiles(a["L3_xattn_Wv"]), "bv3": everywhere(a["L3_xattn_bv"]),
    }
    out = np.zeros((P, NCOLS), np.float32)
    for name, (at, p, n) in COLS.items():
        assert parts[name].shape == (p, n), (name, parts[name].shape, p, n)
        out[:p, at:at + n] = parts[name]
    return out


def kernel(**inputs):
    import concourse.bacc as bacc
    from concourse.bass_utils import run_bass_kernel_spmd

    a = {k: np.asarray(v) for k, v in inputs.items()}
    arrays = {
        "x_in": np.ascontiguousarray(a["x"]),
        "ctx_in": np.ascontiguousarray(a["ctx_1024"]),
        "mask_in": np.ascontiguousarray(a["mask_BxS2_ff1"]),
        "pack": packed(a),
        "nomask": tiles(np.where(cantor_mask(), np.float32(0), np.float32(OFF)).astype(np.float32)),
        "ipack": np.ascontiguousarray(np.concatenate(
            [tiles(a["L3_ffn_w_gate"].T), tiles(a["L3_ffn_w_up"].T), tiles(a["L3_ffn_w_down"].T)], 1)),
    }
    nc = bacc.Bacc("TRN2", target_bir_lowering=False, num_devices=1)
    aps = [nc.dram_tensor(n, v.shape, mybir.dt.from_np(v.dtype), kind="ExternalInput").ap() for n, v in arrays.items()]
    scratch = nc.dram_tensor("scratch", (LANES, 2, D, 3, S), BF16).ap()
    out = nc.dram_tensor("out", (B, S, D), F32, kind="ExternalOutput").ap()
    program(nc, *aps, scratch, out)
    r = run_bass_kernel_spmd(nc, [arrays], core_ids=[0])
    return r.results[0]["out"]
```

```python
import numpy as np
import concourse.bass as bass
from concourse import mybir
from contextlib import ExitStack

F32 = mybir.dt.float32
BF16 = mybir.dt.bfloat16
I32 = mybir.dt.int32
ALU = mybir.AluOpType
ACT = mybir.ActivationFunctionType
AX = mybir.AxisListType

P = 128
B, S, D = 8, 256, 256
LANES = 2
ITERS = B // LANES
T = S // P
KT = D // P
H, HD = 16, 16
GH = 4
ITEMS = LANES * H // GH
PARTS = 6
QPART = [0, 0, 1, 1, 0, 2]
KPART = [0, 1, 0, 1, 2, 0]
KR = PARTS * HD
KM = KR + 2
E = 8
R = 4
HID = 768
HT = HID // P
LAYERS = 8
EPS = 1e-5
OFF = -1.0e30


def cantor_mask():
    idx = np.arange(S)
    d = np.abs(idx[:, None] - idx[None, :])
    x, ok = d.copy(), np.ones_like(d, dtype=bool)
    for _ in range(7):
        ok &= x % 3 != 1
        x //= 3
    ok &= x == 0
    return ok | (d <= 64)


PACK = [
    ("ident", P, P), ("wk0", P, KT * D), ("ak", P, KT * H), ("bk0", P, KT), ("bq0", P, KT), ("bk1", P, KT),
    ("bq1", P, KT), ("bq3", P, KT), ("bk3", P, KT), ("cb1", P, KT), ("cb2", P, 1), ("cb3", 64, 1), ("cb4", P, 1),
    ("gb1", P, 1), ("gb2", 64, 1), ("gb3", P, 1), ("range", P, 1), ("mean", P, 1), ("baq", H, 1), ("bak", P, T * H),
    "cut",
    ("wq0", P, KT * D), ("wv0", P, KT * D), ("bv0", P, D), ("av", P, KT * D), ("bav", 1, D), ("ao", P, KT * D),
    ("diag", H, D), ("tri", H, H), ("pick", P, KT * H), ("ones", P, P),
    "cut",
    ("wo0", P, KT * D), ("bo0", P, D), ("gate0", P, KT * E), ("desc", P, E), ("exp0", P, KT * E * D),
    "cut",
    ("wk1", P, KT * D), ("wv1", P, KT * D), ("bv1", P, D), ("wq1", P, KT * D), ("wo1", P, KT * D), ("bo1", P, D),
    "cut",
    ("cw1", P, KT * D), ("cw2", P, KT * P), ("cw3", P, 64), ("cw4", 64, 1), ("gw1", P, KT * P), ("gw2", P, 64),
    ("gw3", 64, 1), ("aq", P, KT * H), ("bao", P, D), ("lin", P, KT * D), ("blin", P, D),
    ("gl", P, KT * (E + E * R)), ("right", E * R, D), ("wq3", P, KT * D), ("wk3", P, KT * D), ("wv3", P, KT * D),
    ("bv3", P, D),
]
COLS, CUTS = {}, [0]
_at = 0
for _e in PACK:
    if _e == "cut":
        CUTS.append(_at)
    else:
        COLS[_e[0]] = (_at, _e[1], _e[2])
        _at += _e[2]
NCOLS = _at
CUTS.append(NCOLS)
IPACK = [("wg", KT * HID), ("wu", KT * HID), ("wd", HT * D)]
NI = sum(n for _, n in IPACK)


def program(nc, x_in, ctx_in, mask_in, pack, nomask, ipack, scratch, out):
    ctx = ExitStack()
    with ctx:
        def sb(name, shape, dt=F32):
            return ctx.enter_context(nc.sbuf_tensor(name, shape, dt))

        per = {}

        def sem(name, n=0):
            s = ctx.enter_context(nc.semaphore(name))
            per[s.name] = n
            return s

        def lane_sem(name, n):
            return [sem(f"{name}{b}", n) for b in range(LANES)]

        def nth(s, it, n):
            return it * per[s.name] + n

        w = sb("w", [P, NCOLS])
        wi = sb("wi", [P, NI])

        def W(name, *dims):
            at, p, n = COLS[name]
            v = w[0:p, at:at + n]
            return v.rearrange("p (a b) -> p a b", a=dims[0]) if dims else v

        ident = W("ident")
        identb = sb("identb", [P, P], BF16)
        maskb = sb("maskb", [P, T, S], BF16)
        bqs = [sb(f"bqs{m}", [P, KT]) for m in range(3)]
        hb4 = sb("hb4", [P, 1])
        hb3 = sb("hb3", [P, 1])
        hbaq = sb("hbaq", [H, 1])
        powm = sb("powm", [P, T])
        epsm = sb("epsm", [P, T])
        junk = sb("junk", [1, 1])
        xin = [sb(f"xin{b}", [P, T, D]) for b in range(LANES)]
        cin = [sb(f"cin{b}", [P, T, D]) for b in range(LANES)]
        mrow = [sb(f"mrow{b}", [1, S]) for b in range(LANES)]
        x = [sb(f"x{b}", [P, T, D]) for b in range(LANES)]
        xb = [sb(f"xb{b}", [P, T, D]) for b in range(LANES)]
        xh = [sb(f"xh{b}", [P, T, D]) for b in range(LANES)]
        xhT = [sb(f"xhT{b}", [P, KT, S]) for b in range(LANES)]
        ctxT = [sb(f"ctxT{b}", [P, KT, S]) for b in range(LANES)]
        bst = [sb(f"bst{b}", [P, T, 6]) for b in range(LANES)]
        mv = [sb(f"mv{b}", [P, T, 2]) for b in range(LANES)]
        veps = [sb(f"veps{b}", [P, T]) for b in range(LANES)]
        rstd = [sb(f"rstd{b}", [P, T]) for b in range(LANES)]
        kf = [sb(f"kf{b}", [P, KT, S]) for b in range(LANES)]
        qf = [sb(f"qf{b}", [P, KT, S]) for b in range(LANES)]
        resid = [sb(f"resid{b}", [P, KT, S]) for b in range(LANES)]
        kparts = [sb(f"kparts{b}", [P, KT, 3, S], BF16) for b in range(LANES)]
        qparts = kparts
        KA = [sb(f"KA{b}", [KM, H, S], BF16) for b in range(LANES)]
        QA = [sb(f"QA{b}", [KM, H, S], BF16) for b in range(LANES)]
        vaug = [sb(f"vaug{b}", [P, T, H, 32]) for b in range(LANES)]
        mx = sb("mx", [P, 2, GH, T])
        mq = sb("mq", [P, 2, T, 2, GH], BF16)
        negm = sb("negm", [2 * GH, 2, S], BF16)
        PT = [sb(f"PT{i}", [P, GH, T, S]) for i in range(2)]
        OT = [sb(f"OT{i}", [P, S]) for i in range(2)]
        rc = sb("rc", [P, T, GH])
        att = [sb(f"att{b}", [P, T, D]) for b in range(LANES)]
        attT = [sb(f"attT{b}", [P, KT, S]) for b in range(LANES)]
        sc = [sb(f"sc{b}", [P, T, E + E * R]) for b in range(LANES)]
        r1 = [sb(f"r1{b}", [P, T, E]) for b in range(LANES)]
        r2 = [sb(f"r2{b}", [P, T, E]) for b in range(LANES)]
        r3 = [sb(f"r3{b}", [P, T, E]) for b in range(LANES)]
        one = [sb(f"one{b}", [P, T, E]) for b in range(LANES)]
        m1 = [sb(f"m1{b}", [P, T]) for b in range(LANES)]
        m2 = [sb(f"m2{b}", [P, T]) for b in range(LANES)]
        o2, h1T, h2T = qf, kf, OT
        h3T = [sb(f"h3T{b}", [64, S]) for b in range(LANES)]
        gcT = [sb(f"gcT{b}", [P, KT]) for b in range(LANES)]
        g1 = [sb(f"g1{b}", [P, 1]) for b in range(LANES)]
        g2 = [sb(f"g2{b}", [64, P]) for b in range(LANES)]
        tg = [sb(f"tg{b}", [P, 1]) for b in range(LANES)]
        cbase = [sb(f"cbase{b}", [P, 1]) for b in range(LANES)]
        r03 = sb("r03", [P, 1])
        r07 = sb("r07", [P, 1])
        th = [sb(f"th{b}", [P, T]) for b in range(LANES)]
        cc = [sb(f"cc{b}", [P, T]) for b in range(LANES)]
        cn = [sb(f"cn{b}", [P, T]) for b in range(LANES)]
        kz = [sb(f"kz{b}", [P, T, H]) for b in range(LANES)]
        kh = [sb(f"kh{b}", [P, T, H]) for b in range(LANES)]
        qh = [sb(f"qh{b}", [H, S]) for b in range(LANES)]
        AT = [sb(f"AT{b}", [P, KT, H]) for b in range(LANES)]
        ks = [sb(f"ks{b}", [1, H]) for b in range(LANES)]
        kvm = [h3T[b][0:H, :] for b in range(LANES)]
        dg = [sb(f"dg{b}", [H, HD]) for b in range(LANES)]
        drep = [sb(f"drep{b}", [H, P]) for b in range(LANES)]
        sx = [sb(f"sx{b}", [P, KT, H]) for b in range(LANES)]
        mm = [sb(f"mm{b}", [H, D]) for b in range(LANES)]
        tw = [sb(f"tw{b}", [P, T, E * R]) for b in range(LANES)]
        twT = [h3T[b][0:E * R, :] for b in range(LANES)]
        v3 = resid
        rs = [sb(f"rs{b}", [P, T]) for b in range(LANES)]
        sg = attT
        hT = [PT[b][:, :, :, :].rearrange("p a b c -> p (a b) c") for b in range(LANES)]

        bank = [ctx.enter_context(nc.psum_tensor(f"bank{i}", [P, 512], F32)) for i in range(8)]
        dense = [[bank[4 * b + i] for i in range(4)] for b in range(LANES)]
        s_bank = [bank[i] for i in (0, 1, 7)]
        st_bank = [bank[i] for i in (2, 3, 5)]
        bank6b = bank[6][:, :].bitcast(BF16)

        w_in = [sem(f"w_in{n}") for n in range(len(CUTS) - 1)]
        wi_in = sem("wi_in")
        nomask_in = sem("nomask_in")
        small_ready = sem("small_ready")
        ones_ready = sem("ones_ready")
        wi_ready = sem("wi_ready")
        x_in_s = lane_sem("x_in", 16)
        c_in_s = lane_sem("c_in", 16)
        m_in_s = lane_sem("m_in", 16)
        ctx_ps = lane_sem("ctx_ps", 1)
        ctx_t = lane_sem("ctx_t", 1)
        stats = lane_sem("stats", LAYERS)
        rstd_s = lane_sem("rstd_s", LAYERS)
        xh_s = lane_sem("xh_s", LAYERS)
        xhT_ps = lane_sem("xhT_ps", LAYERS)
        xhT_s = lane_sem("xhT_s", LAYERS)
        xb_s = lane_sem("xb_s", 5)
        x_new = lane_sem("x_new", LAYERS - 1)
        k_ps, v_ps, q_ps = (lane_sem(n, 2) for n in ("k_ps", "v_ps", "q_ps"))
        k_f, q_f, v_s = (lane_sem(n, 2) for n in ("k_f", "q_f", "v_s"))
        k_split, q_split = (lane_sem(n, 2) for n in ("k_split", "q_split"))
        k_out, q_out = (lane_sem(n, 2 * 16) for n in ("k_out", "q_out"))
        k_rows, q_rows = (lane_sem(n, 2 * 16 * PARTS) for n in ("k_rows", "q_rows"))
        attT_ps, attT_s, o_ps = (lane_sem(n, 2) for n in ("attT_ps", "attT_s", "o_ps"))
        NI2 = 2 * ITEMS
        s_ps = sem("s_ps", NI2 * GH)
        max_s = sem("max_s", NI2 * GH)
        mq_s = sem("mq_s", NI2)
        mT_ps = sem("mT_ps", NI2)
        negm_s = sem("negm_s", NI2)
        m_rows = [sem(f"m_rows{i}", NI2 * 16) for i in range(2)]
        st_ps = sem("st_ps", NI2 * GH)
        exp_s = sem("exp_s", NI2 * GH)
        pv_ps = sem("pv_ps", NI2)
        ot_s = sem("ot_s", NI2)
        otT_ps = sem("otT_ps", NI2)
        att_s = sem("att_s", NI2)
        gate_ps = lane_sem("gate_ps", 1)
        one_s = lane_sem("one_s", 1)
        ex_ps = lane_sem("ex_ps", T * 4)
        ex_used = lane_sem("ex_used", T * 4)
        oT_ps, oT_s = (lane_sem(n, 2) for n in ("oT_ps", "oT_s"))
        o_new = lane_sem("o_new", 3)
        n1_ps = lane_sem("n1_ps", 6)
        n1_s = lane_sem("n1_s", 6)
        n2_ps, n2_s, n3_ps, n3_s, n4_ps, n4_s = (lane_sem(n, 3) for n in ("n2_ps", "n2_s", "n3_ps", "n3_s", "n4_ps", "n4_s"))
        gc_ps, gc_s = (lane_sem(n, 4) for n in ("gc_ps", "gc_s"))
        third_pe, third_act, third_dve = lane_sem("third_pe", 7), lane_sem("third_act", 4), lane_sem("third_dve", 5)
        rank_pe, rank_act, rank_dve = lane_sem("rank_pe", 3), lane_sem("rank_act", 2), lane_sem("rank_dve", 2)
        last_pe, last_act, last_dve = lane_sem("last_pe", 6), lane_sem("last_act", 4), lane_sem("last_dve", 3)
        gu_ps, silu_s, hid_s = (lane_sem(n, HT) for n in ("gu_ps", "silu_s", "hid_s"))
        dn_ps = lane_sem("dn_ps", 1)
        stored = lane_sem("stored", 16)
        DVE_LINKS, ACT_LINKS, POOL_LINKS = 0, 0, 0
        dve_own = sem("dve_own")
        pool_own = sem("pool_own")

        block = ctx.enter_context(nc.Block())

        item = [(b, g) for b in range(LANES) for g in range(H // GH)]
        MHA = {0: dict(k="wk0", bk="bk0", v="wv0", bv="bv0", q="wq0", o="wo0", bo="bo0"),
               1: dict(k="wk1", bk="bk1", v="wv1", bv="bv1", q="wq1", o="wo1", bo="bo1")}
        LANE = range(LANES)

        @block.sync
        def _(sp):
            def load(n):
                sp.dma_start(w[:, CUTS[n]:CUTS[n + 1]], pack[:, CUTS[n]:CUTS[n + 1]]).then_inc(w_in[n], 16)

            for b in LANE:
                sp.dma_start(cin[b][:, :, :], ctx_in[b].rearrange("(t p) d -> p t d", p=P)).then_inc(c_in_s[b], 16)
            load(0)
            for b in LANE:
                sp.dma_start(xin[b][:, :, :], x_in[b].rearrange("(t p) d -> p t d", p=P)).then_inc(x_in_s[b], 16)
                sp.dma_start(mrow[b][:, :], mask_in[b:b + 1, :]).then_inc(m_in_s[b], 16)
            for i in range(2):
                sp.dma_start(OT[i][:, :], nomask[:, i * S:(i + 1) * S]).then_inc(nomask_in, 16)
            for n in range(1, len(CUTS) - 1):
                load(n)
            sp.dma_start(wi[:, :].bitcast(I32), ipack).then_inc(wi_in, 16)

            def write(parts, which, out_s, split_s, b, r, m):
                sp.wait_ge(split_s[b], nth(split_s[b], r, m + 1))
                sp.dma_start(scratch[b, which].rearrange("(k p) c s -> p k c s", p=P),
                             parts[b][:, :, :, :]).then_inc(out_s[b], 16)

            def read(dst, which, part_of, out_s, rows_s, b, r, m):
                sp.wait_ge(out_s[b], nth(out_s[b], r, 16 * (m + 1)))
                for c in range(PARTS):
                    sp.dma_start(dst[b][c * HD:(c + 1) * HD, :, :],
                                 scratch[b, which, :, part_of[c], :].rearrange("(h d) s -> d h s", d=HD)
                                 ).then_inc(rows_s[b], 16)

            def keys(r, m):
                for b in LANE:
                    write(kparts, 1, k_out, k_split, b, r, m)
                for b in LANE:
                    read(KA, 1, KPART, k_out, k_rows, b, r, m)

            def queries(b, r, m):
                write(qparts, 0, q_out, q_split, b, r, m)
                read(QA, 0, QPART, q_out, q_rows, b, r, m)

            keys(0, 0)
            with sp.Fori(0, ITERS) as it:
                for m in range(2):
                    if m:
                        keys(it, 1)
                    queries(0, it, m)
                    if m == 0:
                        queries(1, it, m)
                    for n, (b, g) in enumerate(item):
                        if m == 1 and n == 2:
                            queries(1, it, 1)
                        j = m * ITEMS + n
                        sp.wait_ge(negm_s, nth(negm_s, it, j + 1))
                        for c in range(2):
                            sp.dma_start(QA[b][KR + c:KR + c + 1, g * GH:(g + 1) * GH, :],
                                         negm[c * GH:(c + 1) * GH, j % 2, :]).then_inc(m_rows[j % 2], 16)
                    if m == 0:
                        for b in LANE:
                            nx = (it * LANES + LANES + b) % B
                            sp.wait_ge(third_pe[b], nth(third_pe[b], it, 2))
                            sp.dma_start(cin[b][:, :, :], ctx_in[bass.ds(nx, 1), :, :].rearrange("a (t p) d -> p (a t) d", p=P)
                                         ).then_inc(c_in_s[b], 16)
                            sp.wait_ge(xb_s[b], nth(xb_s[b], it, 1))
                            sp.dma_start(xin[b][:, :, :], x_in[bass.ds(nx, 1), :, :].rearrange("a (t p) d -> p (a t) d", p=P)
                                         ).then_inc(x_in_s[b], 16)
                keys(it + 1, 0)
                for b in LANE:
                    sp.wait_ge(x_new[b], nth(x_new[b], it, LAYERS - 1))
                    sp.dma_start(out[bass.ds(it * LANES + b, 1), :, :].rearrange("a (t p) d -> p (a t) d", p=P),
                                 x[b][:, :, :]).then_inc(stored[b], 16)
                for b in LANE:
                    nx = (it * LANES + LANES + b) % B
                    sp.wait_ge(stored[b], nth(stored[b], it, 16))
                    sp.dma_start(mrow[b][:, :], mask_in[bass.ds(nx, 1), :]).then_inc(m_in_s[b], 16)
            for b in LANE:
                sp.wait_ge(stored[b], 16 * ITERS)
                sp.wait_ge(x_in_s[b], 16 * (ITERS + 1))
                sp.wait_ge(c_in_s[b], 16 * (ITERS + 1))
                sp.wait_ge(m_in_s[b], 16 * (ITERS + 1))
                sp.wait_ge(k_out[b], nth(k_out[b], ITERS, 16))
                sp.wait_ge(k_rows[b], nth(k_rows[b], ITERS, 16 * PARTS))

        @block.gpsimd
        def _(pool):
            chain = [0]
            per[pool_own.name] = POOL_N = 2 * LAYERS + 2 * 2

            def link(ins, it=None):
                chain[0] += 1
                ins.then_inc(pool_own, 1)
                pool.wait_ge(pool_own, chain[0] if it is None else base + it * POOL_N + chain[0])

            def norm(b, L, r, it):
                pool.wait_ge(stats[b], nth(stats[b], r, L + 1))
                link(pool.tensor_tensor(veps[b][:, :], mv[b][:, :, 1], epsm[:, :], ALU.add), it)
                pool.tensor_tensor(rstd[b][:, :], veps[b][:, :], powm[:, :], ALU.pow).then_inc(rstd_s[b], 1)

            def split_k(b, m, r, it):
                f, parts = kf, kparts
                pool.wait_ge(k_f[b], nth(k_f[b], r, m + 1))
                pool.tensor_tensor(resid[b][:, :, :], f[b][:, :, :], parts[b][:, :, 0, :], ALU.subtract)
                link(pool.tensor_tensor(parts[b][:, :, 1, :], f[b][:, :, :], parts[b][:, :, 0, :], ALU.subtract), it)
                pool.tensor_tensor(parts[b][:, :, 2, :], resid[b][:, :, :], parts[b][:, :, 1, :],
                                   ALU.subtract).then_inc(k_split[b], 1)

            def prepare(r, it=None):
                for b in LANE:
                    norm(b, 0, r, it)
                for b in LANE:
                    split_k(b, 0, r, it)

            link(pool.memset(powm[:, :], -0.5))
            link(pool.memset(epsm[:, :], EPS))
            prepare(0)
            for b in LANE:
                link(pool.memset(vaug[b][:, :, :, HD:32], 0.0))
                pool.memset(vaug[b][:, :, :, HD:HD + 1], 1.0).then_inc(ones_ready, 1)
            base = chain[0]
            for n in range(len(CUTS) - 1):
                pool.wait_ge(w_in[n], 16)
            pool.wait_ge(wi_in, 16)
            pool.tensor_scalar(wi[:, :], wi[:, :].bitcast(I32), 1.0 / 127.0, None, ALU.mult).then_inc(wi_ready, 1)

            with pool.Fori(0, ITERS) as it:
                chain[0] = 0

                def plus(b, bias, src=x):
                    for t in range(T):
                        last = pool.tensor_tensor(xb[b][:, t, :], src[b][:, t, :], W(bias), ALU.add)
                    last.then_inc(xb_s[b], 1)

                for b in LANE:
                    pool.wait_ge(x_in_s[b], nth(x_in_s[b], it, 16))
                    plus(b, "bo0", xin)
                for b in LANE:
                    norm(b, 1, it, it)
                    pool.wait_ge(xh_s[b], nth(xh_s[b], it, 2))
                    pool.tensor_tensor(xb[b][:, :, :], x[b][:, :, :], xh[b][:, :, :], ALU.add).then_inc(xb_s[b], 1)
                norm(0, 2, it, it)
                for b in LANE:
                    split_k(b, 1, it, it)
                plus(0, "bo1")
                norm(1, 2, it, it)
                plus(1, "bo1")
                for b in LANE:
                    norm(b, 3, it, it)
                for L, bias in ((4, "bao"), (5, "blin"), (6, None), (7, None)):
                    for b in LANE:
                        norm(b, L, it, it)
                        if bias:
                            plus(b, bias)
                prepare(it + 1, it)
                assert chain[0] == POOL_N, chain[0]

        @block.scalar
        def _(act):
            act.wait_ge(w_in[0], 16)

            def keys(b, m, r, ps):
                act.wait_ge(k_ps[b], nth(k_ps[b], r, m + 1))
                for k in range(KT):
                    act.activation(kparts[b][:, k, 0, :], ps[:, k * S:(k + 1) * S], ACT.Identity,
                                   bias=W(MHA[m]["bk"])[:, k:k + 1])
                    last = act.activation(kf[b][:, k, :], ps[:, k * S:(k + 1) * S], ACT.Identity,
                                          bias=W(MHA[m]["bk"])[:, k:k + 1])
                last.then_inc(k_f[b], 1)

            def context(b, r):
                act.wait_ge(ctx_ps[b], nth(ctx_ps[b], r, 1))
                act.copy(ctxT[b][:, :, :].rearrange("p k s -> p (k s)"), dense[b][0][:, :]).then_inc(ctx_t[b], 1)

            for b in LANE:
                context(b, 0)
            for b in LANE:
                keys(b, 0, 0, dense[b][0])
            act.wait_ge(small_ready, 1)
            with act.Fori(0, ITERS) as it:
                def evac_xhT(b, L):
                    act.wait_ge(xhT_ps[b], nth(xhT_ps[b], it, L + 1))
                    act.copy(xhT[b][:, :, :].rearrange("p k s -> p (k s)"), dense[b][0][:, :]).then_inc(xhT_s[b], 1)

                def queries(b, m):
                    act.wait_ge(q_ps[b], nth(q_ps[b], it, m + 1))
                    for k in range(KT):
                        last = act.activation(qf[b][:, k, :], dense[b][1][:, k * S:(k + 1) * S], ACT.Identity,
                                              bias=bqs[m][:, k:k + 1], scale=1.0 / HD ** 0.5)
                    last.then_inc(q_f[b], 1)

                def evac_att(b, m):
                    act.wait_ge(attT_ps[b], nth(attT_ps[b], it, m + 1))
                    act.copy(attT[b][:, :, :].rearrange("p k s -> p (k s)"), dense[b][0][:, :]).then_inc(attT_s[b], 1)

                for b in LANE:
                    act.wait_ge(third_dve[b], nth(third_dve[b], it, 1))
                    act.activation(kh[b][:, :, :], kz[b][:, :, :], ACT.Exp, scale=-1.0).then_inc(third_act[b], 1)
                for b in LANE:
                    evac_xhT(b, 0)
                for b in LANE:
                    queries(b, 0)
                for b in LANE:
                    act.wait_ge(third_pe[b], nth(third_pe[b], it, 2))
                    act.copy(AT[b][:, :, :].rearrange("p k h -> p (k h)"), dense[b][3][:, 0:KT * H])
                    act.copy(ks[b][:, :], dense[b][3][0:1, 64:64 + H]).then_inc(third_act[b], 1)
                for b in LANE:
                    act.wait_ge(third_pe[b], nth(third_pe[b], it, 5))
                    act.copy(mm[b][:, :], dense[b][3][0:H, 0:D]).then_inc(third_act[b], 1)
                for m in range(2):
                    L = 2 * m
                    if m == 1:
                        for b in LANE:
                            act.wait_ge(k_split[b], nth(k_split[b], it, 1))
                            act.wait_ge(q_out[b], nth(q_out[b], it, 16))
                            keys(b, 1, it, (dense[0][2], dense[1][0])[b])
                        evac_xhT(0, 2)
                        queries(0, 1)
                    for s in range(ITEMS + 5):
                        j = m * ITEMS + s
                        for h in range(GH):
                            if 0 <= s - 3 < ITEMS:
                                n = j - 3
                                act.wait_ge(st_ps, nth(st_ps, it, GH * n + h + 1))
                                if n >= 2 and h == 0:
                                    act.wait_ge(pv_ps, nth(pv_ps, it, n - 1))
                                act.activation(PT[n % 2][:, h, :, :].rearrange("p t s -> p (t s)"),
                                               st_bank[(GH * n + h) % 3][:, :], ACT.Exp).then_inc(exp_s, 1)
                            if h == 1 and 0 <= s - 1 < ITEMS:
                                act.wait_ge(mT_ps, nth(mT_ps, it, j))
                                if j - 1 >= 2:
                                    act.wait_ge(m_rows[(j - 3) % 2], nth(m_rows[0], it, 32 * ((j - 3) // 2 + 1)))
                                act.copy(negm[:, (j - 1) % 2, :], bank6b[0:2 * GH, 512:512 + S]).then_inc(negm_s, 1)
                            if h == 1 and 0 <= s - 4 < ITEMS:
                                n = j - 4
                                act.wait_ge(pv_ps, nth(pv_ps, it, n + 1))
                                if n >= 2:
                                    act.wait_ge(otT_ps, nth(otT_ps, it, n - 1))
                                act.copy(OT[n % 2][:, :], bank[4][:, 0:S]).then_inc(ot_s, 1)
                        if m == 1 and s == 0:
                            evac_xhT(1, 2)
                        if m == 1 and s == 1:
                            queries(1, 1)
                        if s == 9:
                            evac_att(0, m)
                    evac_att(1, m)
                    if m == 0:
                        for b in LANE:
                            evac_xhT(b, 1)
                def glob(b, n):
                    act.wait_ge(gc_ps[b], nth(gc_ps[b], it, n))
                    if n == 1:
                        ins = act.copy(gcT[b][:, :], dense[b][3][:, 0:KT])
                    elif n == 2:
                        ins = act.activation(g1[b][:, :], dense[b][3][:, 4:5], ACT.Gelu, bias=W("gb1"))
                    elif n == 3:
                        ins = act.activation(g2[b][:, :], dense[b][3][0:64, 8:9].to_broadcast([64, P]), ACT.Gelu, bias=W("gb2"))
                    else:
                        ins = act.activation(tg[b][:, :], dense[b][3][:, 12:13], ACT.Tanh, bias=hb3[:, :], scale=0.5)
                    ins.then_inc(gc_s[b], 1)

                def turn(b, c):
                    if c == 0:
                        evac_xhT(b, 3)
                    else:
                        act.wait_ge(oT_ps[b], nth(oT_ps[b], it, c))
                        act.copy(xhT[b][:, :, :].rearrange("p k s -> p (k s)"), dense[b][0][:, :]).then_inc(oT_s[b], 1)

                def net(b, c, layer):
                    if c == 0:
                        glob(b, layer)
                    if layer == 1:
                        for k in range(KT):
                            act.wait_ge(n1_ps[b], nth(n1_ps[b], it, 2 * c + k + 1))
                            act.activation(h1T[b][:, k, :], dense[b][1 + k][:, 0:S], ACT.Gelu,
                                           bias=W("cb1")[:, k:k + 1]).then_inc(n1_s[b], 1)
                    elif layer == 2:
                        act.wait_ge(n2_ps[b], nth(n2_ps[b], it, c + 1))
                        act.activation(h2T[b][:, :], dense[b][0][:, 0:S], ACT.Gelu, bias=W("cb2")).then_inc(n2_s[b], 1)
                    elif layer == 3:
                        act.wait_ge(n3_ps[b], nth(n3_ps[b], it, c + 1))
                        act.activation(h3T[b][:, :], dense[b][1][0:64, 0:S], ACT.Gelu, bias=W("cb3")).then_inc(n3_s[b], 1)
                    else:
                        act.wait_ge(n4_ps[b], nth(n4_ps[b], it, c + 1))
                        act.activation(th[b][:, :], dense[b][2][:, 0:T], ACT.Tanh, bias=hb4[:, :], scale=0.5).then_inc(n4_s[b], 1)

                def last_key(b):
                    act.wait_ge(last_pe[b], nth(last_pe[b], it, 1))
                    for k in range(KT):
                        last = act.activation(kf[b][:, k, :], dense[b][3][:, k * S:(k + 1) * S], ACT.Identity,
                                              bias=W("bk3")[:, k:k + 1])
                    last.then_inc(last_act[b], 1)

                for c in range(3):
                    turn(0, c)
                    if c:
                        net(1, c - 1, 3)
                    net(0, c, 1)
                    if c:
                        net(1, c - 1, 4)
                    net(0, c, 2)
                    turn(1, c)
                    net(0, c, 3)
                    net(1, c, 1)
                    net(0, c, 4)
                    net(1, c, 2)
                net(1, 2, 3)
                last_key(0)
                net(1, 2, 4)
                last_key(1)
                for b in LANE:
                    evac_xhT(b, 4)
                    act.wait_ge(third_pe[b], nth(third_pe[b], it, 6))
                    act.activation(qh[b][:, :], dense[b][1][0:H, 0:S], ACT.Tanh, bias=hbaq[:, :], scale=0.5).then_inc(third_act[b], 1)
                for b in LANE:
                    evac_xhT(b, 5)
                    act.wait_ge(rank_dve[b], nth(rank_dve[b], it, 1))
                    for t in range(T):
                        last = act.activation(r1[b][:, t, :], sc[b][:, t, 0:E], ACT.Exp, bias=m1[b][:, t:t + 1])
                    last.then_inc(rank_act[b], 1)
                for b in LANE:
                    act.wait_ge(rank_pe[b], nth(rank_pe[b], it, 2))
                    act.copy(twT[b], dense[b][2][0:E * R, 0:S]).then_inc(rank_act[b], 1)
                for b in LANE:
                    evac_xhT(b, 6)
                for b in LANE:
                    act.wait_ge(last_pe[b], nth(last_pe[b], it, 3))
                    for k in range(KT):
                        last = act.activation(qf[b][:, k, :], dense[b][1][:, k * S:(k + 1) * S], ACT.Identity,
                                              bias=bqs[2][:, k:k + 1], scale=1.0 / HD ** 0.5)
                    last.then_inc(last_act[b], 1)
                for b in LANE:
                    act.wait_ge(last_dve[b], nth(last_dve[b], it, 3))
                    for t in range(T):
                        last = act.activation(att[b][:, t, :], dense[b][0][:, t * S:(t + 1) * S], ACT.Exp,
                                              bias=m1[b][:, t:t + 1], accum_out=rs[b][:, t:t + 1])
                    last.then_inc(last_act[b], 1)
                for b in LANE:
                    act.wait_ge(last_pe[b], nth(last_pe[b], it, 5))
                    act.copy(attT[b][:, :, :].rearrange("p k s -> p (k s)"), dense[b][1][:, :]).then_inc(last_act[b], 1)
                for b in LANE:
                    evac_xhT(b, 7)
                for k in range(HT):
                    for b in LANE:
                        act.wait_ge(gu_ps[b], nth(gu_ps[b], it, k + 1))
                        if k >= 2:
                            act.wait_ge(hid_s[b], nth(hid_s[b], it, k - 1))
                        act.activation(sg[b][:, k % 2, :], dense[b][1 + k % 2][:, 0:S], ACT.Silu).then_inc(silu_s[b], 1)
                    if k == 1:
                        for b in LANE:
                            context(b, it + 1)
                    if k >= 4:
                        act.wait_ge(q_out[k - 4], nth(q_out[k - 4], it, 16 * 2))
                        keys(k - 4, 0, it + 1, dense[k - 4][0])

        @block.vector
        def _(dve):
            chain = [0]
            per[dve_own.name] = DVE_N = 140

            def link(ins, it=None, part=False):
                chain[0] += 1
                ins.then_inc(dve_own, 1)
                dve.wait_ge(dve_own, chain[0] if it is None else base + it * DVE_N + chain[0])
                if part:
                    dve.memset(junk[:, :], 0.0)

            def norm(b, L, it, src=x):
                for t in range(T):
                    last = dve.bn_stats(bst[b][:, t, :], src[b][:, t, :])
                link(last, it, part=True)
                for t in range(T):
                    last = dve.bn_aggr(mv[b][:, t, :], bst[b][:, t, :])
                last.then_inc(stats[b], 1)

            def norm2(b, L, r, src=x):
                dve.wait_ge(rstd_s[b], nth(rstd_s[b], r, L + 1))
                for t in range(T):
                    last = dve.tensor_scalar(xh[b][:, t, :], src[b][:, t, :], mv[b][:, t, 0:1], rstd[b][:, t:t + 1],
                                             ALU.subtract, ALU.mult)
                last.then_inc(xh_s[b], 1)

            def prepare(r, it=None):
                for b in LANE:
                    dve.wait_ge(x_in_s[b], nth(x_in_s[b], r, 16))
                    norm(b, 0, it, xin)
                for b in LANE:
                    norm2(b, 0, r, xin)

            for b in LANE:
                dve.memset(KA[b][KR:KM, :, :], 1.0)
            dve.memset(mx[:, :, :, :], 0.0)
            prepare(0)
            dve.wait_ge(w_in[0], 16)
            dve.tensor_copy(identb[:, :], ident)
            for m, name in enumerate(("bq0", "bq1", "bq3")):
                dve.tensor_scalar(bqs[m][:, :], W(name), 1.0 / HD ** 0.5, None, ALU.mult)
            dve.tensor_scalar(hb4[:, :], W("cb4"), 0.5, None, ALU.mult)
            dve.tensor_scalar(hb3[:, :], W("gb3"), 0.5, None, ALU.mult)
            dve.tensor_scalar(hbaq[:, :], W("baq"), 0.5, None, ALU.mult)
            dve.tensor_scalar(r03[:, :], W("range"), 0.3, None, ALU.mult)
            dve.tensor_scalar(r07[:, :], W("range"), 0.7, None, ALU.mult)
            dve.wait_ge(nomask_in, 32)
            for t in range(T):
                last = dve.tensor_copy(maskb[:, t, :], OT[t][:, :])
            last.then_inc(small_ready, 1)
            dve.wait_ge(small_ready, 1)
            base = chain[0]

            with dve.Fori(0, ITERS) as it:
                chain[0] = 0

                def update(b, L, ps, out_s, n, early, k):
                    dve.wait_ge(out_s[b], nth(out_s[b], it, n))
                    if early:
                        dve.wait_ge(xb_s[b], nth(xb_s[b], it, k))
                    src = xb if early else x
                    ins = dve.tensor_tensor(x[b][:, :, :].rearrange("p t d -> p (t d)"), ps,
                                            src[b][:, :, :].rearrange("p t d -> p (t d)"), ALU.add)
                    ins.then_inc(x_new[b], 1)
                    dve.wait_ge(x_new[b], nth(x_new[b], it, max(L, 1)))

                def values(b, m):
                    dve.wait_ge(v_ps[b], nth(v_ps[b], it, m + 1))
                    for t in range(T):
                        last = dve.tensor_tensor(
                            vaug[b][:, t, :, 0:HD],
                            dense[b][3][:, t * D:(t + 1) * D].rearrange("p (h d) -> p h d", h=H),
                            W(MHA[m]["bv"]).rearrange("p (h d) -> p h d", h=H), ALU.add)
                    last.then_inc(v_s[b], 1)

                def split(b, f, parts, s):
                    link(dve.tensor_copy(parts[b][:, :, 0, :], f[b][:, :, :]), it)
                    link(dve.tensor_tensor(f[b][:, :, :], f[b][:, :, :], parts[b][:, :, 0, :], ALU.subtract), it)
                    link(dve.tensor_copy(parts[b][:, :, 1, :], f[b][:, :, :]), it)
                    dve.tensor_tensor(parts[b][:, :, 2, :], f[b][:, :, :], parts[b][:, :, 1, :], ALU.subtract).then_inc(s[b], 1)

                def split_q(b, m):
                    dve.wait_ge(q_f[b], nth(q_f[b], it, m + 1))
                    dve.wait_ge(k_out[b], nth(k_out[b], it, 16 * (m + 1)))
                    split(b, qf, qparts, q_split)

                def choose(b):
                    dve.wait_ge(gate_ps[b], nth(gate_ps[b], it, 1))
                    v = dense[b][1][:, 0:T * E].rearrange("p (t e) -> p t e", t=T)
                    link(dve.tensor_reduce(m1[b][:, :], v, AX.X, ALU.max), it)
                    for t in range(T):
                        last = dve.scalar_tensor_tensor(r1[b][:, t, :], v[:, t, :], m1[b][:, t:t + 1], W("desc"),
                                                        ALU.is_equal, ALU.mult)
                    link(last, it)
                    link(dve.tensor_reduce(m2[b][:, :], r1[b][:, :, :], AX.X, ALU.max), it)
                    for t in range(T):
                        last = dve.tensor_scalar(one[b][:, t, :], r1[b][:, t, :], m2[b][:, t:t + 1], None, ALU.is_equal)
                    last.then_inc(one_s[b], 1)

                def experts(b, n):
                    t, i = n // 4, n % 4
                    if n == 0:
                        dve.wait_ge(one_s[b], nth(one_s[b], it, 1))
                        dve.wait_ge(xb_s[b], nth(xb_s[b], it, 2))
                    dve.wait_ge(ex_ps[b], nth(ex_ps[b], it, n + 1))
                    ps = dense[b][2 + i % 2]
                    for e in range(2):
                        k = 2 * i + e
                        src, dst = (xb, x) if k % 2 == 0 else (x, xb)
                        if k == E - 1:
                            dst = x
                        ins = dve.scalar_tensor_tensor(
                            dst[b][:, t, :], ps[:, e * D:(e + 1) * D], one[b][:, t, k:k + 1],
                            src[b][:, t, :], ALU.mult, ALU.add)
                        if e == 0:
                            link(ins, it)
                    ins.then_inc(ex_used[b], 1)
                    dve.wait_ge(ex_used[b], nth(ex_used[b], it, n + 1))

                dve.wait_ge(w_in[0], 16)
                dve.wait_ge(w_in[1], 16)
                for b in LANE:
                    dve.wait_ge(third_pe[b], nth(third_pe[b], it, 1))
                    dve.tensor_tensor(kz[b][:, :, :].rearrange("p t h -> p (t h)"), dense[b][2][:, 0:T * H], W("bak"),
                                      ALU.add).then_inc(third_dve[b], 1)
                for b in LANE:
                    dve.wait_ge(third_act[b], nth(third_act[b], it, 1))
                    link(dve.tensor_scalar(kz[b][:, :, :], kh[b][:, :, :], 1.0, None, ALU.add), it)
                    dve.reciprocal(kh[b][:, :, :], kz[b][:, :, :]).then_inc(third_dve[b], 1)
                for b in LANE:
                    split_q(b, 0)
                for b in LANE:
                    dve.wait_ge(third_pe[b], nth(third_pe[b], it, 3))
                    link(dve.tensor_tensor(kvm[b], dense[b][3][0:H, 0:D], W("diag"), ALU.mult), it)
                    link(dve.tensor_reduce(dg[b][:, :], kvm[b].rearrange("h (g d) -> h d g", d=HD), AX.X, ALU.add), it)
                    dve.tensor_copy(drep[b][:, :].rearrange("h (g d) -> h g d", d=HD),
                                    dg[b][:, :].unsqueeze(1).to_broadcast([H, P // HD, HD])).then_inc(third_dve[b], 1)
                for b in LANE:
                    dve.wait_ge(third_pe[b], nth(third_pe[b], it, 4))
                    dve.tensor_tensor(sx[b][:, :, :], dense[b][3][:, 0:H].unsqueeze(1).to_broadcast([P, KT, H]),
                                      W("pick", KT), ALU.mult).then_inc(third_dve[b], 1)
                for b in LANE:
                    values(b, 0)
                for m in range(2):
                    L = 2 * m
                    for s in range(ITEMS + 5):
                        j = m * ITEMS + s
                        for h in range(GH):
                            if s < ITEMS:
                                dve.wait_ge(s_ps, nth(s_ps, it, GH * j + h + 1))
                                dve.tensor_reduce(mx[:, j % 2, h, :], s_bank[(GH * j + h) % 3][:, :].rearrange("p (t s) -> p t s", t=T),
                                                  AX.X, ALU.max).then_inc(max_s, 1)
                            if h == 0 and 0 <= s - 5 < ITEMS:
                                n, (b, g) = j - 5, item[s - 5]
                                dve.wait_ge(otT_ps, nth(otT_ps, it, n + 1))
                                v = bank[6][:, 0:S].rearrange("p (t h e) -> p t h e", t=T, h=GH)
                                link(dve.reciprocal(rc[:, :, :], v[:, :, :, HD]), it)
                                dve.tensor_tensor(
                                    att[b][:, :, g * GH * HD:(g + 1) * GH * HD].rearrange("p t (h d) -> p t h d", h=GH),
                                    v[:, :, :, 0:HD], rc[:, :, :].unsqueeze(3).to_broadcast([P, T, GH, HD]),
                                    ALU.mult).then_inc(att_s, 1)
                        if s < ITEMS:
                            dve.wait_ge(max_s, nth(max_s, it, GH * (j + 1)))
                            if j >= 2:
                                dve.wait_ge(mT_ps, nth(mT_ps, it, j - 1))
                            v = mx[:, j % 2, :, :].rearrange("p h t -> p t h")
                            link(dve.tensor_scalar(mq[:, j % 2, :, 0, :], v, -1.0, None, ALU.mult), it)
                            dve.scalar_tensor_tensor(mq[:, j % 2, :, 1, :], v, -1.0, mq[:, j % 2, :, 0, :],
                                                     ALU.mult, ALU.subtract).then_inc(mq_s, 1)
                        if m == 1 and s == 1:
                            split_q(1, 1)
                        if s == 11:
                            update(0, L, dense[0][1][:, :], o_ps, m + 1, True, 1 + 2 * m)
                            norm(0, L + 1, it)
                        if s == 12:
                            norm2(0, L + 1, it)
                    update(1, L, dense[1][1][:, :], o_ps, m + 1, True, 1 + 2 * m)
                    norm(1, L + 1, it)
                    if m == 0:
                        dve.wait_ge(w_in[2], 16)
                        choose(0)
                        norm2(1, 1, it)
                        for n in range(T * 4):
                            experts(0, n)
                            if n == 3:
                                choose(1)
                        norm(0, 2, it)
                        for n in range(T * 4):
                            experts(1, n)
                            if n == 0:
                                norm2(0, 2, it)
                                dve.wait_ge(w_in[3], 16)
                                values(0, 1)
                            if n == 5:
                                split_q(0, 1)
                        norm(1, 2, it)
                        values(1, 1)
                        norm2(1, 2, it)
                    else:
                        norm2(1, 3, it)
                def couple(b, c):
                    src, dst = (xh, o2) if c % 2 == 0 else (o2, xh)
                    if c == 0:
                        dve.wait_ge(gc_s[b], nth(gc_s[b], it, 4))
                        link(dve.tensor_scalar(cbase[b][:, :], tg[b][:, :], r07[:, :], 0.1, ALU.mult, ALU.add), it)
                    dve.wait_ge(n4_s[b], nth(n4_s[b], it, c + 1))
                    link(dve.tensor_scalar(cc[b][:, :], th[b][:, :], r03[:, :], cbase[b][:, :], ALU.mult, ALU.add), it)
                    link(dve.tensor_scalar(cn[b][:, :], cc[b][:, :], -1.0, None, ALU.mult), it)
                    for t in range(T):
                        for to, of, sign in ((0, 2, cc), (1, 3, cn), (2, 0, cn), (3, 1, cc)):
                            last = dve.scalar_tensor_tensor(
                                dst[b][:, t, to * 64:(to + 1) * 64], src[b][:, t, of * 64:(of + 1) * 64],
                                sign[b][:, t:t + 1], src[b][:, t, to * 64:(to + 1) * 64], ALU.mult, ALU.add)
                    last.then_inc(o_new[b], 1)
                    if c == 2:
                        dve.wait_ge(o_new[b], nth(o_new[b], it, 3))
                        dve.tensor_tensor(x[b][:, :, :], x[b][:, :, :], dst[b][:, :, :], ALU.add).then_inc(x_new[b], 1)
                        dve.wait_ge(x_new[b], nth(x_new[b], it, 3))
                        norm(b, 4, it)

                def third_query(b):
                    dve.wait_ge(third_act[b], nth(third_act[b], it, 4))
                    dve.tensor_scalar(qh[b][:, :], qh[b][:, :], 0.5, 0.5, ALU.mult, ALU.add).then_inc(third_dve[b], 1)

                def last_value(b):
                    dve.wait_ge(last_pe[b], nth(last_pe[b], it, 2))
                    for t in range(T):
                        last = dve.tensor_tensor(v3[b][:, t, :], dense[b][3][:, t * D:(t + 1) * D], W("bv3"), ALU.add)
                    last.then_inc(last_dve[b], 1)

                def logits(b):
                    dve.wait_ge(rank_pe[b], nth(rank_pe[b], it, 1))
                    v = dense[b][1][:, 0:T * 40].rearrange("p (t e) -> p t e", t=T)
                    link(dve.tensor_copy(sc[b][:, :, :], v), it)
                    link(dve.tensor_reduce(m2[b][:, :], sc[b][:, :, 0:E], AX.X, ALU.max), it)
                    dve.tensor_scalar(m1[b][:, :], m2[b][:, :], -1.0, None, ALU.mult).then_inc(rank_dve[b], 1)

                def top2(b):
                    dve.wait_ge(rank_act[b], nth(rank_act[b], it, 1))
                    link(dve.tensor_reduce(m1[b][:, :], r1[b][:, :, :], AX.X, ALU.add), it)
                    link(dve.reciprocal(m1[b][:, :], m1[b][:, :]), it)
                    link(dve.tensor_copy(r3[b][:, :, :], r1[b][:, :, :]), it)
                    for k in range(2):
                        link(dve.tensor_reduce(m2[b][:, :], r3[b][:, :, :], AX.X, ALU.max), it)
                        for t in range(T):
                            last = dve.scalar_tensor_tensor(r2[b][:, t, :], r3[b][:, t, :], m2[b][:, t:t + 1], W("desc"),
                                                            ALU.is_equal, ALU.mult)
                        link(last, it)
                        link(dve.tensor_reduce(m2[b][:, :], r2[b][:, :, :], AX.X, ALU.max), it)
                        for t in range(T):
                            last = dve.tensor_scalar(one[b][:, t, :], r2[b][:, t, :], m2[b][:, t:t + 1], None, ALU.is_equal)
                        link(last, it)
                        link(dve.scalar_tensor_tensor(r3[b][:, :, :], one[b][:, :, :], -4.0, r3[b][:, :, :], ALU.mult, ALU.add), it)
                    link(dve.scalar_tensor_tensor(r2[b][:, :, :], r3[b][:, :, :], 0.0, r1[b][:, :, :], ALU.is_lt, ALU.mult), it)
                    for t in range(T):
                        last = dve.tensor_scalar(r2[b][:, t, :], r2[b][:, t, :], m1[b][:, t:t + 1], None, ALU.mult)
                    link(last, it)
                    dve.tensor_tensor(tw[b][:, :, :].rearrange("p t (e r) -> p t e r", r=R),
                                      sc[b][:, :, E:E + E * R].rearrange("p t (e r) -> p t e r", r=R),
                                      r2[b][:, :, :].unsqueeze(3).to_broadcast([P, T, E, R]), ALU.mult).then_inc(rank_dve[b], 1)

                for c in range(3):
                    couple(0, c)
                    if c == 2:
                        norm2(0, 4, it)
                    couple(1, c)
                third_query(0)
                norm2(1, 4, it)
                update(0, 4, dense[0][0][:, :], third_pe, 7, True, 4)
                norm(0, 5, it)
                third_query(1)
                norm2(0, 5, it)
                dve.wait_ge(w_in[4], 16)
                last_value(0)
                update(1, 4, dense[1][0][:, :], third_pe, 7, True, 4)
                norm(1, 5, it)
                logits(0)
                norm2(1, 5, it)
                last_value(1)
                top2(0)
                logits(1)
                top2(1)
                for b in LANE:
                    dve.wait_ge(rank_pe[b], nth(rank_pe[b], it, 3))
                    dve.wait_ge(xb_s[b], nth(xb_s[b], it, 5))
                    for t in range(T):
                        last = dve.tensor_tensor(x[b][:, t, :], dense[b][3 - 3 * t][:, 0:D], xb[b][:, t, :], ALU.add)
                    last.then_inc(x_new[b], 1)
                    dve.wait_ge(x_new[b], nth(x_new[b], it, 5))
                    norm(b, 6, it)
                for b in LANE:
                    norm2(b, 6, it)
                for b in LANE:
                    dve.wait_ge(m_in_s[b], nth(m_in_s[b], it, 16))
                    dve.tensor_scalar(mrow[b][:, :], mrow[b][:, :], -1.0, 10000.0, ALU.add, ALU.mult).then_inc(last_dve[b], 1)
                for b in LANE:
                    dve.wait_ge(last_pe[b], nth(last_pe[b], it, 4))
                    link(dve.tensor_reduce(m2[b][:, :], dense[b][0][:, :].rearrange("p (t s) -> p t s", t=T), AX.X, ALU.max), it)
                    dve.tensor_scalar(m1[b][:, :], m2[b][:, :], -1.0, None, ALU.mult).then_inc(last_dve[b], 1)
                for b in LANE:
                    dve.wait_ge(last_act[b], nth(last_act[b], it, 3))
                    link(dve.reciprocal(m2[b][:, :], rs[b][:, :]), it)
                    dve.wait_ge(last_pe[b], nth(last_pe[b], it, 6))
                    for t in range(T):
                        last = dve.scalar_tensor_tensor(x[b][:, t, :], dense[b][3][:, t * D:(t + 1) * D], m2[b][:, t:t + 1],
                                                        x[b][:, t, :], ALU.mult, ALU.add)
                    last.then_inc(x_new[b], 1)
                    dve.wait_ge(x_new[b], nth(x_new[b], it, 6))
                    norm(b, 7, it)
                for b in LANE:
                    norm2(b, 7, it)
                for k in range(HT):
                    for b in LANE:
                        dve.wait_ge(silu_s[b], nth(silu_s[b], it, k + 1))
                        dve.tensor_tensor(hT[b][:, k, :], sg[b][:, k % 2, :], dense[b][1 + k % 2][:, S:2 * S],
                                          ALU.mult).then_inc(hid_s[b], 1)
                    if k == 2:
                        prepare(it + 1, it)
                for b in LANE:
                    update(b, 7, dense[b][3][:, :], dn_ps, 1, False, 0)
                assert chain[0] == DVE_N, chain[0]

        @block.tensor
        def _(pe):
            pe.wait_ge(w_in[0], 16)

            def project_T(ps, name, src, rows=KT):
                for k in range(rows):
                    for kk in range(KT):
                        last = pe.matmul(ps[:, k * S:(k + 1) * S], W(name, KT)[:, kk, k * P:(k + 1) * P],
                                         src[:, kk, :], start=(kk == 0), stop=(kk == KT - 1))
                return last

            def project(ps, name, src):
                for t in range(T):
                    for kk in range(KT):
                        last = pe.matmul(ps[:, t * D:(t + 1) * D], src[:, kk, t * P:(t + 1) * P],
                                         W(name, KT)[:, kk, :], start=(kk == 0), stop=(kk == KT - 1))
                return last

            def transpose_all(ps, src):
                for k in range(KT):
                    for t in range(T):
                        last = pe.transpose(ps[:, k * S + t * P:k * S + (t + 1) * P], src[:, t, k * P:(k + 1) * P], ident)
                return last

            def context(b, r):
                pe.wait_ge(c_in_s[b], nth(c_in_s[b], r, 16))
                transpose_all(dense[b][0], cin[b]).then_inc(ctx_ps[b], 1)

            def keys(b, r):
                pe.wait_ge(ctx_t[b], nth(ctx_t[b], r, 1))
                project_T(dense[b][0], "wk0", ctxT[b]).then_inc(k_ps[b], 1)

            for b in LANE:
                context(b, 0)
            for b in LANE:
                keys(b, 0)
            with pe.Fori(0, ITERS) as it:
                def norm(b, L):
                    pe.wait_ge(xh_s[b], nth(xh_s[b], it, L + 1))
                    transpose_all(dense[b][0], xh[b]).then_inc(xhT_ps[b], 1)

                def queries(b, m):
                    pe.wait_ge(xhT_s[b], nth(xhT_s[b], it, 2 * m + 1))
                    project_T(dense[b][1], MHA[m]["q"], xhT[b]).then_inc(q_ps[b], 1)

                def turn_att(b, m):
                    pe.wait_ge(att_s, nth(att_s, it, m * ITEMS + (b + 1) * ITEMS // LANES))
                    transpose_all(dense[b][0], att[b]).then_inc(attT_ps[b], 1)

                def att_out(b, m):
                    pe.wait_ge(attT_s[b], nth(attT_s[b], it, m + 1))
                    project(dense[b][1], MHA[m]["o"], attT[b]).then_inc(o_ps[b], 1)

                def gate(b):
                    pe.wait_ge(xhT_s[b], nth(xhT_s[b], it, 2))
                    for t in range(T):
                        for kk in range(KT):
                            last = pe.matmul(dense[b][1][:, t * E:(t + 1) * E], xhT[b][:, kk, t * P:(t + 1) * P],
                                             W("gate0", KT)[:, kk, :], start=(kk == 0), stop=(kk == KT - 1))
                    last.then_inc(gate_ps[b], 1)

                def experts(b, n):
                    t, i = n // 4, n % 4
                    if n >= 2:
                        pe.wait_ge(ex_used[b], nth(ex_used[b], it, n - 1))
                    for kk in range(KT):
                        last = pe.matmul(dense[b][2 + i % 2][:, :], xhT[b][:, kk, t * P:(t + 1) * P],
                                         W("exp0", KT)[:, kk, i * 512:(i + 1) * 512],
                                         start=(kk == 0), stop=(kk == KT - 1))
                    last.then_inc(ex_ps[b], 1)

                for b in LANE:
                    pe.wait_ge(ctx_t[b], nth(ctx_t[b], it, 1))
                    for t in range(T):
                        for kk in range(KT):
                            last = pe.matmul(dense[b][2][:, t * H:(t + 1) * H], ctxT[b][:, kk, t * P:(t + 1) * P],
                                             W("ak", KT)[:, kk, :], start=(kk == 0), stop=(kk == KT - 1))
                    last.then_inc(third_pe[b], 1)
                for b in LANE:
                    pe.wait_ge(k_f[b], nth(k_f[b], it, 1))
                    norm(b, 0)
                pe.wait_ge(w_in[1], 16)
                pe.wait_ge(small_ready, 1)
                pe.wait_ge(ones_ready, LANES)
                for b in LANE:
                    queries(b, 0)
                for b in LANE:
                    pe.wait_ge(third_dve[b], nth(third_dve[b], it, 2))
                    for k in range(KT):
                        for t in range(T):
                            pe.matmul(dense[b][3][:, k * H:(k + 1) * H], cin[b][:, t, k * P:(k + 1) * P], kh[b][:, t, :],
                                      start=(t == 0), stop=(t == T - 1))
                    for t in range(T):
                        last = pe.matmul(dense[b][3][0:1, 64:64 + H], W("ones")[:, 0:1], kh[b][:, t, :],
                                         start=(t == 0), stop=(t == T - 1))
                    last.then_inc(third_pe[b], 1)
                for b in LANE:
                    pe.wait_ge(third_act[b], nth(third_act[b], it, 2))
                    for kk in range(KT):
                        pe.matmul(dense[b][3][0:H, 0:D], AT[b][:, kk, :], W("av", KT)[:, kk, :], start=(kk == 0), stop=False)
                    pe.matmul(dense[b][3][0:H, 0:D], ks[b][:, :], W("bav"), start=False, stop=True).then_inc(third_pe[b], 1)
                for b in LANE:
                    pe.wait_ge(third_dve[b], nth(third_dve[b], it, 3))
                    pe.matmul(dense[b][3][:, 0:H], drep[b][:, :], W("tri"), start=True, stop=True).then_inc(third_pe[b], 1)
                for b in LANE:
                    pe.wait_ge(third_dve[b], nth(third_dve[b], it, 4))
                    for kk in range(KT):
                        last = pe.matmul(dense[b][3][0:H, 0:D], sx[b][:, kk, :], W("ao", KT)[:, kk, :],
                                         start=(kk == 0), stop=(kk == KT - 1))
                    last.then_inc(third_pe[b], 1)
                for b in LANE:
                    pe.wait_ge(third_act[b], nth(third_act[b], it, 3))
                    project(dense[b][3], "wv0", ctxT[b]).then_inc(v_ps[b], 1)
                for m in range(2):
                    L = 2 * m
                    for s in range(ITEMS + 5):
                        j = m * ITEMS + s
                        for h in range(GH):
                            if s < ITEMS:
                                b, g = item[s]
                                hh = g * GH + h
                                if g == 0 and h == 0:
                                    pe.wait_ge(k_rows[b], nth(k_rows[b], it, 16 * PARTS * (m + 1)))
                                    pe.wait_ge(q_rows[b], nth(q_rows[b], it, 16 * PARTS * (m + 1)))
                                    if s == 0:
                                        for bb in LANE:
                                            pe.wait_ge(v_s[bb], nth(v_s[bb], it, m + 1))
                                if GH * j + h >= 3:
                                    pe.wait_ge(max_s, nth(max_s, it, GH * j + h - 2))
                                ps = s_bank[(GH * j + h) % 3]
                                for t in range(T):
                                    last = pe.matmul(ps[:, t * S:(t + 1) * S], QA[b][0:KR, hh, t * P:(t + 1) * P],
                                                     KA[b][0:KR, hh, :], start=True, stop=(m == 0))
                                    if m == 1:
                                        last = pe.matmul(ps[:, t * S:(t + 1) * S], identb[:, :], maskb[:, t, :],
                                                         start=False, stop=True)
                                last.then_inc(s_ps, 1)
                            if 0 <= s - 3 < ITEMS:
                                n, (b, g) = j - 3, item[s - 3]
                                hh = g * GH + h
                                if h == 0:
                                    pe.wait_ge(m_rows[n % 2], nth(m_rows[0], it, 32 * (n // 2 + 1)))
                                if GH * n + h >= 3:
                                    pe.wait_ge(exp_s, nth(exp_s, it, GH * n + h - 2))
                                ps = st_bank[(GH * n + h) % 3]
                                for t in range(T):
                                    last = pe.matmul(ps[:, t * S:(t + 1) * S], KA[b][0:KM, hh, t * P:(t + 1) * P],
                                                     QA[b][0:KM, hh, :], start=True, stop=(m == 0))
                                    if m == 1:
                                        last = pe.matmul(ps[:, t * S:(t + 1) * S], identb[:, :], maskb[:, t, :],
                                                         start=False, stop=True)
                                last.then_inc(st_ps, 1)
                            if h == 0 and 0 <= s - 4 < ITEMS:
                                n, (b, g) = j - 4, item[s - 4]
                                if g == 0:
                                    pe.wait_ge(v_s[b], nth(v_s[b], it, m + 1))
                                pe.wait_ge(exp_s, nth(exp_s, it, GH * (n + 1)))
                                if n >= 1:
                                    pe.wait_ge(ot_s, nth(ot_s, it, n))
                                for t in range(T):
                                    for i in range(GH):
                                        last = pe.matmul(bank[4][32 * i:32 * i + 32, 0:S], vaug[b][:, t, g * GH + i, :],
                                                         PT[n % 2][:, i, t, :], start=(t == 0), stop=(t == T - 1),
                                                         tile_position=(0, 32 * i))
                                last.then_inc(pv_ps, 1)
                            if h == 1 and 0 <= s - 1 < ITEMS:
                                n = j - 1
                                pe.wait_ge(mq_s, nth(mq_s, it, n + 1))
                                if n >= 1:
                                    pe.wait_ge(negm_s, nth(negm_s, it, n))
                                if s >= 5:
                                    pe.wait_ge(att_s, nth(att_s, it, j - 4))
                                for t in range(T):
                                    last = pe.transpose(bank6b[0:2 * GH, 512 + t * P:512 + (t + 1) * P],
                                                        mq[:, n % 2, t, :, :].rearrange("p c h -> p (c h)"), identb[:, :])
                                last.then_inc(mT_ps, 1)
                        if 0 <= s - 4 < ITEMS:
                            n = j - 4
                            pe.wait_ge(ot_s, nth(ot_s, it, n + 1))
                            if n >= 1:
                                pe.wait_ge(att_s, nth(att_s, it, n))
                            pe.wait_ge(negm_s, nth(negm_s, it, min(j, (m + 1) * ITEMS)))
                            for t in range(T):
                                last = pe.transpose(bank[6][:, t * P:(t + 1) * P], OT[n % 2][:, t * P:(t + 1) * P], ident)
                            last.then_inc(otT_ps, 1)
                        if m == 1 and s == 0:
                            norm(1, 2)
                        if m == 1 and s == 1:
                            queries(1, 1)
                        if s == 9:
                            turn_att(0, m)
                        if s == 10:
                            pe.wait_ge(w_in[2 + m], 16)
                            att_out(0, m)
                    turn_att(1, m)
                    norm(0, L + 1)
                    att_out(1, m)
                    if m == 0:
                        gate(0)
                        for n in range(T * 4):
                            experts(0, n)
                            if n == 1:
                                norm(1, 1)
                            if n == 2:
                                gate(1)
                        pe.wait_ge(ex_used[0], nth(ex_used[0], it, T * 4 - 1))
                        pe.wait_ge(w_in[3], 16)
                        project_T(dense[0][2], "wk1", ctxT[0]).then_inc(k_ps[0], 1)
                        project_T(dense[1][0], "wk1", ctxT[1]).then_inc(k_ps[1], 1)
                        pe.wait_ge(ex_used[0], nth(ex_used[0], it, T * 4))
                        project(dense[0][3], "wv1", ctxT[0]).then_inc(v_ps[0], 1)
                        for n in range(T * 4):
                            experts(1, n)
                            if n == 1:
                                norm(0, 2)
                            if n == 2:
                                queries(0, 1)
                        pe.wait_ge(ex_used[1], nth(ex_used[1], it, T * 4))
                        project(dense[1][3], "wv1", ctxT[1]).then_inc(v_ps[1], 1)
                def glob(b, n):
                    if n > 1:
                        pe.wait_ge(gc_s[b], nth(gc_s[b], it, n - 1))
                    if n == 1:
                        for k in range(KT):
                            for t in range(T):
                                last = pe.matmul(dense[b][3][:, k:k + 1], xh[b][:, t, k * P:(k + 1) * P], W("mean"),
                                                 start=(t == 0), stop=(t == T - 1))
                    elif n == 2:
                        for kk in range(KT):
                            last = pe.matmul(dense[b][3][:, 4:5], W("gw1", KT)[:, kk, :], gcT[b][:, kk:kk + 1],
                                             start=(kk == 0), stop=(kk == KT - 1))
                    elif n == 3:
                        last = pe.matmul(dense[b][3][0:64, 8:9], W("gw2"), g1[b][:, :], start=True, stop=True)
                    else:
                        last = pe.matmul(dense[b][3][:, 12:13], g2[b][:, :], W("gw3"), start=True, stop=True)
                    last.then_inc(gc_ps[b], 1)

                pe.wait_ge(w_in[4], 16)
                def turn(b, c):
                    if c:
                        pe.wait_ge(o_new[b], nth(o_new[b], it, c))
                        transpose_all(dense[b][0], (o2 if c == 1 else xh)[b]).then_inc(oT_ps[b], 1)
                    elif b == 1:
                        norm(1, 3)

                def net(b, c, layer):
                    if c == 0:
                        glob(b, layer)
                    if layer == 1:
                        if c:
                            pe.wait_ge(oT_s[b], nth(oT_s[b], it, c))
                        else:
                            pe.wait_ge(xhT_s[b], nth(xhT_s[b], it, 4))
                        for k in range(KT):
                            for kk in range(KT):
                                last = pe.matmul(dense[b][1 + k][:, 0:S], W("cw1", KT)[:, kk, k * P:(k + 1) * P],
                                                 xhT[b][:, kk, :], start=(kk == 0), stop=(kk == KT - 1))
                            last.then_inc(n1_ps[b], 1)
                    elif layer == 2:
                        for kk in range(KT):
                            pe.wait_ge(n1_s[b], nth(n1_s[b], it, 2 * c + kk + 1))
                            last = pe.matmul(dense[b][0][:, 0:S], W("cw2", KT)[:, kk, :], h1T[b][:, kk, :],
                                             start=(kk == 0), stop=(kk == KT - 1))
                        last.then_inc(n2_ps[b], 1)
                    elif layer == 3:
                        pe.wait_ge(n2_s[b], nth(n2_s[b], it, c + 1))
                        pe.matmul(dense[b][1][0:64, 0:S], W("cw3"), h2T[b][:, :], start=True, stop=True).then_inc(n3_ps[b], 1)
                    else:
                        pe.wait_ge(n3_s[b], nth(n3_s[b], it, c + 1))
                        for t in range(T):
                            last = pe.matmul(dense[b][2][:, t:t + 1], h3T[b][:, t * P:(t + 1) * P], W("cw4"),
                                             start=True, stop=True)
                        last.then_inc(n4_ps[b], 1)

                def last_key(b):
                    pe.wait_ge(gc_s[b], nth(gc_s[b], it, 4))
                    project_T(dense[b][3], "wk3", ctxT[b]).then_inc(last_pe[b], 1)

                def last_value(b):
                    pe.wait_ge(last_act[b], nth(last_act[b], it, 1))
                    project(dense[b][3], "wv3", ctxT[b]).then_inc(last_pe[b], 1)

                def third_query(b):
                    norm(b, 4)
                    pe.wait_ge(xhT_s[b], nth(xhT_s[b], it, 5))
                    for kk in range(KT):
                        last = pe.matmul(dense[b][1][0:H, 0:S], W("aq", KT)[:, kk, :], xhT[b][:, kk, :],
                                         start=(kk == 0), stop=(kk == KT - 1))
                    last.then_inc(third_pe[b], 1)

                def third_out(b):
                    pe.wait_ge(third_dve[b], nth(third_dve[b], it, 5))
                    pe.wait_ge(third_act[b], nth(third_act[b], it, 3))
                    for t in range(T):
                        last = pe.matmul(dense[b][0][:, t * D:(t + 1) * D], qh[b][:, t * P:(t + 1) * P], mm[b][:, :],
                                         start=True, stop=True)
                    last.then_inc(third_pe[b], 1)

                def logits(b):
                    pe.wait_ge(xhT_s[b], nth(xhT_s[b], it, 6))
                    for t in range(T):
                        for kk in range(KT):
                            last = pe.matmul(dense[b][1][:, t * 40:(t + 1) * 40], xhT[b][:, kk, t * P:(t + 1) * P],
                                             W("gl", KT)[:, kk, :], start=(kk == 0), stop=(kk == KT - 1))
                    last.then_inc(rank_pe[b], 1)

                def linear(b):
                    pe.wait_ge(last_dve[b], nth(last_dve[b], it, 1))
                    for t in range(T):
                        for kk in range(KT):
                            pe.matmul(dense[b][3 - 3 * t][:, 0:D], xhT[b][:, kk, t * P:(t + 1) * P], W("lin", KT)[:, kk, :],
                                      start=(kk == 0), stop=False)

                def turn_low_rank(b):
                    pe.wait_ge(rank_dve[b], nth(rank_dve[b], it, 2))
                    for t in range(T):
                        last = pe.transpose(dense[b][2][0:E * R, t * P:(t + 1) * P], tw[b][:, t, :], ident)
                    last.then_inc(rank_pe[b], 1)

                def low_rank(b):
                    pe.wait_ge(rank_act[b], nth(rank_act[b], it, 2))
                    for t in range(T):
                        last = pe.matmul(dense[b][3 - 3 * t][:, 0:D], twT[b][:, t * P:(t + 1) * P], W("right"),
                                         start=False, stop=True)
                    last.then_inc(rank_pe[b], 1)

                for c in range(3):
                    turn(0, c)
                    if c:
                        net(1, c - 1, 3)
                    net(0, c, 1)
                    if c:
                        net(1, c - 1, 4)
                    net(0, c, 2)
                    turn(1, c)
                    net(0, c, 3)
                    net(1, c, 1)
                    net(0, c, 4)
                    net(1, c, 2)
                net(1, 2, 3)
                last_key(0)
                net(1, 2, 4)
                last_key(1)
                third_query(0)
                third_out(0)
                third_query(1)
                last_value(0)
                third_out(1)
                norm(0, 5)
                logits(0)
                last_value(1)
                linear(0)
                norm(1, 5)
                logits(1)
                linear(1)
                turn_low_rank(0)
                low_rank(0)
                turn_low_rank(1)
                low_rank(1)
                for b in LANE:
                    norm(b, 6)
                for b in LANE:
                    pe.wait_ge(xhT_s[b], nth(xhT_s[b], it, 7))
                    project_T(dense[b][1], "wq3", xhT[b]).then_inc(last_pe[b], 1)
                for b in LANE:
                    pe.wait_ge(last_act[b], nth(last_act[b], it, 1))
                    pe.wait_ge(last_act[b], nth(last_act[b], it, 2))
                    pe.wait_ge(last_dve[b], nth(last_dve[b], it, 2))
                    for t in range(T):
                        ps = dense[b][0][:, t * S:(t + 1) * S]
                        for kk in range(KT):
                            pe.matmul(ps, qf[b][:, kk, t * P:(t + 1) * P], kf[b][:, kk, :], start=(kk == 0), stop=False)
                        last = pe.matmul(ps, W("ones")[0:1, :], mrow[b][:, :], start=False, stop=True)
                    last.then_inc(last_pe[b], 1)
                for b in LANE:
                    pe.wait_ge(last_act[b], nth(last_act[b], it, 3))
                    transpose_all(dense[b][1], att[b]).then_inc(last_pe[b], 1)
                for b in LANE:
                    pe.wait_ge(last_act[b], nth(last_act[b], it, 4))
                    pe.wait_ge(last_dve[b], nth(last_dve[b], it, 1))
                    for t in range(T):
                        for kk in range(T):
                            last = pe.matmul(dense[b][3][:, t * D:(t + 1) * D], attT[b][:, kk, t * P:(t + 1) * P],
                                             v3[b][:, kk, :], start=(kk == 0), stop=(kk == T - 1))
                    last.then_inc(last_pe[b], 1)
                for b in LANE:
                    norm(b, 7)
                for b in LANE:
                    pe.wait_ge(xhT_s[b], nth(xhT_s[b], it, 8))
                wg = wi[:, 0:KT * HID].rearrange("p (k n) -> p k n", k=KT)
                wu = wi[:, KT * HID:2 * KT * HID].rearrange("p (k n) -> p k n", k=KT)
                wd = wi[:, 2 * KT * HID:NI].rearrange("p (k n) -> p k n", k=HT)
                pe.wait_ge(wi_ready, 1)
                for k in range(HT):
                    for b in LANE:
                        if k >= 2:
                            pe.wait_ge(hid_s[b], nth(hid_s[b], it, k - 1))
                        for i, ww in enumerate((wg, wu)):
                            for kk in range(KT):
                                last = pe.matmul(dense[b][1 + k % 2][:, i * S:(i + 1) * S], ww[:, kk, k * P:(k + 1) * P],
                                                 xhT[b][:, kk, :], start=(kk == 0), stop=(kk == KT - 1))
                        last.then_inc(gu_ps[b], 1)
                    if k == 1:
                        for b in LANE:
                            context(b, it + 1)
                    if k == 3:
                        for b in LANE:
                            keys(b, it + 1)
                for b in LANE:
                    pe.wait_ge(hid_s[b], nth(hid_s[b], it, HT))
                    for t in range(T):
                        for kk in range(HT):
                            last = pe.matmul(dense[b][3][:, t * D:(t + 1) * D], hT[b][:, kk, t * P:(t + 1) * P],
                                             wd[:, kk, :], start=(kk == 0), stop=(kk == HT - 1))
                    last.then_inc(dn_ps[b], 1)



def tiles(a):
    k, n = a.shape
    return a.reshape(k // P, P, n).transpose(1, 0, 2).reshape(P, -1)


def column(v):
    return v.reshape(-1, P).T


def everywhere(v):
    return np.broadcast_to(v.reshape(1, -1), (P, v.size))


def packed(a):
    wkv, bkv = a["L1_xattn_Wkv"], a["L1_xattn_bkv"]
    heads = np.arange(D) // HD
    parts = {
        "ident": np.eye(P, dtype=np.float32),
        "wk0": tiles(a["L0_xattn_W_K"]), "bk0": column(a["L0_xattn_b_K"]),
        "wv0": tiles(a["L0_xattn_W_V"]), "bv0": everywhere(a["L0_xattn_b_V"]),
        "wq0": tiles(a["L0_xattn_W_Q"]), "bq0": column(a["L0_xattn_b_Q"]),
        "wo0": tiles(a["L0_xattn_W_O"]), "bo0": everywhere(a["L0_xattn_b_O"]),
        "gate0": tiles(a["L0_ffn_gate_w"].T), "desc": everywhere(np.arange(E, 0, -1).astype(np.float32)),
        "exp0": tiles(a["L0_ffn_expert_w"].transpose(2, 0, 1).reshape(D, E * D)),
        "wk1": tiles(wkv[:, :D]), "bk1": column(bkv[:D]), "wv1": tiles(wkv[:, D:]), "bv1": everywhere(bkv[D:]),
        "wq1": tiles(a["L1_xattn_Wq"]), "bq1": column(a["L1_xattn_bq"]),
        "wo1": tiles(a["L1_xattn_Wo"]), "bo1": everywhere(a["L1_xattn_bo"]),
        "cw1": tiles(a["L1_ffn_cn_w1"]), "cb1": column(a["L1_ffn_cn_b1"]),
        "cw2": tiles(a["L1_ffn_cn_w2"]), "cb2": column(a["L1_ffn_cn_b2"]),
        "cw3": a["L1_ffn_cn_w3"], "cb3": a["L1_ffn_cn_b3"].reshape(64, 1),
        "cw4": a["L1_ffn_cn_w4"], "cb4": everywhere(a["L1_ffn_cn_b4"]),
        "gw1": tiles(a["L1_ffn_gc_w1"]), "gb1": column(a["L1_ffn_gc_b1"]),
        "gw2": a["L1_ffn_gc_w2"], "gb2": a["L1_ffn_gc_b2"].reshape(64, 1),
        "gw3": a["L1_ffn_gc_w3"], "gb3": everywhere(a["L1_ffn_gc_b3"]),
        "range": everywhere(a["L1_ffn_adaptive_range"]), "mean": np.full((P, 1), 1.0 / S, np.float32),
        "aq": tiles(a["L2_xattn_wq"]), "ak": tiles(a["L2_xattn_wk"]), "baq": a["L2_xattn_bq"].reshape(H, 1),
        "bak": np.tile(everywhere(a["L2_xattn_bk"]), (1, T)), "av": tiles(a["L2_xattn_wv"]),
        "bav": a["L2_xattn_bv"].reshape(1, D), "ao": tiles(a["L2_xattn_wo"]), "bao": everywhere(a["L2_xattn_bo"]),
        "diag": (heads[None, :] == np.arange(H)[:, None]).astype(np.float32),
        "tri": np.triu(np.ones((H, H), np.float32)),
        "pick": tiles((heads[:, None] == np.arange(H)[None, :]).astype(np.float32)),
        "ones": np.ones((P, P), np.float32),
        "lin": tiles(a["L2_ffn_W_lin"].T), "blin": everywhere(a["L2_ffn_b_lin"]),
        "gl": tiles(np.concatenate([a["L2_ffn_gate_w"].T, a["L2_ffn_left"].transpose(1, 0, 2).reshape(D, E * R)], 1)),
        "right": a["L2_ffn_right"].reshape(E * R, D),
        "wq3": tiles(a["L3_xattn_Wq"]), "bq3": column(a["L3_xattn_bq"]),
        "wk3": tiles(a["L3_xattn_Wk"]), "bk3": column(a["L3_xattn_bk"]),
        "wv3": tiles(a["L3_xattn_Wv"]), "bv3": everywhere(a["L3_xattn_bv"]),
    }
    out = np.zeros((P, NCOLS), np.float32)
    for name, (at, p, n) in COLS.items():
        assert parts[name].shape == (p, n), (name, parts[name].shape, p, n)
        out[:p, at:at + n] = parts[name]
    return out


def kernel(**inputs):
    import concourse.bacc as bacc
    from concourse.bass_utils import run_bass_kernel_spmd

    a = {k: np.asarray(v) for k, v in inputs.items()}
    arrays = {
        "x_in": np.ascontiguousarray(a["x"]),
        "ctx_in": np.ascontiguousarray(a["ctx_1024"]),
        "mask_in": np.ascontiguousarray(a["mask_BxS2_ff1"]),
        "pack": packed(a),
        "nomask": tiles(np.where(cantor_mask(), np.float32(0), np.float32(OFF)).astype(np.float32)),
        "ipack": np.ascontiguousarray(np.concatenate(
            [tiles(a["L3_ffn_w_gate"].T), tiles(a["L3_ffn_w_up"].T), tiles(a["L3_ffn_w_down"].T)], 1)),
    }
    nc = bacc.Bacc("TRN2", target_bir_lowering=False, num_devices=1)
    aps = [nc.dram_tensor(n, v.shape, mybir.dt.from_np(v.dtype), kind="ExternalInput").ap() for n, v in arrays.items()]
    scratch = nc.dram_tensor("scratch", (LANES, 2, D, 3, S), BF16).ap()
    out = nc.dram_tensor("out", (B, S, D), F32, kind="ExternalOutput").ap()
    program(nc, *aps, scratch, out)
    r = run_bass_kernel_spmd(nc, [arrays], core_ids=[0])
    return r.results[0]["out"]
```

```python
import numpy as np
import concourse.bass as bass
from concourse import mybir
from contextlib import ExitStack

F32 = mybir.dt.float32
BF16 = mybir.dt.bfloat16
I32 = mybir.dt.int32
ALU = mybir.AluOpType
ACT = mybir.ActivationFunctionType
AX = mybir.AxisListType

P = 128
B, S, D = 8, 256, 256
LANES = 2
ITERS = B // LANES
T = S // P
KT = D // P
H, HD = 16, 16
GH = 4
ITEMS = LANES * H // GH
PARTS = 6
GROUPS = [(0, 3), (1, 2), (2, 1)]
KR = PARTS * HD
KM = KR + 2
E = 8
R = 4
HID = 768
HT = HID // P
LAYERS = 8
EPS = 1e-5
OFF = -1.0e30


def cantor_mask():
    idx = np.arange(S)
    d = np.abs(idx[:, None] - idx[None, :])
    x, ok = d.copy(), np.ones_like(d, dtype=bool)
    for _ in range(7):
        ok &= x % 3 != 1
        x //= 3
    ok &= x == 0
    return ok | (d <= 64)


PACK = [
    ("ident", P, P), ("wk0", P, KT * D), ("ak", P, KT * H), ("bk0", P, KT), ("bq0", P, KT), ("bk1", P, KT),
    ("bq1", P, KT), ("bq3", P, KT), ("bk3", P, KT), ("cb1", P, KT), ("cb2", P, 1), ("cb3", 64, 1), ("cb4", P, 1),
    ("gb1", P, 1), ("gb2", 64, 1), ("gb3", P, 1), ("range", P, 1), ("mean", P, 1), ("baq", H, 1), ("bak", P, T * H),
    "cut",
    ("wq0", P, KT * D), ("wv0", P, KT * D), ("bv0", P, D), ("av", P, KT * D), ("bav", 1, D), ("ao", P, KT * D),
    ("diag", H, D), ("tri", H, H), ("pick", P, KT * H), ("ones", P, P),
    "cut",
    ("wo0", P, KT * D), ("bo0", P, D), ("gate0", P, KT * E), ("desc", P, E), ("exp0", P, KT * E * D),
    "cut",
    ("wk1", P, KT * D), ("wv1", P, KT * D), ("bv1", P, D), ("wq1", P, KT * D), ("wo1", P, KT * D), ("bo1", P, D),
    "cut",
    ("cw1", P, KT * D), ("cw2", P, KT * P), ("cw3", P, 64), ("cw4", 64, 1), ("gw1", P, KT * P), ("gw2", P, 64),
    ("gw3", 64, 1), ("aq", P, KT * H), ("bao", P, D), ("lin", P, KT * D), ("blin", P, D),
    ("gl", P, KT * (E + E * R)), ("right", E * R, D), ("wq3", P, KT * D), ("wk3", P, KT * D), ("wv3", P, KT * D),
    ("bv3", P, D),
]
COLS, CUTS = {}, [0]
_at = 0
for _e in PACK:
    if _e == "cut":
        CUTS.append(_at)
    else:
        COLS[_e[0]] = (_at, _e[1], _e[2])
        _at += _e[2]
NCOLS = _at
CUTS.append(NCOLS)
IPACK = [("wg", KT * HID), ("wu", KT * HID), ("wd", HT * D)]
NI = sum(n for _, n in IPACK)


def program(nc, x_in, ctx_in, mask_in, pack, nomask, ipack, scratch, out):
    ctx = ExitStack()
    with ctx:
        def sb(name, shape, dt=F32):
            return ctx.enter_context(nc.sbuf_tensor(name, shape, dt))

        per = {}

        def sem(name, n=0):
            s = ctx.enter_context(nc.semaphore(name))
            per[s.name] = n
            return s

        def lane_sem(name, n):
            return [sem(f"{name}{b}", n) for b in range(LANES)]

        def nth(s, it, n):
            return it * per[s.name] + n

        w = sb("w", [P, NCOLS])
        wi = sb("wi", [P, NI])

        def W(name, *dims):
            at, p, n = COLS[name]
            v = w[0:p, at:at + n]
            return v.rearrange("p (a b) -> p a b", a=dims[0]) if dims else v

        ident = W("ident")
        identb = sb("identb", [P, P], BF16)
        maskb = sb("maskb", [P, T, S], BF16)
        bqs = [sb(f"bqs{m}", [P, KT]) for m in range(3)]
        hb4 = sb("hb4", [P, 1])
        hb3 = sb("hb3", [P, 1])
        hbaq = sb("hbaq", [H, 1])
        powm = sb("powm", [P, T])
        epsm = sb("epsm", [P, T])
        junk = sb("junk", [1, 1])
        xin = [sb(f"xin{b}", [P, T, D]) for b in range(LANES)]
        cin = [sb(f"cin{b}", [P, T, D]) for b in range(LANES)]
        mrow = [sb(f"mrow{b}", [1, S]) for b in range(LANES)]
        x = [sb(f"x{b}", [P, T, D]) for b in range(LANES)]
        xb = [sb(f"xb{b}", [P, T, D]) for b in range(LANES)]
        xh = [sb(f"xh{b}", [P, T, D]) for b in range(LANES)]
        xhT = [sb(f"xhT{b}", [P, KT, S]) for b in range(LANES)]
        ctxT = [sb(f"ctxT{b}", [P, KT, S]) for b in range(LANES)]
        bst = [sb(f"bst{b}", [P, T, 6]) for b in range(LANES)]
        mv = [sb(f"mv{b}", [P, T, 2]) for b in range(LANES)]
        veps = [sb(f"veps{b}", [P, T]) for b in range(LANES)]
        rstd = [sb(f"rstd{b}", [P, T]) for b in range(LANES)]
        kf = [sb(f"kf{b}", [P, KT, S]) for b in range(LANES)]
        qf = [sb(f"qf{b}", [P, KT, S]) for b in range(LANES)]
        resid = [sb(f"resid{b}", [P, KT, S]) for b in range(LANES)]
        kparts = [sb(f"kparts{b}", [P, KT, 3, S], BF16) for b in range(LANES)]
        qparts = kparts
        KA = [sb(f"KA{b}", [KM, H, S], BF16) for b in range(LANES)]
        QA = [sb(f"QA{b}", [KM, H, S], BF16) for b in range(LANES)]
        k_of = (xb, kf)
        vaug = [sb(f"vaug{b}", [P, T, H, 32]) for b in range(LANES)]
        mx = sb("mx", [P, 2, GH, T])
        mq = sb("mq", [P, 2, T, 2, GH], BF16)
        negm = sb("negm", [2 * GH, 2, S], BF16)
        PT = [sb(f"PT{i}", [P, GH, T, S]) for i in range(2)]
        OT = [sb(f"OT{i}", [P, S]) for i in range(2)]
        rc = sb("rc", [P, T, GH])
        att = [sb(f"att{b}", [P, T, D]) for b in range(LANES)]
        attT = [sb(f"attT{b}", [P, KT, S]) for b in range(LANES)]
        sc = [sb(f"sc{b}", [P, T, E + E * R]) for b in range(LANES)]
        r1 = [sb(f"r1{b}", [P, T, E]) for b in range(LANES)]
        r2 = [sb(f"r2{b}", [P, T, E]) for b in range(LANES)]
        r3 = [sb(f"r3{b}", [P, T, E]) for b in range(LANES)]
        one = [sb(f"one{b}", [P, T, E]) for b in range(LANES)]
        m1 = [sb(f"m1{b}", [P, T]) for b in range(LANES)]
        m2 = [sb(f"m2{b}", [P, T]) for b in range(LANES)]
        o2, h1T, h2T = qf, kf, OT
        h3T = [sb(f"h3T{b}", [64, S]) for b in range(LANES)]
        gcT = [sb(f"gcT{b}", [P, KT]) for b in range(LANES)]
        g1 = [sb(f"g1{b}", [P, 1]) for b in range(LANES)]
        g2 = [sb(f"g2{b}", [64, P]) for b in range(LANES)]
        tg = [sb(f"tg{b}", [P, 1]) for b in range(LANES)]
        cbase = [sb(f"cbase{b}", [P, 1]) for b in range(LANES)]
        r03 = sb("r03", [P, 1])
        r07 = sb("r07", [P, 1])
        th = [sb(f"th{b}", [P, T]) for b in range(LANES)]
        cc = [sb(f"cc{b}", [P, T]) for b in range(LANES)]
        cn = [sb(f"cn{b}", [P, T]) for b in range(LANES)]
        kz = [sb(f"kz{b}", [P, T, H]) for b in range(LANES)]
        kh = [sb(f"kh{b}", [P, T, H]) for b in range(LANES)]
        qh = [sb(f"qh{b}", [H, S]) for b in range(LANES)]
        AT = [sb(f"AT{b}", [P, KT, H]) for b in range(LANES)]
        ks = [sb(f"ks{b}", [1, H]) for b in range(LANES)]
        kvm = [h3T[b][0:H, :] for b in range(LANES)]
        dg = [sb(f"dg{b}", [H, HD]) for b in range(LANES)]
        drep = [sb(f"drep{b}", [H, P]) for b in range(LANES)]
        sx = [sb(f"sx{b}", [P, KT, H]) for b in range(LANES)]
        mm = [sb(f"mm{b}", [H, D]) for b in range(LANES)]
        tw = [sb(f"tw{b}", [P, T, E * R]) for b in range(LANES)]
        twT = [h3T[b][0:E * R, :] for b in range(LANES)]
        v3 = resid
        rs = [sb(f"rs{b}", [P, T]) for b in range(LANES)]
        sg = attT
        hT = [PT[b][:, :, :, :].rearrange("p a b c -> p (a b) c") for b in range(LANES)]

        bank = [ctx.enter_context(nc.psum_tensor(f"bank{i}", [P, 512], F32)) for i in range(8)]
        dense = [[bank[4 * b + i] for i in range(4)] for b in range(LANES)]
        s_bank = [bank[i] for i in (0, 1, 7)]
        st_bank = [bank[i] for i in (2, 3, 5)]
        bank6b = bank[6][:, :].bitcast(BF16)

        w_in = [sem(f"w_in{n}") for n in range(len(CUTS) - 1)]
        wi_in = sem("wi_in")
        nomask_in = sem("nomask_in")
        small_ready = sem("small_ready")
        mask_ready = sem("mask_ready")
        ones_ready = sem("ones_ready")
        wi_ready = sem("wi_ready")
        x_in_s = lane_sem("x_in", 16)
        c_in_s = lane_sem("c_in", 16)
        m_in_s = lane_sem("m_in", 16)
        ctx_ps = lane_sem("ctx_ps", 1)
        ctx_t = lane_sem("ctx_t", 1)
        stats = lane_sem("stats", LAYERS)
        rstd_s = lane_sem("rstd_s", LAYERS)
        xh_s = lane_sem("xh_s", LAYERS)
        xhT_ps = lane_sem("xhT_ps", LAYERS)
        xhT_s = lane_sem("xhT_s", LAYERS)
        xb_s = lane_sem("xb_s", 5)
        x_new = lane_sem("x_new", LAYERS - 1)
        k_ps, v_ps, q_ps = (lane_sem(n, 2) for n in ("k_ps", "v_ps", "q_ps"))
        k_f, q_f, v_s = (lane_sem(n, 2) for n in ("k_f", "q_f", "v_s"))
        k_split, q_split = (lane_sem(n, 2) for n in ("k_split", "q_split"))
        k_out, q_out = (lane_sem(n, 2 * 16 * KT) for n in ("k_out", "q_out"))
        k_rows, q_rows = (lane_sem(n, 2 * 16 * len(GROUPS)) for n in ("k_rows", "q_rows"))
        attT_ps, attT_s, o_ps = (lane_sem(n, 2) for n in ("attT_ps", "attT_s", "o_ps"))
        NI2 = 2 * ITEMS
        s_ps = sem("s_ps", NI2 * GH)
        max_s = sem("max_s", NI2 * GH)
        mq_s = sem("mq_s", NI2)
        mT_ps = sem("mT_ps", NI2)
        negm_s = sem("negm_s", NI2)
        m_rows = [sem(f"m_rows{i}", NI2 * 16) for i in range(2)]
        st_ps = sem("st_ps", NI2 * GH)
        exp_s = sem("exp_s", NI2 * GH)
        pv_ps = sem("pv_ps", NI2)
        ot_s = sem("ot_s", NI2)
        otT_ps = sem("otT_ps", NI2)
        att_s = sem("att_s", NI2)
        gate_ps = lane_sem("gate_ps", 1)
        one_s = lane_sem("one_s", 1)
        ex_ps = lane_sem("ex_ps", T * 4)
        ex_used = lane_sem("ex_used", T * 4)
        oT_ps, oT_s = (lane_sem(n, 2) for n in ("oT_ps", "oT_s"))
        o_new = lane_sem("o_new", 3)
        n1_ps = lane_sem("n1_ps", 6)
        n1_s = lane_sem("n1_s", 6)
        n2_ps, n2_s, n3_ps, n3_s, n4_ps, n4_s = (lane_sem(n, 3) for n in ("n2_ps", "n2_s", "n3_ps", "n3_s", "n4_ps", "n4_s"))
        gc_ps, gc_s = (lane_sem(n, 4) for n in ("gc_ps", "gc_s"))
        third_pe, third_act, third_dve = lane_sem("third_pe", 7), lane_sem("third_act", 4), lane_sem("third_dve", 5)
        rank_pe, rank_act, rank_dve = lane_sem("rank_pe", 3), lane_sem("rank_act", 2), lane_sem("rank_dve", 2)
        last_pe, last_act, last_dve = lane_sem("last_pe", 6), lane_sem("last_act", 4), lane_sem("last_dve", 3)
        gu_ps, silu_s, hid_s = (lane_sem(n, HT) for n in ("gu_ps", "silu_s", "hid_s"))
        dn_ps = lane_sem("dn_ps", 1)
        stored = lane_sem("stored", 16)
        DVE_LINKS, ACT_LINKS, POOL_LINKS = 0, 0, 0
        dve_own = sem("dve_own")
        pool_own = sem("pool_own")

        block = ctx.enter_context(nc.Block())

        item = [(b, g) for b in range(LANES) for g in range(H // GH)]
        MHA = {0: dict(k="wk0", bk="bk0", v="wv0", bv="bv0", q="wq0", o="wo0", bo="bo0"),
               1: dict(k="wk1", bk="bk1", v="wv1", bv="bv1", q="wq1", o="wo1", bo="bo1")}
        LANE = range(LANES)

        @block.sync
        def _(sp):
            def load(n):
                sp.dma_start(w[:, CUTS[n]:CUTS[n + 1]], pack[:, CUTS[n]:CUTS[n + 1]]).then_inc(w_in[n], 16)

            for b in LANE:
                sp.dma_start(cin[b][:, :, :], ctx_in[b].rearrange("(t p) d -> p t d", p=P)).then_inc(c_in_s[b], 16)
            load(0)
            for b in LANE:
                sp.dma_start(xin[b][:, :, :], x_in[b].rearrange("(t p) d -> p t d", p=P)).then_inc(x_in_s[b], 16)
                sp.dma_start(mrow[b][:, :], mask_in[b:b + 1, :]).then_inc(m_in_s[b], 16)
            for i in range(2):
                sp.dma_start(OT[i][:, :], nomask[:, i * S:(i + 1) * S]).then_inc(nomask_in, 16)
            load(1)

            def write(parts, which, out_s, split_s, b, r, m):
                sp.wait_ge(split_s[b], nth(split_s[b], r, m + 1))
                for k in range(KT):
                    sp.dma_start(scratch[b, which, :, k * P:(k + 1) * P, :].rearrange("c p s -> p c s"),
                                 parts[b][:, k, :, :]).then_inc(out_s[b], 16)

            def read(dst, which, out_s, rows_s, b, r, m):
                sp.wait_ge(out_s[b], nth(out_s[b], r, 16 * KT * (m + 1)))
                at = 0
                for part, n in GROUPS:
                    src = scratch[b, which].rearrange("c (d h) s -> c d (h s)", h=H)
                    src = src[0:n] if which else src[part:part + 1].to_broadcast([n, HD, H * S])
                    sp.dma_start(dst[b][at * HD:(at + n) * HD, :, :].rearrange("p h s -> p (h s)"), src
                                 ).then_inc(rows_s[b], 16)
                    at += n

            def keys(r, m):
                for b in LANE:
                    write(kparts, 1, k_out, k_split, b, r, m)
                for b in LANE:
                    read(KA, 1, k_out, k_rows, b, r, m)

            def queries(b, r, m):
                write(qparts, 0, q_out, q_split, b, r, m)
                read(QA, 0, q_out, q_rows, b, r, m)

            keys(0, 0)
            for b in LANE:
                queries(b, 0, 0)
            load(2)
            LOADS = {4: 3, 6: 4}

            def a_round(it, first):
                for m in range(2):
                    if m:
                        keys(it, 1)
                        queries(0, it, 1)
                    for n, (b, g) in enumerate(item):
                        if m == 1 and n == 2:
                            queries(1, it, 1)
                        if first and m == 0 and n in LOADS:
                            load(LOADS[n])
                        if first and m == 0 and n == 2:
                            sp.dma_start(wi[:, :].bitcast(I32), ipack).then_inc(wi_in, 16)
                        j = m * ITEMS + n
                        sp.wait_ge(negm_s, nth(negm_s, it, j + 1))
                        for c in range(2):
                            sp.dma_start(QA[b][KR + c:KR + c + 1, g * GH:(g + 1) * GH, :],
                                         negm[c * GH:(c + 1) * GH, j % 2, :]).then_inc(m_rows[j % 2], 16)
                    if m == 0:
                        for b in LANE:
                            nx = (it * LANES + LANES + b) % B
                            sp.wait_ge(third_pe[b], nth(third_pe[b], it, 2))
                            sp.dma_start(cin[b][:, :, :], ctx_in[bass.ds(nx, 1), :, :].rearrange("a (t p) d -> p (a t) d", p=P)
                                         ).then_inc(c_in_s[b], 16)
                            sp.wait_ge(xb_s[b], nth(xb_s[b], it, 1))
                            sp.dma_start(xin[b][:, :, :], x_in[bass.ds(nx, 1), :, :].rearrange("a (t p) d -> p (a t) d", p=P)
                                         ).then_inc(x_in_s[b], 16)
                keys(it + 1, 0)
                for b in LANE:
                    queries(b, it + 1, 0)
                for b in LANE:
                    sp.wait_ge(x_new[b], nth(x_new[b], it, LAYERS - 1))
                    sp.dma_start(out[bass.ds(it * LANES + b, 1), :, :].rearrange("a (t p) d -> p (a t) d", p=P),
                                 x[b][:, :, :]).then_inc(stored[b], 16)
                for b in LANE:
                    nx = (it * LANES + LANES + b) % B
                    sp.wait_ge(stored[b], nth(stored[b], it, 16))
                    sp.dma_start(mrow[b][:, :], mask_in[bass.ds(nx, 1), :]).then_inc(m_in_s[b], 16)

            a_round(0, True)
            with sp.Fori(1, ITERS) as it:
                a_round(it, False)
            for b in LANE:
                sp.wait_ge(stored[b], 16 * ITERS)
                sp.wait_ge(x_in_s[b], 16 * (ITERS + 1))
                sp.wait_ge(c_in_s[b], 16 * (ITERS + 1))
                sp.wait_ge(m_in_s[b], 16 * (ITERS + 1))
                sp.wait_ge(k_out[b], nth(k_out[b], ITERS, 16 * KT))
                sp.wait_ge(k_rows[b], nth(k_rows[b], ITERS, 16 * len(GROUPS)))
                sp.wait_ge(q_out[b], nth(q_out[b], ITERS, 16 * KT))
                sp.wait_ge(q_rows[b], nth(q_rows[b], ITERS, 16 * len(GROUPS)))

        @block.gpsimd
        def _(pool):
            chain = [0]
            per[pool_own.name] = POOL_N = 2 * LAYERS + 2 * 2

            def link(ins, it=None):
                chain[0] += 1
                ins.then_inc(pool_own, 1)
                pool.wait_ge(pool_own, chain[0] if it is None else base + it * POOL_N + chain[0])

            def norm(b, L, r, it):
                pool.wait_ge(stats[b], nth(stats[b], r, L + 1))
                link(pool.tensor_tensor(veps[b][:, :], mv[b][:, :, 1], epsm[:, :], ALU.add), it)
                pool.tensor_tensor(rstd[b][:, :], veps[b][:, :], powm[:, :], ALU.pow).then_inc(rstd_s[b], 1)

            def split_k(b, m, r, it):
                f, parts = k_of[m], kparts
                pool.wait_ge(k_f[b], nth(k_f[b], r, m + 1))
                pool.tensor_tensor(parts[b][:, :, 1, :], f[b][:, :, :], parts[b][:, :, 0, :], ALU.subtract)
                link(pool.tensor_tensor(f[b][:, :, :], f[b][:, :, :], parts[b][:, :, 0, :], ALU.subtract), it)
                pool.tensor_tensor(parts[b][:, :, 2, :], f[b][:, :, :], parts[b][:, :, 1, :],
                                   ALU.subtract).then_inc(k_split[b], 1)

            def prepare(r, it=None):
                for b in LANE:
                    norm(b, 0, r, it)

            link(pool.memset(powm[:, :], -0.5))
            link(pool.memset(epsm[:, :], EPS))
            prepare(0)
            for b in LANE:
                split_k(b, 0, 0, None)
            for b in LANE:
                link(pool.memset(vaug[b][:, :, :, HD:32], 0.0))
                pool.memset(vaug[b][:, :, :, HD:HD + 1], 1.0).then_inc(ones_ready, 1)
            base = chain[0]
            pool.wait_ge(w_in[2], 16)
            pool.wait_ge(wi_in, 16)
            pool.tensor_scalar(wi[:, :], wi[:, :].bitcast(I32), 1.0 / 127.0, None, ALU.mult).then_inc(wi_ready, 1)

            with pool.Fori(0, ITERS) as it:
                chain[0] = 0

                def plus(b, bias, src=x):
                    for t in range(T):
                        last = pool.tensor_tensor(xb[b][:, t, :], src[b][:, t, :], W(bias), ALU.add)
                    last.then_inc(xb_s[b], 1)

                for b in LANE:
                    pool.wait_ge(x_in_s[b], nth(x_in_s[b], it, 16))
                    plus(b, "bo0", xin)
                for b in LANE:
                    norm(b, 1, it, it)
                    pool.wait_ge(xh_s[b], nth(xh_s[b], it, 2))
                    pool.tensor_tensor(xb[b][:, :, :], x[b][:, :, :], xh[b][:, :, :], ALU.add).then_inc(xb_s[b], 1)
                pool.wait_ge(w_in[3], 16)
                norm(0, 2, it, it)
                for b in LANE:
                    split_k(b, 1, it, it)
                plus(0, "bo1")
                norm(1, 2, it, it)
                plus(1, "bo1")
                for b in LANE:
                    norm(b, 3, it, it)
                pool.wait_ge(w_in[4], 16)
                for L, bias in ((4, "bao"), (5, "blin"), (6, None), (7, None)):
                    for b in LANE:
                        norm(b, L, it, it)
                        if bias:
                            plus(b, bias)
                    if L == 6:
                        for b in LANE:
                            split_k(b, 0, it + 1, it)
                prepare(it + 1, it)
                assert chain[0] == POOL_N, chain[0]

        @block.scalar
        def _(act):
            act.wait_ge(w_in[0], 16)

            def keys(b, m, r, ps):
                act.wait_ge(k_ps[b], nth(k_ps[b], r, m + 1))
                for k in range(KT):
                    act.activation(kparts[b][:, k, 0, :], ps[:, k * S:(k + 1) * S], ACT.Identity,
                                   bias=W(MHA[m]["bk"])[:, k:k + 1])
                    last = act.activation(k_of[m][b][:, k, :], ps[:, k * S:(k + 1) * S], ACT.Identity,
                                          bias=W(MHA[m]["bk"])[:, k:k + 1])
                last.then_inc(k_f[b], 1)

            def context(b, r):
                act.wait_ge(ctx_ps[b], nth(ctx_ps[b], r, 1))
                act.copy(ctxT[b][:, :, :].rearrange("p k s -> p (k s)"), dense[b][2][:, :]).then_inc(ctx_t[b], 1)

            def turned(b, L, r):
                act.wait_ge(xhT_ps[b], nth(xhT_ps[b], r, L + 1))
                act.copy(xhT[b][:, :, :].rearrange("p k s -> p (k s)"), dense[b][0][:, :]).then_inc(xhT_s[b], 1)

            def queries(b, m, r):
                act.wait_ge(q_ps[b], nth(q_ps[b], r, m + 1))
                for k in range(KT):
                    last = act.activation(qf[b][:, k, :], dense[b][m][:, k * S:(k + 1) * S], ACT.Identity,
                                          bias=bqs[m][:, k:k + 1], scale=1.0 / HD ** 0.5)
                last.then_inc(q_f[b], 1)

            def third_exp(b, r):
                act.wait_ge(third_dve[b], nth(third_dve[b], r, 1))
                act.activation(kh[b][:, :, :], kz[b][:, :, :], ACT.Exp, scale=-1.0).then_inc(third_act[b], 1)

            def third_sums(b, r):
                act.wait_ge(third_pe[b], nth(third_pe[b], r, 2))
                act.copy(AT[b][:, :, :].rearrange("p k h -> p (k h)"), dense[b][3][:, 0:KT * H])
                act.copy(ks[b][:, :], dense[b][3][0:1, 64:64 + H]).then_inc(third_act[b], 1)

            def third_mm(b, r, ps):
                act.wait_ge(third_pe[b], nth(third_pe[b], r, 5))
                act.copy(mm[b][:, :], ps[0:H, 0:D]).then_inc(third_act[b], 1)

            for b in LANE:
                context(b, 0)
            for b in LANE:
                third_exp(b, 0)
            for b in LANE:
                keys(b, 0, 0, dense[b][2])
            for b in LANE:
                turned(b, 0, 0)
            act.wait_ge(small_ready, 1)
            for b in LANE:
                queries(b, 0, 0)
            for b in LANE:
                third_sums(b, 0)
            for b in LANE:
                third_mm(b, 0, dense[b][3])
            act.wait_ge(mask_ready, 1)
            with act.Fori(0, ITERS) as it:
                def evac_xhT(b, L):
                    turned(b, L, it)

                def evac_att(b, m):
                    act.wait_ge(attT_ps[b], nth(attT_ps[b], it, m + 1))
                    act.copy(attT[b][:, :, :].rearrange("p k s -> p (k s)"), dense[b][0][:, :]).then_inc(attT_s[b], 1)

                for m in range(2):
                    L = 2 * m
                    if m == 1:
                        for b in LANE:
                            act.wait_ge(k_split[b], nth(k_split[b], it, 1))
                            act.wait_ge(q_out[b], nth(q_out[b], it, 16 * KT))
                            keys(b, 1, it, (dense[0][2], dense[1][0])[b])
                        evac_xhT(0, 2)
                        queries(0, 1, it)
                    for s in range(ITEMS + 5):
                        j = m * ITEMS + s
                        for h in range(GH):
                            if 0 <= s - 3 < ITEMS:
                                n = j - 3
                                act.wait_ge(st_ps, nth(st_ps, it, GH * n + h + 1))
                                if n >= 2 and h == 0:
                                    act.wait_ge(pv_ps, nth(pv_ps, it, n - 1))
                                act.activation(PT[n % 2][:, h, :, :].rearrange("p t s -> p (t s)"),
                                               st_bank[(GH * (s - 3) + h) % 3][:, :], ACT.Exp).then_inc(exp_s, 1)
                            if h == 1 and 0 <= s - 1 < ITEMS:
                                act.wait_ge(mT_ps, nth(mT_ps, it, j))
                                if j - 1 >= 2:
                                    act.wait_ge(m_rows[(j - 3) % 2], nth(m_rows[0], it, 32 * ((j - 3) // 2 + 1)))
                                act.copy(negm[:, (j - 1) % 2, :], bank6b[0:2 * GH, 512:512 + S]).then_inc(negm_s, 1)
                            if h == 1 and 0 <= s - 4 < ITEMS:
                                n = j - 4
                                act.wait_ge(pv_ps, nth(pv_ps, it, n + 1))
                                if n >= 2:
                                    act.wait_ge(otT_ps, nth(otT_ps, it, n - 1))
                                act.copy(OT[n % 2][:, :], bank[4][:, 0:S]).then_inc(ot_s, 1)
                        if m == 1 and s == 0:
                            evac_xhT(1, 2)
                        if m == 1 and s == 1:
                            queries(1, 1, it)
                        if s == 8:
                            evac_att(0, m)
                        if s == 11:
                            evac_xhT(0, L + 1)
                    evac_att(1, m)
                    if m == 0:
                        evac_xhT(1, 1)
                def glob(b, n):
                    act.wait_ge(gc_ps[b], nth(gc_ps[b], it, n))
                    if n == 1:
                        ins = act.copy(gcT[b][:, :], dense[b][3][:, 0:KT])
                    elif n == 2:
                        ins = act.activation(g1[b][:, :], dense[b][3][:, 4:5], ACT.Gelu, bias=W("gb1"))
                    elif n == 3:
                        ins = act.activation(g2[b][:, :], dense[b][3][0:64, 8:9].to_broadcast([64, P]), ACT.Gelu, bias=W("gb2"))
                    else:
                        ins = act.activation(tg[b][:, :], dense[b][3][:, 12:13], ACT.Tanh, bias=hb3[:, :], scale=0.5)
                    ins.then_inc(gc_s[b], 1)

                def turn(b, c):
                    if c == 0 and b == 1:
                        evac_xhT(b, 3)
                    elif c:
                        act.wait_ge(oT_ps[b], nth(oT_ps[b], it, c))
                        act.copy(xhT[b][:, :, :].rearrange("p k s -> p (k s)"), dense[b][0][:, :]).then_inc(oT_s[b], 1)

                def net(b, c, layer):
                    if c == 0:
                        glob(b, layer)
                    if layer == 1:
                        for k in range(KT):
                            act.wait_ge(n1_ps[b], nth(n1_ps[b], it, 2 * c + k + 1))
                            act.activation(h1T[b][:, k, :], dense[b][1 + k][:, 0:S], ACT.Gelu,
                                           bias=W("cb1")[:, k:k + 1]).then_inc(n1_s[b], 1)
                    elif layer == 2:
                        act.wait_ge(n2_ps[b], nth(n2_ps[b], it, c + 1))
                        act.activation(h2T[b][:, :], dense[b][0][:, 0:S], ACT.Gelu, bias=W("cb2")).then_inc(n2_s[b], 1)
                    elif layer == 3:
                        act.wait_ge(n3_ps[b], nth(n3_ps[b], it, c + 1))
                        act.activation(h3T[b][:, :], dense[b][1][0:64, 0:S], ACT.Gelu, bias=W("cb3")).then_inc(n3_s[b], 1)
                    else:
                        act.wait_ge(n4_ps[b], nth(n4_ps[b], it, c + 1))
                        act.activation(th[b][:, :], dense[b][2][:, 0:T], ACT.Tanh, bias=hb4[:, :], scale=0.5).then_inc(n4_s[b], 1)

                def last_key(b):
                    act.wait_ge(last_pe[b], nth(last_pe[b], it, 1))
                    for k in range(KT):
                        last = act.activation(kf[b][:, k, :], dense[b][3][:, k * S:(k + 1) * S], ACT.Identity,
                                              bias=W("bk3")[:, k:k + 1])
                    last.then_inc(last_act[b], 1)

                net(0, 0, 1)
                for c in range(3):
                    turn(0, c)
                    if c:
                        net(1, c - 1, 3)
                        net(0, c, 1)
                        net(1, c - 1, 4)
                    net(0, c, 2)
                    turn(1, c)
                    net(0, c, 3)
                    net(1, c, 1)
                    net(0, c, 4)
                    net(1, c, 2)
                net(1, 2, 3)
                last_key(0)
                net(1, 2, 4)
                last_key(1)
                for b in LANE:
                    evac_xhT(b, 4)
                    act.wait_ge(third_pe[b], nth(third_pe[b], it, 6))
                    act.activation(qh[b][:, :], dense[b][1][0:H, 0:S], ACT.Tanh, bias=hbaq[:, :], scale=0.5).then_inc(third_act[b], 1)
                for b in LANE:
                    evac_xhT(b, 5)
                    act.wait_ge(rank_dve[b], nth(rank_dve[b], it, 1))
                    for t in range(T):
                        last = act.activation(r1[b][:, t, :], sc[b][:, t, 0:E], ACT.Exp, bias=m1[b][:, t:t + 1])
                    last.then_inc(rank_act[b], 1)

                def turn_low_rank(b):
                    act.wait_ge(rank_pe[b], nth(rank_pe[b], it, 2))
                    act.copy(twT[b], dense[b][2][0:E * R, 0:S]).then_inc(rank_act[b], 1)

                for b in LANE:
                    turn_low_rank(b)
                    context(b, it + 1)
                def last_query(b):
                    evac_xhT(b, 6)
                    act.wait_ge(last_pe[b], nth(last_pe[b], it, 3))
                    for k in range(KT):
                        last = act.activation(qf[b][:, k, :], dense[b][1][:, k * S:(k + 1) * S], ACT.Identity,
                                              bias=bqs[2][:, k:k + 1], scale=1.0 / HD ** 0.5)
                    last.then_inc(last_act[b], 1)

                def last_exp(b):
                    act.wait_ge(last_dve[b], nth(last_dve[b], it, 3))
                    for t in range(T):
                        last = act.activation(att[b][:, t, :], dense[b][0][:, t * S:(t + 1) * S], ACT.Exp,
                                              bias=m1[b][:, t:t + 1], accum_out=rs[b][:, t:t + 1])
                    last.then_inc(last_act[b], 1)

                def last_turn(b):
                    act.wait_ge(last_pe[b], nth(last_pe[b], it, 5))
                    act.copy(attT[b][:, :, :].rearrange("p k s -> p (k s)"), dense[b][1][:, :]).then_inc(last_act[b], 1)

                def next_keys(b):
                    act.wait_ge(q_out[b], nth(q_out[b], it, 2 * 16 * KT))
                    act.wait_ge(x_new[b], nth(x_new[b], it, 5))
                    keys(b, 0, it + 1, dense[b][2])

                last_query(0)
                next_keys(0)
                third_exp(0, it + 1)
                last_query(1)
                last_exp(0)
                third_exp(1, it + 1)
                next_keys(1)
                for b in LANE:
                    third_sums(b, it + 1)
                last_exp(1)
                last_turn(0)
                last_turn(1)
                for b in LANE:
                    evac_xhT(b, 7)
                for k in range(HT):
                    for b in LANE:
                        act.wait_ge(gu_ps[b], nth(gu_ps[b], it, k + 1))
                        if k >= 2:
                            act.wait_ge(hid_s[b], nth(hid_s[b], it, k - 1))
                        act.activation(sg[b][:, k % 2, :], dense[b][1 + k % 2][:, 0:S], ACT.Silu).then_inc(silu_s[b], 1)
                    if k == 4:
                        for b in LANE:
                            third_mm(b, it + 1, dense[b][0])
                for b in LANE:
                    turned(b, 0, it + 1)
                for b in LANE:
                    queries(b, 0, it + 1)

        @block.vector
        def _(dve):
            chain = [0]
            per[dve_own.name] = DVE_N = 140

            def link(ins, it=None, part=False):
                chain[0] += 1
                ins.then_inc(dve_own, 1)
                dve.wait_ge(dve_own, chain[0] if it is None else base + it * DVE_N + chain[0])
                if part:
                    dve.memset(junk[:, :], 0.0)

            def norm(b, L, it, src=x):
                for t in range(T):
                    last = dve.bn_stats(bst[b][:, t, :], src[b][:, t, :])
                link(last, it, part=True)
                for t in range(T):
                    last = dve.bn_aggr(mv[b][:, t, :], bst[b][:, t, :])
                last.then_inc(stats[b], 1)

            def norm2(b, L, r, src=x):
                dve.wait_ge(rstd_s[b], nth(rstd_s[b], r, L + 1))
                for t in range(T):
                    last = dve.tensor_scalar(xh[b][:, t, :], src[b][:, t, :], mv[b][:, t, 0:1], rstd[b][:, t:t + 1],
                                             ALU.subtract, ALU.mult)
                last.then_inc(xh_s[b], 1)

            def values(b, m, r):
                dve.wait_ge(v_ps[b], nth(v_ps[b], r, m + 1))
                ps = dense[b][2] if m == 0 else (dense[0][3], dense[1][1])[b]
                for t in range(T):
                    last = dve.tensor_tensor(
                        vaug[b][:, t, :, 0:HD], ps[:, t * D:(t + 1) * D].rearrange("p (h d) -> p h d", h=H),
                        W(MHA[m]["bv"]).rearrange("p (h d) -> p h d", h=H), ALU.add)
                last.then_inc(v_s[b], 1)

            def prepare(r, it=None):
                for b in LANE:
                    dve.wait_ge(x_in_s[b], nth(x_in_s[b], r, 16))
                    norm(b, 0, it, xin)
                for b in LANE:
                    norm2(b, 0, r, xin)

            def split_q(b, m, r, it):
                f, parts = qf, qparts
                dve.wait_ge(q_f[b], nth(q_f[b], r, m + 1))
                dve.wait_ge(k_out[b], nth(k_out[b], r, 16 * KT * (m + 1)))
                link(dve.tensor_copy(parts[b][:, :, 0, :], f[b][:, :, :]), it)
                link(dve.tensor_tensor(f[b][:, :, :], f[b][:, :, :], parts[b][:, :, 0, :], ALU.subtract), it)
                link(dve.tensor_copy(parts[b][:, :, 1, :], f[b][:, :, :]), it)
                dve.tensor_tensor(parts[b][:, :, 2, :], f[b][:, :, :], parts[b][:, :, 1, :], ALU.subtract).then_inc(q_split[b], 1)

            def third_z(b, r):
                dve.wait_ge(third_pe[b], nth(third_pe[b], r, 1))
                dve.tensor_tensor(kz[b][:, :, :].rearrange("p t h -> p (t h)"), dense[b][3][:, 0:T * H], W("bak"),
                                  ALU.add).then_inc(third_dve[b], 1)

            def third_sigmoid(b, r, it):
                dve.wait_ge(third_act[b], nth(third_act[b], r, 1))
                link(dve.tensor_scalar(kz[b][:, :, :], kh[b][:, :, :], 1.0, None, ALU.add), it)
                dve.reciprocal(kh[b][:, :, :], kz[b][:, :, :]).then_inc(third_dve[b], 1)

            def third_diagonal(b, r, it, ps):
                dve.wait_ge(third_pe[b], nth(third_pe[b], r, 3))
                link(dve.tensor_tensor(kvm[b], ps[0:H, 0:D], W("diag"), ALU.mult), it)
                link(dve.tensor_reduce(dg[b][:, :], kvm[b].rearrange("h (g d) -> h d g", d=HD), AX.X, ALU.add), it)
                dve.tensor_copy(drep[b][:, :].rearrange("h (g d) -> h g d", d=HD),
                                dg[b][:, :].unsqueeze(1).to_broadcast([H, P // HD, HD])).then_inc(third_dve[b], 1)

            def third_state(b, r, ps):
                dve.wait_ge(third_pe[b], nth(third_pe[b], r, 4))
                dve.tensor_tensor(sx[b][:, :, :], ps[:, 0:H].unsqueeze(1).to_broadcast([P, KT, H]),
                                  W("pick", KT), ALU.mult).then_inc(third_dve[b], 1)

            for b in LANE:
                dve.memset(KA[b][KR:KM, :, :], 1.0)
            dve.memset(mx[:, :, :, :], 0.0)
            prepare(0)
            dve.wait_ge(w_in[0], 16)
            dve.tensor_copy(identb[:, :], ident)
            for m, name in enumerate(("bq0", "bq1", "bq3")):
                dve.tensor_scalar(bqs[m][:, :], W(name), 1.0 / HD ** 0.5, None, ALU.mult)
            dve.tensor_scalar(hb4[:, :], W("cb4"), 0.5, None, ALU.mult)
            dve.tensor_scalar(hb3[:, :], W("gb3"), 0.5, None, ALU.mult)
            dve.tensor_scalar(hbaq[:, :], W("baq"), 0.5, None, ALU.mult)
            dve.tensor_scalar(r03[:, :], W("range"), 0.3, None, ALU.mult)
            dve.tensor_scalar(r07[:, :], W("range"), 0.7, None, ALU.mult).then_inc(small_ready, 1)
            dve.wait_ge(small_ready, 1)
            for b in LANE:
                third_z(b, 0)
            for b in LANE:
                third_sigmoid(b, 0, None)
            dve.wait_ge(w_in[1], 16)
            for b in LANE:
                split_q(b, 0, 0, None)
            for b in LANE:
                third_diagonal(b, 0, None, dense[b][3])
            for b in LANE:
                third_state(b, 0, dense[b][3])
            for b in LANE:
                values(b, 0, 0)
            dve.wait_ge(nomask_in, 32)
            for t in range(T):
                last = dve.tensor_copy(maskb[:, t, :], OT[t][:, :])
            last.then_inc(mask_ready, 1)
            base = chain[0]

            with dve.Fori(0, ITERS) as it:
                chain[0] = 0

                def update(b, L, ps, out_s, n, early, k):
                    dve.wait_ge(out_s[b], nth(out_s[b], it, n))
                    if early:
                        dve.wait_ge(xb_s[b], nth(xb_s[b], it, k))
                    src = xb if early else x
                    ins = dve.tensor_tensor(x[b][:, :, :].rearrange("p t d -> p (t d)"), ps,
                                            src[b][:, :, :].rearrange("p t d -> p (t d)"), ALU.add)
                    ins.then_inc(x_new[b], 1)
                    dve.wait_ge(x_new[b], nth(x_new[b], it, max(L, 1)))

                def choose(b):
                    dve.wait_ge(gate_ps[b], nth(gate_ps[b], it, 1))
                    v = dense[b][1][:, 0:T * E].rearrange("p (t e) -> p t e", t=T)
                    link(dve.tensor_reduce(m1[b][:, :], v, AX.X, ALU.max), it)
                    for t in range(T):
                        last = dve.scalar_tensor_tensor(r1[b][:, t, :], v[:, t, :], m1[b][:, t:t + 1], W("desc"),
                                                        ALU.is_equal, ALU.mult)
                    link(last, it)
                    link(dve.tensor_reduce(m2[b][:, :], r1[b][:, :, :], AX.X, ALU.max), it)
                    for t in range(T):
                        last = dve.tensor_scalar(one[b][:, t, :], r1[b][:, t, :], m2[b][:, t:t + 1], None, ALU.is_equal)
                    last.then_inc(one_s[b], 1)

                def experts(b, n):
                    t, i = n // 4, n % 4
                    if n == 0:
                        dve.wait_ge(one_s[b], nth(one_s[b], it, 1))
                        dve.wait_ge(xb_s[b], nth(xb_s[b], it, 2))
                    dve.wait_ge(ex_ps[b], nth(ex_ps[b], it, n + 1))
                    ps = dense[b][2 + i % 2]
                    for e in range(2):
                        k = 2 * i + e
                        src, dst = (xb, x) if k % 2 == 0 else (x, xb)
                        if k == E - 1:
                            dst = x
                        ins = dve.scalar_tensor_tensor(
                            dst[b][:, t, :], ps[:, e * D:(e + 1) * D], one[b][:, t, k:k + 1],
                            src[b][:, t, :], ALU.mult, ALU.add)
                        if e == 0:
                            link(ins, it)
                    ins.then_inc(ex_used[b], 1)
                    dve.wait_ge(ex_used[b], nth(ex_used[b], it, n + 1))

                dve.wait_ge(w_in[0], 16)
                dve.wait_ge(w_in[1], 16)
                for m in range(2):
                    L = 2 * m
                    for s in range(ITEMS + 5):
                        j = m * ITEMS + s
                        for h in range(GH):
                            if s < ITEMS:
                                dve.wait_ge(s_ps, nth(s_ps, it, GH * j + h + 1))
                                dve.tensor_reduce(mx[:, j % 2, h, :], s_bank[(GH * s + h) % 3][:, :].rearrange("p (t s) -> p t s", t=T),
                                                  AX.X, ALU.max).then_inc(max_s, 1)
                            if h == 0 and 0 <= s - 5 < ITEMS:
                                n, (b, g) = j - 5, item[s - 5]
                                dve.wait_ge(otT_ps, nth(otT_ps, it, n + 1))
                                v = bank[6][:, 0:S].rearrange("p (t h e) -> p t h e", t=T, h=GH)
                                link(dve.reciprocal(rc[:, :, :], v[:, :, :, HD]), it)
                                dve.tensor_tensor(
                                    att[b][:, :, g * GH * HD:(g + 1) * GH * HD].rearrange("p t (h d) -> p t h d", h=GH),
                                    v[:, :, :, 0:HD], rc[:, :, :].unsqueeze(3).to_broadcast([P, T, GH, HD]),
                                    ALU.mult).then_inc(att_s, 1)
                        if s < ITEMS:
                            dve.wait_ge(max_s, nth(max_s, it, GH * (j + 1)))
                            if j >= 2:
                                dve.wait_ge(mT_ps, nth(mT_ps, it, j - 1))
                            v = mx[:, j % 2, :, :].rearrange("p h t -> p t h")
                            link(dve.tensor_scalar(mq[:, j % 2, :, 0, :], v, -1.0, None, ALU.mult), it)
                            dve.scalar_tensor_tensor(mq[:, j % 2, :, 1, :], v, -1.0, mq[:, j % 2, :, 0, :],
                                                     ALU.mult, ALU.subtract).then_inc(mq_s, 1)
                        if m == 1 and s == 1:
                            split_q(1, 1, it, it)
                        if m == 1 and s == 2:
                            values(0, 1, it)
                        if s == 10:
                            update(0, L, dense[0][1][:, :], o_ps, m + 1, True, 1 + 2 * m)
                            norm(0, L + 1, it)
                            norm2(0, L + 1, it)
                    if m == 0:
                        dve.wait_ge(w_in[2], 16)
                        choose(0)
                    update(1, L, dense[1][1][:, :], o_ps, m + 1, True, 1 + 2 * m)
                    norm(1, L + 1, it)
                    if m == 0:
                        for n in range(T * 4):
                            experts(0, n)
                            if n == 1:
                                norm2(1, 1, it)
                            if n == 4:
                                choose(1)
                        norm(0, 2, it)
                        for n in range(T * 4):
                            experts(1, n)
                            if n == 0:
                                norm2(0, 2, it)
                                dve.wait_ge(w_in[3], 16)
                            if n == 2:
                                split_q(0, 1, it, it)
                        norm(1, 2, it)
                        values(1, 1, it)
                        norm2(1, 2, it)
                    else:
                        norm2(1, 3, it)
                def couple(b, c):
                    src, dst = (xh, o2) if c % 2 == 0 else (o2, xh)
                    if c == 0:
                        dve.wait_ge(gc_s[b], nth(gc_s[b], it, 4))
                        link(dve.tensor_scalar(cbase[b][:, :], tg[b][:, :], r07[:, :], 0.1, ALU.mult, ALU.add), it)
                    dve.wait_ge(n4_s[b], nth(n4_s[b], it, c + 1))
                    link(dve.tensor_scalar(cc[b][:, :], th[b][:, :], r03[:, :], cbase[b][:, :], ALU.mult, ALU.add), it)
                    link(dve.tensor_scalar(cn[b][:, :], cc[b][:, :], -1.0, None, ALU.mult), it)
                    for t in range(T):
                        for to, of, sign in ((0, 2, cc), (1, 3, cn), (2, 0, cn), (3, 1, cc)):
                            last = dve.scalar_tensor_tensor(
                                dst[b][:, t, to * 64:(to + 1) * 64], src[b][:, t, of * 64:(of + 1) * 64],
                                sign[b][:, t:t + 1], src[b][:, t, to * 64:(to + 1) * 64], ALU.mult, ALU.add)
                    last.then_inc(o_new[b], 1)
                    if c == 2:
                        dve.wait_ge(o_new[b], nth(o_new[b], it, 3))
                        dve.tensor_tensor(x[b][:, :, :], x[b][:, :, :], dst[b][:, :, :], ALU.add).then_inc(x_new[b], 1)
                        dve.wait_ge(x_new[b], nth(x_new[b], it, 3))
                        norm(b, 4, it)

                def third_query(b):
                    dve.wait_ge(third_act[b], nth(third_act[b], it, 4))
                    dve.tensor_scalar(qh[b][:, :], qh[b][:, :], 0.5, 0.5, ALU.mult, ALU.add).then_inc(third_dve[b], 1)

                def last_value(b):
                    dve.wait_ge(last_pe[b], nth(last_pe[b], it, 2))
                    for t in range(T):
                        last = dve.tensor_tensor(v3[b][:, t, :], dense[b][3][:, t * D:(t + 1) * D], W("bv3"), ALU.add)
                    last.then_inc(last_dve[b], 1)

                def logits(b):
                    dve.wait_ge(rank_pe[b], nth(rank_pe[b], it, 1))
                    v = dense[b][1][:, 0:T * 40].rearrange("p (t e) -> p t e", t=T)
                    link(dve.tensor_copy(sc[b][:, :, :], v), it)
                    link(dve.tensor_reduce(m2[b][:, :], sc[b][:, :, 0:E], AX.X, ALU.max), it)
                    dve.tensor_scalar(m1[b][:, :], m2[b][:, :], -1.0, None, ALU.mult).then_inc(rank_dve[b], 1)

                def top2(b):
                    dve.wait_ge(rank_act[b], nth(rank_act[b], it, 1))
                    link(dve.tensor_reduce(m1[b][:, :], r1[b][:, :, :], AX.X, ALU.add), it)
                    link(dve.reciprocal(m1[b][:, :], m1[b][:, :]), it)
                    link(dve.tensor_copy(r3[b][:, :, :], r1[b][:, :, :]), it)
                    for k in range(2):
                        link(dve.tensor_reduce(m2[b][:, :], r3[b][:, :, :], AX.X, ALU.max), it)
                        for t in range(T):
                            last = dve.scalar_tensor_tensor(r2[b][:, t, :], r3[b][:, t, :], m2[b][:, t:t + 1], W("desc"),
                                                            ALU.is_equal, ALU.mult)
                        link(last, it)
                        link(dve.tensor_reduce(m2[b][:, :], r2[b][:, :, :], AX.X, ALU.max), it)
                        for t in range(T):
                            last = dve.tensor_scalar(one[b][:, t, :], r2[b][:, t, :], m2[b][:, t:t + 1], None, ALU.is_equal)
                        link(last, it)
                        link(dve.scalar_tensor_tensor(r3[b][:, :, :], one[b][:, :, :], -4.0, r3[b][:, :, :], ALU.mult, ALU.add), it)
                    link(dve.scalar_tensor_tensor(r2[b][:, :, :], r3[b][:, :, :], 0.0, r1[b][:, :, :], ALU.is_lt, ALU.mult), it)
                    for t in range(T):
                        last = dve.tensor_scalar(r2[b][:, t, :], r2[b][:, t, :], m1[b][:, t:t + 1], None, ALU.mult)
                    link(last, it)
                    dve.tensor_tensor(tw[b][:, :, :].rearrange("p t (e r) -> p t e r", r=R),
                                      sc[b][:, :, E:E + E * R].rearrange("p t (e r) -> p t e r", r=R),
                                      r2[b][:, :, :].unsqueeze(3).to_broadcast([P, T, E, R]), ALU.mult).then_inc(rank_dve[b], 1)

                for c in range(3):
                    couple(0, c)
                    if c == 2:
                        norm2(0, 4, it)
                    couple(1, c)
                third_query(0)
                norm2(1, 4, it)
                update(0, 4, dense[0][0][:, :], third_pe, 7, True, 4)
                norm(0, 5, it)
                third_query(1)
                norm2(0, 5, it)
                dve.wait_ge(w_in[4], 16)
                last_value(0)
                update(1, 4, dense[1][0][:, :], third_pe, 7, True, 4)
                norm(1, 5, it)
                logits(0)
                norm2(1, 5, it)
                last_value(1)
                top2(0)
                logits(1)

                def low_rank(b):
                    dve.wait_ge(rank_pe[b], nth(rank_pe[b], it, 3))
                    dve.wait_ge(xb_s[b], nth(xb_s[b], it, 5))
                    for t in range(T):
                        last = dve.tensor_tensor(x[b][:, t, :], dense[b][3 - 3 * t][:, 0:D], xb[b][:, t, :], ALU.add)
                    last.then_inc(x_new[b], 1)
                    dve.wait_ge(x_new[b], nth(x_new[b], it, 5))
                    norm(b, 6, it)

                def last_max(b):
                    dve.wait_ge(last_pe[b], nth(last_pe[b], it, 4))
                    link(dve.tensor_reduce(m2[b][:, :], dense[b][0][:, :].rearrange("p (t s) -> p t s", t=T), AX.X, ALU.max), it)
                    dve.tensor_scalar(m1[b][:, :], m2[b][:, :], -1.0, None, ALU.mult).then_inc(last_dve[b], 1)

                for b in LANE:
                    dve.wait_ge(m_in_s[b], nth(m_in_s[b], it, 16))
                    dve.tensor_scalar(mrow[b][:, :], mrow[b][:, :], -1.0, 10000.0, ALU.add, ALU.mult).then_inc(last_dve[b], 1)
                top2(1)
                for b in LANE:
                    low_rank(b)
                norm2(0, 6, it)
                third_z(0, it + 1)
                norm2(1, 6, it)
                third_z(1, it + 1)
                last_max(0)
                for b in LANE:
                    third_sigmoid(b, it + 1, it)
                last_max(1)

                def last_update(b):
                    dve.wait_ge(last_act[b], nth(last_act[b], it, 3))
                    link(dve.reciprocal(m2[b][:, :], rs[b][:, :]), it)
                    dve.wait_ge(last_pe[b], nth(last_pe[b], it, 6))
                    for t in range(T):
                        last = dve.scalar_tensor_tensor(x[b][:, t, :], dense[b][3][:, t * D:(t + 1) * D], m2[b][:, t:t + 1],
                                                        x[b][:, t, :], ALU.mult, ALU.add)
                    last.then_inc(x_new[b], 1)
                    dve.wait_ge(x_new[b], nth(x_new[b], it, 6))
                    norm(b, 7, it)

                values(0, 0, it + 1)
                last_update(0)
                norm2(0, 7, it)
                last_update(1)
                values(1, 0, it + 1)
                norm2(1, 7, it)
                for k in range(HT):
                    for b in LANE:
                        dve.wait_ge(silu_s[b], nth(silu_s[b], it, k + 1))
                        dve.tensor_tensor(hT[b][:, k, :], sg[b][:, k % 2, :], dense[b][1 + k % 2][:, S:2 * S],
                                          ALU.mult).then_inc(hid_s[b], 1)
                    if k == 1:
                        for b in LANE:
                            third_diagonal(b, it + 1, it, dense[b][0])
                    if k == 2:
                        for b in LANE:
                            third_state(b, it + 1, dense[b][0])
                    if k == 3:
                        prepare(it + 1, it)
                for b in LANE:
                    split_q(b, 0, it + 1, it)
                for b in LANE:
                    update(b, 7, dense[b][3][:, :], dn_ps, 1, False, 0)
                assert chain[0] == DVE_N, chain[0]

        @block.tensor
        def _(pe):
            pe.wait_ge(w_in[0], 16)

            def project_T(ps, name, src, rows=KT):
                for k in range(rows):
                    for kk in range(KT):
                        last = pe.matmul(ps[:, k * S:(k + 1) * S], W(name, KT)[:, kk, k * P:(k + 1) * P],
                                         src[:, kk, :], start=(kk == 0), stop=(kk == KT - 1))
                return last

            def project(ps, name, src):
                for t in range(T):
                    for kk in range(KT):
                        last = pe.matmul(ps[:, t * D:(t + 1) * D], src[:, kk, t * P:(t + 1) * P],
                                         W(name, KT)[:, kk, :], start=(kk == 0), stop=(kk == KT - 1))
                return last

            def transpose_all(ps, src):
                for k in range(KT):
                    for t in range(T):
                        last = pe.transpose(ps[:, k * S + t * P:k * S + (t + 1) * P], src[:, t, k * P:(k + 1) * P], ident)
                return last

            def keep_warm(ps, n):
                for _ in range(n):
                    pe.matmul(ps[:, :], identb[:, :], maskb[:, :, :].rearrange("p t s -> p (t s)"), start=True, stop=True)

            def context(b, r):
                pe.wait_ge(c_in_s[b], nth(c_in_s[b], r, 16))
                transpose_all(dense[b][2], cin[b]).then_inc(ctx_ps[b], 1)

            def keys(b, r):
                pe.wait_ge(ctx_t[b], nth(ctx_t[b], r, 1))
                project_T(dense[b][2], "wk0", ctxT[b]).then_inc(k_ps[b], 1)

            def values(b, r):
                pe.wait_ge(k_f[b], nth(k_f[b], r, 1))
                project(dense[b][2], "wv0", ctxT[b]).then_inc(v_ps[b], 1)

            def turn_x(b, L, r):
                pe.wait_ge(xh_s[b], nth(xh_s[b], r, L + 1))
                transpose_all(dense[b][0], xh[b]).then_inc(xhT_ps[b], 1)

            def queries(b, m, r):
                pe.wait_ge(xhT_s[b], nth(xhT_s[b], r, 2 * m + 1))
                project_T(dense[b][m], MHA[m]["q"], xhT[b]).then_inc(q_ps[b], 1)

            def third_z(b, r):
                pe.wait_ge(ctx_t[b], nth(ctx_t[b], r, 1))
                for t in range(T):
                    for kk in range(KT):
                        last = pe.matmul(dense[b][3][:, t * H:(t + 1) * H], ctxT[b][:, kk, t * P:(t + 1) * P],
                                         W("ak", KT)[:, kk, :], start=(kk == 0), stop=(kk == KT - 1))
                last.then_inc(third_pe[b], 1)

            def third_sums(b, r):
                pe.wait_ge(third_dve[b], nth(third_dve[b], r, 2))
                for k in range(KT):
                    for t in range(T):
                        pe.matmul(dense[b][3][:, k * H:(k + 1) * H], cin[b][:, t, k * P:(k + 1) * P], kh[b][:, t, :],
                                  start=(t == 0), stop=(t == T - 1))
                for t in range(T):
                    last = pe.matmul(dense[b][3][0:1, 64:64 + H], W("ones")[:, 0:1], kh[b][:, t, :],
                                     start=(t == 0), stop=(t == T - 1))
                last.then_inc(third_pe[b], 1)

            def third_kv(b, r, ps):
                pe.wait_ge(third_act[b], nth(third_act[b], r, 2))
                for kk in range(KT):
                    pe.matmul(ps[0:H, 0:D], AT[b][:, kk, :], W("av", KT)[:, kk, :], start=(kk == 0), stop=False)
                pe.matmul(ps[0:H, 0:D], ks[b][:, :], W("bav"), start=False, stop=True).then_inc(third_pe[b], 1)

            def third_state(b, r, ps):
                pe.wait_ge(third_dve[b], nth(third_dve[b], r, 3))
                pe.matmul(ps[:, 0:H], drep[b][:, :], W("tri"), start=True, stop=True).then_inc(third_pe[b], 1)

            def third_mm(b, r, ps):
                pe.wait_ge(third_dve[b], nth(third_dve[b], r, 4))
                for kk in range(KT):
                    last = pe.matmul(ps[0:H, 0:D], sx[b][:, kk, :], W("ao", KT)[:, kk, :],
                                     start=(kk == 0), stop=(kk == KT - 1))
                last.then_inc(third_pe[b], 1)

            for b in LANE:
                context(b, 0)
            for b in LANE:
                third_z(b, 0)
            for b in LANE:
                keys(b, 0)
            for b in LANE:
                turn_x(b, 0, 0)
            pe.wait_ge(w_in[1], 16)
            for b in LANE:
                queries(b, 0, 0)
            for b in LANE:
                third_sums(b, 0)
            for b in LANE:
                third_kv(b, 0, dense[b][3])
            for b in LANE:
                third_state(b, 0, dense[b][3])
            for b in LANE:
                third_mm(b, 0, dense[b][3])
            for b in LANE:
                values(b, 0)
            with pe.Fori(0, ITERS) as it:
                def norm(b, L):
                    turn_x(b, L, it)

                def turn_att(b, m):
                    pe.wait_ge(att_s, nth(att_s, it, m * ITEMS + (b + 1) * ITEMS // LANES))
                    transpose_all(dense[b][0], att[b]).then_inc(attT_ps[b], 1)

                def att_out(b, m):
                    pe.wait_ge(attT_s[b], nth(attT_s[b], it, m + 1))
                    project(dense[b][1], MHA[m]["o"], attT[b]).then_inc(o_ps[b], 1)

                def gate(b):
                    pe.wait_ge(xhT_s[b], nth(xhT_s[b], it, 2))
                    for t in range(T):
                        for kk in range(KT):
                            last = pe.matmul(dense[b][1][:, t * E:(t + 1) * E], xhT[b][:, kk, t * P:(t + 1) * P],
                                             W("gate0", KT)[:, kk, :], start=(kk == 0), stop=(kk == KT - 1))
                    last.then_inc(gate_ps[b], 1)

                def experts(b, n):
                    t, i = n // 4, n % 4
                    if n >= 2:
                        pe.wait_ge(ex_used[b], nth(ex_used[b], it, n - 1))
                    for kk in range(KT):
                        last = pe.matmul(dense[b][2 + i % 2][:, :], xhT[b][:, kk, t * P:(t + 1) * P],
                                         W("exp0", KT)[:, kk, i * 512:(i + 1) * 512],
                                         start=(kk == 0), stop=(kk == KT - 1))
                    last.then_inc(ex_ps[b], 1)

                def glob(b, n):
                    if n > 1:
                        pe.wait_ge(gc_s[b], nth(gc_s[b], it, n - 1))
                    if n == 1:
                        for k in range(KT):
                            for t in range(T):
                                last = pe.matmul(dense[b][3][:, k:k + 1], xh[b][:, t, k * P:(k + 1) * P], W("mean"),
                                                 start=(t == 0), stop=(t == T - 1))
                    elif n == 2:
                        for kk in range(KT):
                            last = pe.matmul(dense[b][3][:, 4:5], W("gw1", KT)[:, kk, :], gcT[b][:, kk:kk + 1],
                                             start=(kk == 0), stop=(kk == KT - 1))
                    elif n == 3:
                        last = pe.matmul(dense[b][3][0:64, 8:9], W("gw2"), g1[b][:, :], start=True, stop=True)
                    else:
                        last = pe.matmul(dense[b][3][:, 12:13], g2[b][:, :], W("gw3"), start=True, stop=True)
                    last.then_inc(gc_ps[b], 1)

                def net(b, c, layer):
                    if c == 0:
                        glob(b, layer)
                    if layer == 1:
                        if c:
                            pe.wait_ge(oT_s[b], nth(oT_s[b], it, c))
                        else:
                            pe.wait_ge(xhT_s[b], nth(xhT_s[b], it, 4))
                        for k in range(KT):
                            for kk in range(KT):
                                last = pe.matmul(dense[b][1 + k][:, 0:S], W("cw1", KT)[:, kk, k * P:(k + 1) * P],
                                                 xhT[b][:, kk, :], start=(kk == 0), stop=(kk == KT - 1))
                            last.then_inc(n1_ps[b], 1)
                    elif layer == 2:
                        for kk in range(KT):
                            pe.wait_ge(n1_s[b], nth(n1_s[b], it, 2 * c + kk + 1))
                            last = pe.matmul(dense[b][0][:, 0:S], W("cw2", KT)[:, kk, :], h1T[b][:, kk, :],
                                             start=(kk == 0), stop=(kk == KT - 1))
                        last.then_inc(n2_ps[b], 1)
                    elif layer == 3:
                        pe.wait_ge(n2_s[b], nth(n2_s[b], it, c + 1))
                        pe.matmul(dense[b][1][0:64, 0:S], W("cw3"), h2T[b][:, :], start=True, stop=True).then_inc(n3_ps[b], 1)
                    else:
                        pe.wait_ge(n3_s[b], nth(n3_s[b], it, c + 1))
                        for t in range(T):
                            last = pe.matmul(dense[b][2][:, t:t + 1], h3T[b][:, t * P:(t + 1) * P], W("cw4"),
                                             start=True, stop=True)
                        last.then_inc(n4_ps[b], 1)

                pe.wait_ge(w_in[1], 16)
                pe.wait_ge(mask_ready, 1)
                pe.wait_ge(ones_ready, LANES)
                keep_warm(bank[1], 6)
                for m in range(2):
                    L = 2 * m
                    for s in range(ITEMS + 5):
                        j = m * ITEMS + s
                        for h in range(GH):
                            if s < ITEMS:
                                b, g = item[s]
                                hh = g * GH + h
                                if g == 0 and h == 0:
                                    pe.wait_ge(k_rows[b], nth(k_rows[b], it, 16 * len(GROUPS) * (m + 1)))
                                    pe.wait_ge(q_rows[b], nth(q_rows[b], it, 16 * len(GROUPS) * (m + 1)))
                                if s == 0 and h == 2:
                                    pe.wait_ge(third_act[1], nth(third_act[1], it, 3))
                                    if m == 0:
                                        pe.wait_ge(max_s, nth(max_s, it, 1))
                                    if m:
                                        pe.wait_ge(ex_used[1], nth(ex_used[1], it, T * 4))
                                if GH * s + h >= 3:
                                    pe.wait_ge(max_s, nth(max_s, it, GH * j + h - 2))
                                ps = s_bank[(GH * s + h) % 3]
                                for t in range(T):
                                    last = pe.matmul(ps[:, t * S:(t + 1) * S], QA[b][0:KR, hh, t * P:(t + 1) * P],
                                                     KA[b][0:KR, hh, :], start=True, stop=(m == 0))
                                    if m == 1:
                                        last = pe.matmul(ps[:, t * S:(t + 1) * S], identb[:, :], maskb[:, t, :],
                                                         start=False, stop=True)
                                last.then_inc(s_ps, 1)
                            if 0 <= s - 3 < ITEMS:
                                n, (b, g) = j - 3, item[s - 3]
                                hh = g * GH + h
                                if h == 0:
                                    pe.wait_ge(m_rows[n % 2], nth(m_rows[0], it, 32 * (n // 2 + 1)))
                                if n % ITEMS == 0 and h == 0:
                                    pe.wait_ge(v_s[0], nth(v_s[0], it, m + 1))
                                    pe.wait_ge(third_act[0], nth(third_act[0], it, 3))
                                if GH * (s - 3) + h >= 3:
                                    pe.wait_ge(exp_s, nth(exp_s, it, GH * n + h - 2))
                                ps = st_bank[(GH * (s - 3) + h) % 3]
                                for t in range(T):
                                    last = pe.matmul(ps[:, t * S:(t + 1) * S], KA[b][0:KM, hh, t * P:(t + 1) * P],
                                                     QA[b][0:KM, hh, :], start=True, stop=(m == 0))
                                    if m == 1:
                                        last = pe.matmul(ps[:, t * S:(t + 1) * S], identb[:, :], maskb[:, t, :],
                                                         start=False, stop=True)
                                last.then_inc(st_ps, 1)
                            if h == 0 and 0 <= s - 4 < ITEMS:
                                n, (b, g) = j - 4, item[s - 4]
                                if g == 0:
                                    pe.wait_ge(v_s[b], nth(v_s[b], it, m + 1))
                                pe.wait_ge(exp_s, nth(exp_s, it, GH * (n + 1)))
                                if n >= 1:
                                    pe.wait_ge(ot_s, nth(ot_s, it, n))
                                for t in range(T):
                                    for i in range(GH):
                                        last = pe.matmul(bank[4][32 * i:32 * i + 32, 0:S], vaug[b][:, t, g * GH + i, :],
                                                         PT[n % 2][:, i, t, :], start=(t == 0), stop=(t == T - 1),
                                                         tile_position=(0, 32 * i))
                                last.then_inc(pv_ps, 1)
                            if m == 1 and s == 1 and h == 1:
                                pe.wait_ge(v_s[1], nth(v_s[1], it, 2))
                                queries(1, 1, it)
                            if h == 1 and 0 <= s - 1 < ITEMS:
                                n = j - 1
                                pe.wait_ge(mq_s, nth(mq_s, it, n + 1))
                                if n >= 1:
                                    pe.wait_ge(negm_s, nth(negm_s, it, n))
                                if s >= 5:
                                    pe.wait_ge(att_s, nth(att_s, it, j - 4))
                                for t in range(T):
                                    last = pe.transpose(bank6b[0:2 * GH, 512 + t * P:512 + (t + 1) * P],
                                                        mq[:, n % 2, t, :, :].rearrange("p c h -> p (c h)"), identb[:, :])
                                last.then_inc(mT_ps, 1)
                        if 0 <= s - 4 < ITEMS:
                            n = j - 4
                            pe.wait_ge(ot_s, nth(ot_s, it, n + 1))
                            if n >= 1:
                                pe.wait_ge(att_s, nth(att_s, it, n))
                            pe.wait_ge(negm_s, nth(negm_s, it, min(j, (m + 1) * ITEMS)))
                            for t in range(T):
                                last = pe.transpose(bank[6][:, t * P:(t + 1) * P], OT[n % 2][:, t * P:(t + 1) * P], ident)
                            last.then_inc(otT_ps, 1)
                        if s in (1, 2):
                            pe.wait_ge(q_f[1], nth(q_f[1], it, 1))
                            keep_warm(bank[4], ((3, 2), (5, 4))[m][s - 1])
                        if m == 1 and s == 0:
                            norm(1, 2)
                        if s == 8:
                            turn_att(0, m)
                        if s == 9:
                            pe.wait_ge(w_in[2 + m], 16)
                            att_out(0, m)
                        if s == 11:
                            pe.wait_ge(max_s, nth(max_s, it, (m + 1) * ITEMS * GH))
                            keep_warm(bank[7], 3)
                            norm(0, L + 1)
                            keep_warm(bank[7], 2)
                    if m == 0:
                        gate(0)
                    turn_att(1, m)
                    keep_warm(bank[7], 2)
                    if m == 0:
                        experts(0, 0)
                    else:
                        pe.wait_ge(w_in[4], 16)
                        net(0, 0, 1)
                    att_out(1, m)
                    if m == 0:
                        for n in range(1, T * 4):
                            experts(0, n)
                            if n == 3:
                                norm(1, 1)
                            if n == 4:
                                gate(1)
                        pe.wait_ge(ex_used[0], nth(ex_used[0], it, T * 4 - 1))
                        pe.wait_ge(w_in[3], 16)
                        project_T(dense[0][2], "wk1", ctxT[0]).then_inc(k_ps[0], 1)
                        project_T(dense[1][0], "wk1", ctxT[1]).then_inc(k_ps[1], 1)
                        for n in range(T * 4):
                            experts(1, n)
                            if n == 1:
                                norm(0, 2)
                            if n == 2:
                                queries(0, 1, it)
                        project(dense[0][3], "wv1", ctxT[0]).then_inc(v_ps[0], 1)
                        project(dense[1][1], "wv1", ctxT[1]).then_inc(v_ps[1], 1)
                def turn(b, c):
                    if c:
                        keep_warm(dense[b][0], 5)
                        pe.wait_ge(o_new[b], nth(o_new[b], it, c))
                        transpose_all(dense[b][0], (o2 if c == 1 else xh)[b]).then_inc(oT_ps[b], 1)
                    elif b == 1:
                        keep_warm(bank[7], 5)
                        norm(1, 3)

                def last_key(b):
                    pe.wait_ge(gc_s[b], nth(gc_s[b], it, 4))
                    project_T(dense[b][3], "wk3", ctxT[b]).then_inc(last_pe[b], 1)

                def last_value(b):
                    pe.wait_ge(last_act[b], nth(last_act[b], it, 1))
                    project(dense[b][3], "wv3", ctxT[b]).then_inc(last_pe[b], 1)

                def third_query(b):
                    norm(b, 4)
                    pe.wait_ge(xhT_s[b], nth(xhT_s[b], it, 5))
                    for kk in range(KT):
                        last = pe.matmul(dense[b][1][0:H, 0:S], W("aq", KT)[:, kk, :], xhT[b][:, kk, :],
                                         start=(kk == 0), stop=(kk == KT - 1))
                    last.then_inc(third_pe[b], 1)

                def third_out(b):
                    pe.wait_ge(third_dve[b], nth(third_dve[b], it, 5))
                    pe.wait_ge(third_act[b], nth(third_act[b], it, 3))
                    for t in range(T):
                        last = pe.matmul(dense[b][0][:, t * D:(t + 1) * D], qh[b][:, t * P:(t + 1) * P], mm[b][:, :],
                                         start=True, stop=True)
                    last.then_inc(third_pe[b], 1)

                def logits(b):
                    pe.wait_ge(xhT_s[b], nth(xhT_s[b], it, 6))
                    for t in range(T):
                        for kk in range(KT):
                            last = pe.matmul(dense[b][1][:, t * 40:(t + 1) * 40], xhT[b][:, kk, t * P:(t + 1) * P],
                                             W("gl", KT)[:, kk, :], start=(kk == 0), stop=(kk == KT - 1))
                    last.then_inc(rank_pe[b], 1)

                def linear(b):
                    pe.wait_ge(last_dve[b], nth(last_dve[b], it, 1))
                    for t in range(T):
                        for kk in range(KT):
                            pe.matmul(dense[b][3 - 3 * t][:, 0:D], xhT[b][:, kk, t * P:(t + 1) * P], W("lin", KT)[:, kk, :],
                                      start=(kk == 0), stop=False)

                def turn_low_rank(b):
                    pe.wait_ge(rank_dve[b], nth(rank_dve[b], it, 2))
                    for t in range(T):
                        last = pe.transpose(dense[b][2][0:E * R, t * P:(t + 1) * P], tw[b][:, t, :], ident)
                    last.then_inc(rank_pe[b], 1)

                def low_rank(b):
                    pe.wait_ge(rank_act[b], nth(rank_act[b], it, 2))
                    for t in range(T):
                        last = pe.matmul(dense[b][3 - 3 * t][:, 0:D], twT[b][:, t * P:(t + 1) * P], W("right"),
                                         start=False, stop=True)
                    last.then_inc(rank_pe[b], 1)

                for c in range(3):
                    turn(0, c)
                    if c:
                        net(1, c - 1, 3)
                        net(0, c, 1)
                        net(1, c - 1, 4)
                    net(0, c, 2)
                    turn(1, c)
                    net(0, c, 3)
                    net(1, c, 1)
                    net(0, c, 4)
                    net(1, c, 2)
                net(1, 2, 3)
                last_key(0)
                net(1, 2, 4)
                last_key(1)
                keep_warm(dense[0][0], 6)
                third_query(0)
                keep_warm(dense[0][2], 5)
                third_out(0)
                third_query(1)
                last_value(0)
                third_out(1)
                keep_warm(dense[0][2], 3)
                norm(0, 5)
                logits(0)
                last_value(1)
                linear(0)
                norm(1, 5)
                logits(1)
                linear(1)
                keep_warm(dense[0][2], 2)
                turn_low_rank(0)
                low_rank(0)
                context(0, it + 1)
                keys(0, it + 1)
                turn_low_rank(1)
                low_rank(1)
                context(1, it + 1)
                def last_query(b):
                    pe.wait_ge(xhT_s[b], nth(xhT_s[b], it, 7))
                    project_T(dense[b][1], "wq3", xhT[b]).then_inc(last_pe[b], 1)

                def last_scores(b):
                    pe.wait_ge(last_act[b], nth(last_act[b], it, 2))
                    pe.wait_ge(last_dve[b], nth(last_dve[b], it, 2))
                    for t in range(T):
                        ps = dense[b][0][:, t * S:(t + 1) * S]
                        for kk in range(KT):
                            pe.matmul(ps, qf[b][:, kk, t * P:(t + 1) * P], kf[b][:, kk, :], start=(kk == 0), stop=False)
                        last = pe.matmul(ps, W("ones")[0:1, :], mrow[b][:, :], start=False, stop=True)
                    last.then_inc(last_pe[b], 1)

                def last_turn(b):
                    pe.wait_ge(last_act[b], nth(last_act[b], it, 3))
                    transpose_all(dense[b][1], att[b]).then_inc(last_pe[b], 1)

                def last_out(b):
                    pe.wait_ge(last_act[b], nth(last_act[b], it, 4))
                    for t in range(T):
                        for kk in range(T):
                            last = pe.matmul(dense[b][3][:, t * D:(t + 1) * D], attT[b][:, kk, t * P:(t + 1) * P],
                                             v3[b][:, kk, :], start=(kk == 0), stop=(kk == T - 1))
                    last.then_inc(last_pe[b], 1)

                keep_warm(dense[0][1], 6)
                norm(0, 6)
                third_z(0, it + 1)
                last_query(0)
                norm(1, 6)
                third_z(1, it + 1)
                last_scores(0)
                last_query(1)
                keys(1, it + 1)
                for b in LANE:
                    third_sums(b, it + 1)
                last_scores(1)
                last_turn(0)
                values(0, it + 1)
                last_out(0)
                last_turn(1)
                last_out(1)
                values(1, it + 1)
                keep_warm(dense[0][1], 7)
                for b in LANE:
                    norm(b, 7)
                for b in LANE:
                    pe.wait_ge(xhT_s[b], nth(xhT_s[b], it, 8))
                wg = wi[:, 0:KT * HID].rearrange("p (k n) -> p k n", k=KT)
                wu = wi[:, KT * HID:2 * KT * HID].rearrange("p (k n) -> p k n", k=KT)
                wd = wi[:, 2 * KT * HID:NI].rearrange("p (k n) -> p k n", k=HT)
                pe.wait_ge(wi_ready, 1)
                for k in range(HT):
                    for b in LANE:
                        if k == 1:
                            pe.wait_ge(v_s[b], nth(v_s[b], it + 1, 1))
                        if k >= 2:
                            pe.wait_ge(hid_s[b], nth(hid_s[b], it, k - 1))
                        for i, ww in enumerate((wg, wu)):
                            for kk in range(KT):
                                last = pe.matmul(dense[b][1 + k % 2][:, i * S:(i + 1) * S], ww[:, kk, k * P:(k + 1) * P],
                                                 xhT[b][:, kk, :], start=(kk == 0), stop=(kk == KT - 1))
                        last.then_inc(gu_ps[b], 1)
                    if k in (0, 2, 3):
                        for b in LANE:
                            {0: third_kv, 2: third_state, 3: third_mm}[k](b, it + 1, dense[b][0])
                for b in LANE:
                    pe.wait_ge(third_act[b], nth(third_act[b], it + 1, 3))
                    turn_x(b, 0, it + 1)
                for b in LANE:
                    queries(b, 0, it + 1)
                for b in LANE:
                    pe.wait_ge(hid_s[b], nth(hid_s[b], it, HT))
                    for t in range(T):
                        for kk in range(HT):
                            last = pe.matmul(dense[b][3][:, t * D:(t + 1) * D], hT[b][:, kk, t * P:(t + 1) * P],
                                             wd[:, kk, :], start=(kk == 0), stop=(kk == HT - 1))
                    last.then_inc(dn_ps[b], 1)



def tiles(a):
    k, n = a.shape
    return a.reshape(k // P, P, n).transpose(1, 0, 2).reshape(P, -1)


def column(v):
    return v.reshape(-1, P).T


def everywhere(v):
    return np.broadcast_to(v.reshape(1, -1), (P, v.size))


def packed(a):
    wkv, bkv = a["L1_xattn_Wkv"], a["L1_xattn_bkv"]
    heads = np.arange(D) // HD
    by_place = np.arange(D).reshape(H, HD).T.reshape(-1)
    parts = {
        "ident": np.eye(P, dtype=np.float32),
        "wk0": tiles(a["L0_xattn_W_K"][:, by_place]), "bk0": column(a["L0_xattn_b_K"][by_place]),
        "wv0": tiles(a["L0_xattn_W_V"]), "bv0": everywhere(a["L0_xattn_b_V"]),
        "wq0": tiles(a["L0_xattn_W_Q"][:, by_place]), "bq0": column(a["L0_xattn_b_Q"][by_place]),
        "wo0": tiles(a["L0_xattn_W_O"]), "bo0": everywhere(a["L0_xattn_b_O"]),
        "gate0": tiles(a["L0_ffn_gate_w"].T), "desc": everywhere(np.arange(E, 0, -1).astype(np.float32)),
        "exp0": tiles(a["L0_ffn_expert_w"].transpose(2, 0, 1).reshape(D, E * D)),
        "wk1": tiles(wkv[:, by_place]), "bk1": column(bkv[by_place]), "wv1": tiles(wkv[:, D:]), "bv1": everywhere(bkv[D:]),
        "wq1": tiles(a["L1_xattn_Wq"][:, by_place]), "bq1": column(a["L1_xattn_bq"][by_place]),
        "wo1": tiles(a["L1_xattn_Wo"]), "bo1": everywhere(a["L1_xattn_bo"]),
        "cw1": tiles(a["L1_ffn_cn_w1"]), "cb1": column(a["L1_ffn_cn_b1"]),
        "cw2": tiles(a["L1_ffn_cn_w2"]), "cb2": column(a["L1_ffn_cn_b2"]),
        "cw3": a["L1_ffn_cn_w3"], "cb3": a["L1_ffn_cn_b3"].reshape(64, 1),
        "cw4": a["L1_ffn_cn_w4"], "cb4": everywhere(a["L1_ffn_cn_b4"]),
        "gw1": tiles(a["L1_ffn_gc_w1"]), "gb1": column(a["L1_ffn_gc_b1"]),
        "gw2": a["L1_ffn_gc_w2"], "gb2": a["L1_ffn_gc_b2"].reshape(64, 1),
        "gw3": a["L1_ffn_gc_w3"], "gb3": everywhere(a["L1_ffn_gc_b3"]),
        "range": everywhere(a["L1_ffn_adaptive_range"]), "mean": np.full((P, 1), 1.0 / S, np.float32),
        "aq": tiles(a["L2_xattn_wq"]), "ak": tiles(a["L2_xattn_wk"]), "baq": a["L2_xattn_bq"].reshape(H, 1),
        "bak": np.tile(everywhere(a["L2_xattn_bk"]), (1, T)), "av": tiles(a["L2_xattn_wv"]),
        "bav": a["L2_xattn_bv"].reshape(1, D), "ao": tiles(a["L2_xattn_wo"]), "bao": everywhere(a["L2_xattn_bo"]),
        "diag": (heads[None, :] == np.arange(H)[:, None]).astype(np.float32),
        "tri": np.triu(np.ones((H, H), np.float32)),
        "pick": tiles((heads[:, None] == np.arange(H)[None, :]).astype(np.float32)),
        "ones": np.ones((P, P), np.float32),
        "lin": tiles(a["L2_ffn_W_lin"].T), "blin": everywhere(a["L2_ffn_b_lin"]),
        "gl": tiles(np.concatenate([a["L2_ffn_gate_w"].T, a["L2_ffn_left"].transpose(1, 0, 2).reshape(D, E * R)], 1)),
        "right": a["L2_ffn_right"].reshape(E * R, D),
        "wq3": tiles(a["L3_xattn_Wq"]), "bq3": column(a["L3_xattn_bq"]),
        "wk3": tiles(a["L3_xattn_Wk"]), "bk3": column(a["L3_xattn_bk"]),
        "wv3": tiles(a["L3_xattn_Wv"]), "bv3": everywhere(a["L3_xattn_bv"]),
    }
    out = np.zeros((P, NCOLS), np.float32)
    for name, (at, p, n) in COLS.items():
        assert parts[name].shape == (p, n), (name, parts[name].shape, p, n)
        out[:p, at:at + n] = parts[name]
    return out


def kernel(**inputs):
    import concourse.bacc as bacc
    from concourse.bass_utils import run_bass_kernel_spmd

    a = {k: np.asarray(v) for k, v in inputs.items()}
    arrays = {
        "x_in": np.ascontiguousarray(a["x"]),
        "ctx_in": np.ascontiguousarray(a["ctx_1024"]),
        "mask_in": np.ascontiguousarray(a["mask_BxS2_ff1"]),
        "pack": packed(a),
        "nomask": tiles(np.where(cantor_mask(), np.float32(0), np.float32(OFF)).astype(np.float32)),
        "ipack": np.ascontiguousarray(np.concatenate(
            [tiles(a["L3_ffn_w_gate"].T), tiles(a["L3_ffn_w_up"].T), tiles(a["L3_ffn_w_down"].T)], 1)),
    }
    nc = bacc.Bacc("TRN2", target_bir_lowering=False, num_devices=1)
    aps = [nc.dram_tensor(n, v.shape, mybir.dt.from_np(v.dtype), kind="ExternalInput").ap() for n, v in arrays.items()]
    scratch = nc.dram_tensor("scratch", (LANES, 2, 3, D, S), BF16).ap()
    out = nc.dram_tensor("out", (B, S, D), F32, kind="ExternalOutput").ap()
    program(nc, *aps, scratch, out)
    r = run_bass_kernel_spmd(nc, [arrays], core_ids=[0])
    return r.results[0]["out"]
```
